# Optimizing a Trainium2 kernel written in Bass

```python
import numpy as np
import jax
import jax.numpy as jnp

def _softmax(x, axis=-1):
    return jax.nn.softmax(x, axis=axis)

def _gelu(x):
    return jax.nn.gelu(x, approximate=True)

def _silu(x):
    return jax.nn.silu(x)

def _sigmoid(x):
    return jax.nn.sigmoid(x)

def _layernorm(x, axis=-1, eps=1e-05):
    m = jnp.mean(x, axis=axis, keepdims=True)
    v = jnp.var(x, axis=axis, keepdims=True)
    return (x - m) / jnp.sqrt(v + eps)

def _scatter_add(tgt, idx, src, axis=0):
    return tgt.at[idx].add(src)

def _segment_sum(src, seg, n):
    return jax.ops.segment_sum(src, seg, n)
kernel_name = 'mk_cond_resid_d4_seqx_r4_f9c2e6'

def setup_inputs(seed: int=0):
    np.random.seed(seed)
    _w = jnp.asarray

    def _rec_inputs():
        import jax
        import jax.numpy as jnp
        _rk = jax.random.key(seed)
        x = 7.22e-05 + 1 * jax.random.normal(jax.random.fold_in(_rk, 1), (2, 1024, 256), jnp.float32)
        _lenS = 1024 - jax.random.randint(jax.random.fold_in(_rk, 7), (2,), 0, max(1, 1024 // 4) + 1, jnp.int32)
        _lenS2 = 1024 - jax.random.randint(jax.random.fold_in(_rk, 8), (2,), 0, max(1, 1024 // 4) + 1, jnp.int32)
        cond_64 = -0.104238 + 1.01173 * jax.random.normal(jax.random.fold_in(_rk, 11), (2, 64), jnp.float32)
        fside_16xSxS_0 = -5.72187e-05 + 0.999849 * jax.random.normal(jax.random.fold_in(_rk, 13), (16, 1024, 1024), jnp.float32)
        _validS = jnp.arange(1024)[None, :] < _lenS[:, None]
        _validS2 = jnp.arange(1024)[None, :] < _lenS2[:, None]
        _causal = jnp.tril(jnp.ones((1024, 1024), dtype=bool))
        mask_BxS_bf1 = jnp.ones((2, 1024), dtype=bool)
        mask_BxS_bk0 = jnp.logical_not(jnp.broadcast_to(_validS[:, :], (2, 1024)))
        return (x, cond_64, fside_16xSxS_0, mask_BxS_bf1, mask_BxS_bk0)
    x, cond_64, fside_16xSxS_0, mask_BxS_bf1, mask_BxS_bk0 = _rec_inputs()

    def _L0_cond_setup():
        import jax, jax.numpy as jnp
        import numpy as np
        B, S, H = (4, 512, 256)
        E = 8
        M = 128
        K = 2
        N_SHARED = 2
        SM = M * N_SHARED
        G = 64
        GE_TEMP = 1.0
        ALPHA = 0.001
        SEQ_AUX = True
        NORM_TOPK = True
        COS_TEMP = 0.78
        CONS_ALPHA = 0.01
        LEAKY_SLOPE = 0.01
        EPS_COS = 1e-08

        def _leaky(x):
            return jnp.where(x >= 0, x, LEAKY_SLOPE * x)

        def _moe_forward(hidden_states, g, wt, wg, w_gate, w_up, w_down, sw_gate, sw_up, sw_down):
            b, s, h = hidden_states.shape
            x = hidden_states.reshape(-1, h)
            T = x.shape[0]
            logits_h = x @ wt.T
            logits_g = g @ wg.T
            logits_g = jnp.repeat(logits_g, s, axis=0)
            logits = (logits_h + logits_g / GE_TEMP) / (1.0 + 1.0 / GE_TEMP)
            scores = jax.nn.softmax(logits, axis=-1)
            topk_w, topk_idx = jax.lax.top_k(scores, K)
            if K > 1 and NORM_TOPK:
                topk_w = topk_w / (topk_w.sum(-1, keepdims=True) + 1e-20)
            onehot = jax.nn.one_hot(topk_idx.reshape(b, s * K), E, dtype=jnp.float32)
            ce = onehot.sum(1) / (s * K / E)
            aux_loss = (ce * scores.reshape(b, s, E).mean(1)).sum(1).mean() * ALPHA
            gp = _leaky(jnp.einsum('th,ehm->etm', x, w_gate))
            up = jnp.einsum('th,ehm->etm', x, w_up)
            y_all = jnp.einsum('etm,emh->eth', gp * up, w_down)
            y_sel = y_all[topk_idx, jnp.arange(T)[:, None], :]
            y = (y_sel * topk_w[..., None]).sum(1).reshape(b, s, h)
            p = _leaky(hidden_states @ sw_gate) * (hidden_states @ sw_up) @ sw_down
            y = y + p
            num = jnp.sum(y * p, -1)
            den = jnp.maximum(jnp.linalg.norm(y, axis=-1), EPS_COS) * jnp.maximum(jnp.linalg.norm(p, axis=-1), EPS_COS)
            closs = CONS_ALPHA * jnp.mean(num / den / (1.0 + COS_TEMP))
            return (y, aux_loss + closs)
        key = jax.random.key(seed)
        ks = jax.random.split(key, 12)
        sh = 1.0 / np.sqrt(H)
        sm = 1.0 / np.sqrt(M)
        ssm = 1.0 / np.sqrt(SM)
        sg = 1.0 / np.sqrt(G)
        return {'hidden_states': jax.random.normal(ks[0], (B, S, H), jnp.float32), 'g': jax.random.normal(ks[1], (B, G), jnp.float32), 'wt': jax.random.uniform(ks[2], (E, H), jnp.float32, -sh, sh), 'wg': jax.random.uniform(ks[3], (E, G), jnp.float32, -sg, sg), 'w_gate': jax.random.uniform(ks[4], (E, H, M), jnp.float32, -sh, sh), 'w_up': jax.random.uniform(ks[5], (E, H, M), jnp.float32, -sh, sh), 'w_down': jax.random.uniform(ks[6], (E, M, H), jnp.float32, -sm, sm), 'sw_gate': jax.random.uniform(ks[7], (H, SM), jnp.float32, -sh, sh), 'sw_up': jax.random.uniform(ks[8], (H, SM), jnp.float32, -sh, sh), 'sw_down': jax.random.uniform(ks[9], (SM, H), jnp.float32, -ssm, ssm)}
    _L0_cond_all = _L0_cond_setup()
    _L0_cond_in = {k: v for k, v in _L0_cond_all.items() if k in ('wt', 'wg', 'w_gate', 'w_up', 'w_down', 'sw_gate', 'sw_up', 'sw_down')}
    del _L0_cond_all

    def _L1_cond_setup():
        import jax, jax.numpy as jnp
        import numpy as np
        DIM = 256
        HEADS = 16
        DIM_HEAD = 64
        SCALE = 8.0

        def ln(x, g, eps=1e-05):
            mean = x.mean(axis=-1, keepdims=True)
            var = ((x - mean) ** 2).mean(axis=-1, keepdims=True)
            return (x - mean) * jax.lax.rsqrt(var + eps) * g

        def l2norm(t):
            n = jnp.maximum(jnp.linalg.norm(t, axis=-1, keepdims=True), 1e-12)
            return t / n

        def rel_pos_bias(n, w0, b0, g0, w1, b1, g1, w2, b2, dtype):
            pos = jnp.arange(-n + 1, n, dtype=dtype)[:, None]
            h = jax.nn.silu(ln(pos @ w0 + b0, g0))
            h = jax.nn.silu(ln(h @ w1 + b1, g1))
            h = h @ w2 + b2
            i = jnp.arange(n)
            idx = i[:, None] - i[None, :] + n - 1
            bias = h[idx]
            return jnp.transpose(bias, (2, 0, 1))
        key = jax.random.key(seed)
        ks = jax.random.split(key, 16)
        b, n = (2, 512)
        inner = HEADS * DIM_HEAD
        s = 0.02
        return {'x': jax.random.normal(ks[0], (b, n, DIM), jnp.float32), 'mask': jnp.ones((b, n), dtype=bool), 'g_norm': jnp.ones((DIM,), jnp.float32), 'Wq': jax.random.normal(ks[1], (DIM, inner), jnp.float32) * s, 'Wkv': jax.random.normal(ks[2], (DIM, 2 * DIM_HEAD), jnp.float32) * s, 'q_scale': jnp.ones((DIM_HEAD,), jnp.float32), 'k_scale': jnp.ones((DIM_HEAD,), jnp.float32), 'null_kv': jax.random.normal(ks[3], (2, DIM_HEAD), jnp.float32), 'null_attn_bias': jax.random.normal(ks[4], (HEADS,), jnp.float32), 'w0': jax.random.normal(ks[5], (1, DIM), jnp.float32) * s, 'b0': jnp.zeros((DIM,), jnp.float32), 'g0': jnp.ones((DIM,), jnp.float32), 'w1': jax.random.normal(ks[6], (DIM, DIM), jnp.float32) * s, 'b1': jnp.zeros((DIM,), jnp.float32), 'g1': jnp.ones((DIM,), jnp.float32), 'w2': jax.random.normal(ks[7], (DIM, HEADS), jnp.float32) * s, 'b2': jnp.zeros((HEADS,), jnp.float32), 'Wout': jax.random.normal(ks[8], (inner, DIM), jnp.float32) * s, 'g_out': jnp.ones((DIM,), jnp.float32)}
    _L1_cond_all = _L1_cond_setup()
    _L1_cond_in = {k: v for k, v in _L1_cond_all.items() if k in ('g_norm', 'Wq', 'Wkv', 'q_scale', 'k_scale', 'null_attn_bias', 'w0', 'b0', 'g0', 'w1', 'b1', 'g1', 'w2', 'b2', 'Wout', 'g_out')}
    del _L1_cond_all

    def _L2_cond_setup():
        import jax, jax.numpy as jnp
        import numpy as np
        B, N, DIM, H, DH = (2, 512, 256, 16, 64)
        INNER = H * DH
        EPS = 1e-05

        def layernorm(x, g):
            mean = jnp.mean(x, axis=-1, keepdims=True)
            var = jnp.var(x, axis=-1, keepdims=True)
            return (x - mean) * jax.lax.rsqrt(var + EPS) * g
        key = jax.random.key(seed)
        ks = jax.random.split(key, 10)
        x = jax.random.normal(ks[0], (B, N, DIM), dtype=jnp.float32)
        attn_bias = jax.random.normal(ks[1], (H, N, N), dtype=jnp.float32)
        mask = jax.random.randint(ks[2], (B, N), 0, 2).astype(bool)
        g_in = jnp.ones((DIM,), dtype=jnp.float32)
        null_attn_bias = jax.random.normal(ks[3], (H,), dtype=jnp.float32)
        null_kv = jax.random.normal(ks[4], (2, DH), dtype=jnp.float32)
        Wq = jax.random.normal(ks[5], (DIM, INNER), dtype=jnp.float32) * 0.02
        Wkv = jax.random.normal(ks[6], (DIM, 2 * DH), dtype=jnp.float32) * 0.02
        Wo = jax.random.normal(ks[7], (INNER, DIM), dtype=jnp.float32) * 0.02
        g_out = jnp.ones((DIM,), dtype=jnp.float32)
        return {'x': x, 'attn_bias': attn_bias, 'mask': mask, 'g_in': g_in, 'null_attn_bias': null_attn_bias, 'null_kv': null_kv, 'Wq': Wq, 'Wkv': Wkv, 'Wo': Wo, 'g_out': g_out}
    _L2_cond_all = _L2_cond_setup()
    _L2_cond_in = {k: v for k, v in _L2_cond_all.items() if k in ('g_in', 'null_attn_bias', 'Wq', 'Wkv', 'Wo', 'g_out')}
    del _L2_cond_all

    def _L3_cond_setup():
        import jax, jax.numpy as jnp
        import numpy as np
        DIM = 256
        HEADS = 16
        DIM_HEAD = 64
        SCALE = 8.0

        def ln(x, g, eps=1e-05):
            mean = x.mean(axis=-1, keepdims=True)
            var = ((x - mean) ** 2).mean(axis=-1, keepdims=True)
            return (x - mean) * jax.lax.rsqrt(var + eps) * g

        def l2norm(t):
            n = jnp.maximum(jnp.linalg.norm(t, axis=-1, keepdims=True), 1e-12)
            return t / n

        def rel_pos_bias(n, w0, b0, g0, w1, b1, g1, w2, b2, dtype):
            pos = jnp.arange(-n + 1, n, dtype=dtype)[:, None]
            h = jax.nn.silu(ln(pos @ w0 + b0, g0))
            h = jax.nn.silu(ln(h @ w1 + b1, g1))
            h = h @ w2 + b2
            i = jnp.arange(n)
            idx = i[:, None] - i[None, :] + n - 1
            bias = h[idx]
            return jnp.transpose(bias, (2, 0, 1))
        key = jax.random.key(seed)
        ks = jax.random.split(key, 16)
        b, n = (2, 512)
        inner = HEADS * DIM_HEAD
        s = 0.02
        return {'x': jax.random.normal(ks[0], (b, n, DIM), jnp.float32), 'mask': jnp.ones((b, n), dtype=bool), 'g_norm': jnp.ones((DIM,), jnp.float32), 'Wq': jax.random.normal(ks[1], (DIM, inner), jnp.float32) * s, 'Wkv': jax.random.normal(ks[2], (DIM, 2 * DIM_HEAD), jnp.float32) * s, 'q_scale': jnp.ones((DIM_HEAD,), jnp.float32), 'k_scale': jnp.ones((DIM_HEAD,), jnp.float32), 'null_kv': jax.random.normal(ks[3], (2, DIM_HEAD), jnp.float32), 'null_attn_bias': jax.random.normal(ks[4], (HEADS,), jnp.float32), 'w0': jax.random.normal(ks[5], (1, DIM), jnp.float32) * s, 'b0': jnp.zeros((DIM,), jnp.float32), 'g0': jnp.ones((DIM,), jnp.float32), 'w1': jax.random.normal(ks[6], (DIM, DIM), jnp.float32) * s, 'b1': jnp.zeros((DIM,), jnp.float32), 'g1': jnp.ones((DIM,), jnp.float32), 'w2': jax.random.normal(ks[7], (DIM, HEADS), jnp.float32) * s, 'b2': jnp.zeros((HEADS,), jnp.float32), 'Wout': jax.random.normal(ks[8], (inner, DIM), jnp.float32) * s, 'g_out': jnp.ones((DIM,), jnp.float32)}
    _L3_cond_all = _L3_cond_setup()
    _L3_cond_in = {k: v for k, v in _L3_cond_all.items() if k in ('g_norm', 'Wq', 'Wkv', 'q_scale', 'k_scale', 'null_attn_bias', 'w0', 'b0', 'g0', 'w1', 'b1', 'g1', 'w2', 'b2', 'Wout', 'g_out')}
    del _L3_cond_all
    return {'x': x, 'cond_64': cond_64, 'fside_16xSxS_0': fside_16xSxS_0, 'mask_BxS_bf1': mask_BxS_bf1, 'mask_BxS_bk0': mask_BxS_bk0, 'L0_cond_wt': _L0_cond_in['wt'], 'L0_cond_wg': _L0_cond_in['wg'], 'L0_cond_w_gate': _L0_cond_in['w_gate'], 'L0_cond_w_up': _L0_cond_in['w_up'], 'L0_cond_w_down': _L0_cond_in['w_down'], 'L0_cond_sw_gate': _L0_cond_in['sw_gate'], 'L0_cond_sw_up': _L0_cond_in['sw_up'], 'L0_cond_sw_down': _L0_cond_in['sw_down'], 'L1_cond_g_norm': _L1_cond_in['g_norm'], 'L1_cond_Wq': _L1_cond_in['Wq'], 'L1_cond_Wkv': _L1_cond_in['Wkv'], 'L1_cond_q_scale': _L1_cond_in['q_scale'], 'L1_cond_k_scale': _L1_cond_in['k_scale'], 'L1_cond_null_attn_bias': _L1_cond_in['null_attn_bias'], 'L1_cond_w0': _L1_cond_in['w0'], 'L1_cond_b0': _L1_cond_in['b0'], 'L1_cond_g0': _L1_cond_in['g0'], 'L1_cond_w1': _L1_cond_in['w1'], 'L1_cond_b1': _L1_cond_in['b1'], 'L1_cond_g1': _L1_cond_in['g1'], 'L1_cond_w2': _L1_cond_in['w2'], 'L1_cond_b2': _L1_cond_in['b2'], 'L1_cond_Wout': _L1_cond_in['Wout'], 'L1_cond_g_out': _L1_cond_in['g_out'], 'L2_cond_g_in': _L2_cond_in['g_in'], 'L2_cond_null_attn_bias': _L2_cond_in['null_attn_bias'], 'L2_cond_Wq': _L2_cond_in['Wq'], 'L2_cond_Wkv': _L2_cond_in['Wkv'], 'L2_cond_Wo': _L2_cond_in['Wo'], 'L2_cond_g_out': _L2_cond_in['g_out'], 'L3_cond_g_norm': _L3_cond_in['g_norm'], 'L3_cond_Wq': _L3_cond_in['Wq'], 'L3_cond_Wkv': _L3_cond_in['Wkv'], 'L3_cond_q_scale': _L3_cond_in['q_scale'], 'L3_cond_k_scale': _L3_cond_in['k_scale'], 'L3_cond_null_attn_bias': _L3_cond_in['null_attn_bias'], 'L3_cond_w0': _L3_cond_in['w0'], 'L3_cond_b0': _L3_cond_in['b0'], 'L3_cond_g0': _L3_cond_in['g0'], 'L3_cond_w1': _L3_cond_in['w1'], 'L3_cond_b1': _L3_cond_in['b1'], 'L3_cond_g1': _L3_cond_in['g1'], 'L3_cond_w2': _L3_cond_in['w2'], 'L3_cond_b2': _L3_cond_in['b2'], 'L3_cond_Wout': _L3_cond_in['Wout'], 'L3_cond_g_out': _L3_cond_in['g_out']}

def reference(x, cond_64, fside_16xSxS_0, mask_BxS_bf1, mask_BxS_bk0, L0_cond_wt, L0_cond_wg, L0_cond_w_gate, L0_cond_w_up, L0_cond_w_down, L0_cond_sw_gate, L0_cond_sw_up, L0_cond_sw_down, L1_cond_g_norm, L1_cond_Wq, L1_cond_Wkv, L1_cond_q_scale, L1_cond_k_scale, L1_cond_null_attn_bias, L1_cond_w0, L1_cond_b0, L1_cond_g0, L1_cond_w1, L1_cond_b1, L1_cond_g1, L1_cond_w2, L1_cond_b2, L1_cond_Wout, L1_cond_g_out, L2_cond_g_in, L2_cond_null_attn_bias, L2_cond_Wq, L2_cond_Wkv, L2_cond_Wo, L2_cond_g_out, L3_cond_g_norm, L3_cond_Wq, L3_cond_Wkv, L3_cond_q_scale, L3_cond_k_scale, L3_cond_null_attn_bias, L3_cond_w0, L3_cond_b0, L3_cond_g0, L3_cond_w1, L3_cond_b1, L3_cond_g1, L3_cond_w2, L3_cond_b2, L3_cond_Wout, L3_cond_g_out):
    import jax
    import jax.numpy as jnp

    def _L0_cond_ref(hidden_states, g, wt, wg, w_gate, w_up, w_down, sw_gate, sw_up, sw_down):
        import jax, jax.numpy as jnp
        import numpy as np
        B, S, H = (4, 512, 256)
        E = 8
        M = 128
        K = 2
        N_SHARED = 2
        SM = M * N_SHARED
        G = 64
        GE_TEMP = 1.0
        ALPHA = 0.001
        SEQ_AUX = True
        NORM_TOPK = True
        COS_TEMP = 0.78
        CONS_ALPHA = 0.01
        LEAKY_SLOPE = 0.01
        EPS_COS = 1e-08

        def _leaky(x):
            return jnp.where(x >= 0, x, LEAKY_SLOPE * x)

        def _moe_forward(hidden_states, g, wt, wg, w_gate, w_up, w_down, sw_gate, sw_up, sw_down):
            b, s, h = hidden_states.shape
            x = hidden_states.reshape(-1, h)
            T = x.shape[0]
            logits_h = x @ wt.T
            logits_g = g @ wg.T
            logits_g = jnp.repeat(logits_g, s, axis=0)
            logits = (logits_h + logits_g / GE_TEMP) / (1.0 + 1.0 / GE_TEMP)
            scores = jax.nn.softmax(logits, axis=-1)
            topk_w, topk_idx = jax.lax.top_k(scores, K)
            if K > 1 and NORM_TOPK:
                topk_w = topk_w / (topk_w.sum(-1, keepdims=True) + 1e-20)
            onehot = jax.nn.one_hot(topk_idx.reshape(b, s * K), E, dtype=jnp.float32)
            ce = onehot.sum(1) / (s * K / E)
            aux_loss = (ce * scores.reshape(b, s, E).mean(1)).sum(1).mean() * ALPHA
            gp = _leaky(jnp.einsum('th,ehm->etm', x, w_gate))
            up = jnp.einsum('th,ehm->etm', x, w_up)
            y_all = jnp.einsum('etm,emh->eth', gp * up, w_down)
            y_sel = y_all[topk_idx, jnp.arange(T)[:, None], :]
            y = (y_sel * topk_w[..., None]).sum(1).reshape(b, s, h)
            p = _leaky(hidden_states @ sw_gate) * (hidden_states @ sw_up) @ sw_down
            y = y + p
            num = jnp.sum(y * p, -1)
            den = jnp.maximum(jnp.linalg.norm(y, axis=-1), EPS_COS) * jnp.maximum(jnp.linalg.norm(p, axis=-1), EPS_COS)
            closs = CONS_ALPHA * jnp.mean(num / den / (1.0 + COS_TEMP))
            return (y, aux_loss + closs)
        y, _ = _moe_forward(hidden_states, g, wt, wg, w_gate, w_up, w_down, sw_gate, sw_up, sw_down)
        return y

    def _L1_cond_ref(x, mask, g_norm, Wq, Wkv, q_scale, k_scale, null_kv, null_attn_bias, w0, b0, g0, w1, b1, g1, w2, b2, Wout, g_out):
        import jax, jax.numpy as jnp
        import numpy as np
        DIM = 256
        HEADS = 16
        DIM_HEAD = 64
        SCALE = 8.0

        def ln(x, g, eps=1e-05):
            mean = x.mean(axis=-1, keepdims=True)
            var = ((x - mean) ** 2).mean(axis=-1, keepdims=True)
            return (x - mean) * jax.lax.rsqrt(var + eps) * g

        def l2norm(t):
            n = jnp.maximum(jnp.linalg.norm(t, axis=-1, keepdims=True), 1e-12)
            return t / n

        def rel_pos_bias(n, w0, b0, g0, w1, b1, g1, w2, b2, dtype):
            pos = jnp.arange(-n + 1, n, dtype=dtype)[:, None]
            h = jax.nn.silu(ln(pos @ w0 + b0, g0))
            h = jax.nn.silu(ln(h @ w1 + b1, g1))
            h = h @ w2 + b2
            i = jnp.arange(n)
            idx = i[:, None] - i[None, :] + n - 1
            bias = h[idx]
            return jnp.transpose(bias, (2, 0, 1))
        b, n, _ = x.shape
        xn = ln(x, g_norm)
        q = (xn @ Wq).reshape(b, n, HEADS, DIM_HEAD).transpose(0, 2, 1, 3)
        kv = xn @ Wkv
        k, v = (kv[..., :DIM_HEAD], kv[..., DIM_HEAD:])
        nk = jnp.broadcast_to(null_kv[0], (b, 1, DIM_HEAD))
        nv = jnp.broadcast_to(null_kv[1], (b, 1, DIM_HEAD))
        k = jnp.concatenate([nk, k], axis=1)
        v = jnp.concatenate([nv, v], axis=1)
        q = l2norm(q) * q_scale
        k = l2norm(k) * k_scale
        sim = jnp.einsum('bhid,bjd->bhij', q, k) * SCALE
        bias = rel_pos_bias(n, w0, b0, g0, w1, b1, g1, w2, b2, q.dtype)
        null_bias = jnp.broadcast_to(null_attn_bias[:, None, None], (HEADS, n, 1))
        attn_bias = jnp.concatenate([null_bias, bias], axis=-1)
        sim = sim + attn_bias
        neg = -jnp.finfo(sim.dtype).max
        causal = jnp.triu(jnp.ones((n, n + 1), dtype=bool), k=2)
        sim = jnp.where(causal, neg, sim)
        m = jnp.pad(mask, ((0, 0), (1, 0)), constant_values=True)[:, None, None, :]
        sim = jnp.where(m, sim, neg)
        attn = jax.nn.softmax(sim, axis=-1)
        out = jnp.einsum('bhij,bjd->bhid', attn, v)
        out = out.transpose(0, 2, 1, 3).reshape(b, n, HEADS * DIM_HEAD)
        return ln(out @ Wout, g_out)

    def _L2_cond_ref(x, attn_bias, mask, g_in, null_attn_bias, null_kv, Wq, Wkv, Wo, g_out):
        import jax, jax.numpy as jnp
        import numpy as np
        B, N, DIM, H, DH = (2, 512, 256, 16, 64)
        INNER = H * DH
        EPS = 1e-05

        def layernorm(x, g):
            mean = jnp.mean(x, axis=-1, keepdims=True)
            var = jnp.var(x, axis=-1, keepdims=True)
            return (x - mean) * jax.lax.rsqrt(var + EPS) * g
        b, n, _ = x.shape
        scale = DH ** (-0.5)
        xn = layernorm(x, g_in)
        q = (xn @ Wq).reshape(b, n, H, DH).transpose(0, 2, 1, 3) * scale
        kv = xn @ Wkv
        k, v = (kv[..., :DH], kv[..., DH:])
        nk = jnp.broadcast_to(null_kv[0], (b, 1, DH))
        nv = jnp.broadcast_to(null_kv[1], (b, 1, DH))
        k = jnp.concatenate([nk, k], axis=1)
        v = jnp.concatenate([nv, v], axis=1)
        sim = jnp.einsum('bhid,bjd->bhij', q, k)
        null_col = jnp.broadcast_to(null_attn_bias[:, None, None], (H, n, 1))
        bias = jnp.concatenate([null_col, attn_bias], axis=-1)
        sim = sim + bias
        neg = -jnp.finfo(sim.dtype).max
        j = n + 1
        causal_mask = jnp.triu(jnp.ones((n, j), dtype=bool), k=j - n + 1)
        sim = jnp.where(causal_mask, neg, sim)
        mask_p = jnp.pad(mask, ((0, 0), (1, 0)), constant_values=True)
        sim = jnp.where(mask_p[:, None, None, :], sim, neg)
        attn = jax.nn.softmax(sim, axis=-1)
        out = jnp.einsum('bhij,bjd->bhid', attn, v)
        out = out.transpose(0, 2, 1, 3).reshape(b, n, INNER)
        out = out @ Wo
        return layernorm(out, g_out)

    def _L3_cond_ref(x, mask, g_norm, Wq, Wkv, q_scale, k_scale, null_kv, null_attn_bias, w0, b0, g0, w1, b1, g1, w2, b2, Wout, g_out):
        import jax, jax.numpy as jnp
        import numpy as np
        DIM = 256
        HEADS = 16
        DIM_HEAD = 64
        SCALE = 8.0

        def ln(x, g, eps=1e-05):
            mean = x.mean(axis=-1, keepdims=True)
            var = ((x - mean) ** 2).mean(axis=-1, keepdims=True)
            return (x - mean) * jax.lax.rsqrt(var + eps) * g

        def l2norm(t):
            n = jnp.maximum(jnp.linalg.norm(t, axis=-1, keepdims=True), 1e-12)
            return t / n

        def rel_pos_bias(n, w0, b0, g0, w1, b1, g1, w2, b2, dtype):
            pos = jnp.arange(-n + 1, n, dtype=dtype)[:, None]
            h = jax.nn.silu(ln(pos @ w0 + b0, g0))
            h = jax.nn.silu(ln(h @ w1 + b1, g1))
            h = h @ w2 + b2
            i = jnp.arange(n)
            idx = i[:, None] - i[None, :] + n - 1
            bias = h[idx]
            return jnp.transpose(bias, (2, 0, 1))
        b, n, _ = x.shape
        xn = ln(x, g_norm)
        q = (xn @ Wq).reshape(b, n, HEADS, DIM_HEAD).transpose(0, 2, 1, 3)
        kv = xn @ Wkv
        k, v = (kv[..., :DIM_HEAD], kv[..., DIM_HEAD:])
        nk = jnp.broadcast_to(null_kv[0], (b, 1, DIM_HEAD))
        nv = jnp.broadcast_to(null_kv[1], (b, 1, DIM_HEAD))
        k = jnp.concatenate([nk, k], axis=1)
        v = jnp.concatenate([nv, v], axis=1)
        q = l2norm(q) * q_scale
        k = l2norm(k) * k_scale
        sim = jnp.einsum('bhid,bjd->bhij', q, k) * SCALE
        bias = rel_pos_bias(n, w0, b0, g0, w1, b1, g1, w2, b2, q.dtype)
        null_bias = jnp.broadcast_to(null_attn_bias[:, None, None], (HEADS, n, 1))
        attn_bias = jnp.concatenate([null_bias, bias], axis=-1)
        sim = sim + attn_bias
        neg = -jnp.finfo(sim.dtype).max
        causal = jnp.triu(jnp.ones((n, n + 1), dtype=bool), k=2)
        sim = jnp.where(causal, neg, sim)
        m = jnp.pad(mask, ((0, 0), (1, 0)), constant_values=True)[:, None, None, :]
        sim = jnp.where(m, sim, neg)
        attn = jax.nn.softmax(sim, axis=-1)
        out = jnp.einsum('bhij,bjd->bhid', attn, v)
        out = out.transpose(0, 2, 1, 3).reshape(b, n, HEADS * DIM_HEAD)
        return ln(out @ Wout, g_out)
    x = x + _L0_cond_ref(x, cond_64, L0_cond_wt, L0_cond_wg, L0_cond_w_gate, L0_cond_w_up, L0_cond_w_down, L0_cond_sw_gate, L0_cond_sw_up, L0_cond_sw_down)
    x = x + _L1_cond_ref(x, mask_BxS_bf1, L1_cond_g_norm, L1_cond_Wq, L1_cond_Wkv, L1_cond_q_scale, L1_cond_k_scale, cond_64, L1_cond_null_attn_bias, L1_cond_w0, L1_cond_b0, L1_cond_g0, L1_cond_w1, L1_cond_b1, L1_cond_g1, L1_cond_w2, L1_cond_b2, L1_cond_Wout, L1_cond_g_out)
    x = x + _L2_cond_ref(x, fside_16xSxS_0, mask_BxS_bk0, L2_cond_g_in, L2_cond_null_attn_bias, cond_64, L2_cond_Wq, L2_cond_Wkv, L2_cond_Wo, L2_cond_g_out)
    x = x + _L3_cond_ref(x, mask_BxS_bf1, L3_cond_g_norm, L3_cond_Wq, L3_cond_Wkv, L3_cond_q_scale, L3_cond_k_scale, cond_64, L3_cond_null_attn_bias, L3_cond_w0, L3_cond_b0, L3_cond_g0, L3_cond_w1, L3_cond_b1, L3_cond_g1, L3_cond_w2, L3_cond_b2, L3_cond_Wout, L3_cond_g_out)
    return x

_drawn_inputs = setup_inputs


def setup_inputs(seed=0):
    import zlib

    import numpy as np

    out = dict(_drawn_inputs(seed))
    spreads = {'L1_cond_g_norm': (1.0, 0.2),
     'L1_cond_q_scale': (1.0, 0.2),
     'L1_cond_k_scale': (1.0, 0.2),
     'L1_cond_b0': (0.0, 2.0),
     'L1_cond_g0': (1.0, 0.6),
     'L1_cond_b1': (0.0, 0.8),
     'L1_cond_g1': (1.0, 0.6),
     'L1_cond_b2': (0.0, 0.8),
     'L1_cond_g_out': (1.0, 0.2),
     'L2_cond_g_in': (1.0, 0.2),
     'L2_cond_g_out': (1.0, 0.2),
     'L3_cond_g_norm': (1.0, 0.2),
     'L3_cond_q_scale': (1.0, 0.6),
     'L3_cond_k_scale': (1.0, 0.6),
     'L3_cond_b0': (0.0, 0.8),
     'L3_cond_g0': (1.0, 0.6),
     'L3_cond_b1': (0.0, 0.8),
     'L3_cond_g1': (1.0, 0.6),
     'L3_cond_b2': (0.0, 0.8),
     'L3_cond_g_out': (1.0, 0.2)}
    factors = {'L1_cond_w0': 26.763,
     'L2_cond_Wq': 3.257,
     'L3_cond_w0': 8.0,
     'L3_cond_w1': 5.443,
     'L3_cond_w2': 4.529,
     'L1_cond_w1': 3.294}
    for name, (base, spread) in spreads.items():
        noise = np.random.default_rng([zlib.crc32(name.encode()), seed]).standard_normal(out[name].shape)
        drawn = base * np.exp(spread * noise) if base else spread * noise
        out[name] = jnp.asarray(drawn.astype(out[name].dtype))
    for name, factor in factors.items():
        out[name] = (out[name] * factor).astype(out[name].dtype)
    return out
```

```python
from contextlib import ExitStack, contextmanager
from itertools import count

import numpy as np

import concourse.bass as bass
from concourse import mybir

F32 = mybir.dt.float32
FR = mybir.dt.float32r
U8 = mybir.dt.uint8
U32 = mybir.dt.uint32
ALU = mybir.AluOpType
ACT = mybir.ActivationFunctionType
AX = mybir.AxisListType

P = 128
B, S, D = 2, 1024, 256
NT = S // P
NTT = B * NT
KD = D // P
H, DH = 16, 64
NPAIR = H // 2
E, TOPK, M = 8, 2, 128
NU = E + 2
G = 64
BANK = 512
BIG = 1e30
EPS = 1e-5
BROW = S + P


SERIAL = count()


class Phase:

    POOL = 40

    def __init__(self, nc, t, names):
        self.nc, self.pool, self.names = nc, t["pool"], names

    def __enter__(self):
        self.stack = ExitStack()
        self.block = self.stack.enter_context(self.nc.Block())
        assert len(self.names) <= self.POOL
        return self.block, dict(zip(self.names, self.pool))

    def __exit__(self, *exc):
        self.stack.close()
        if exc[0] is None:
            self.nc.all_engine_barrier(sems_to_clear=range(self.pool[0].num, self.pool[len(self.names) - 1].num + 1))


class Own:

    def __init__(self, eng, sem, start=0):
        self.eng, self.sem, self.start, self.n = eng, sem, start, 0

    def step(self, instruction):
        instruction.then_inc(self.sem, 1)
        self.n += 1

    def settle(self):
        self.eng.wait_ge(self.sem, self.start + self.n)


class Turns:

    def __init__(self, sems, turn, marks):
        self.sems, self.turn, self.marks = sems, turn, marks

    def wait(self, eng, name, n):
        eng.wait_ge(self.sems[name], self.turn * self.marks[name] + (self.marks[name] + n))


def start(eng, sems, marks, *names):
    for name in names:
        eng.sem_inc(sems[name], marks[name])


@contextmanager
def tensors(nc):
    serial = next(SERIAL)
    with ExitStack() as stack:
        def sb(name, shape, dt=F32):
            return stack.enter_context(nc.sbuf_tensor(f"{name}_{serial}", shape, dt))

        def ps(name, shape, dt=F32):
            return stack.enter_context(nc.psum_tensor(f"{name}_{serial}", shape, dt))

        yield sb, ps


def rows(vector, n=P):
    return bass.AP(vector.tensor, vector.offset, [[0, n], [1, vector.shape[-1]]])


def f32(ap):
    return ap.bitcast(F32)


def three_products(eng, out, left, right, start, stop):
    pairs = ((0, 0), (0, 1), (1, 0))
    for n, (a, b) in enumerate(pairs):
        last = eng.matmul(out, left[a], right[b], start=start and n == 0, stop=stop and n == len(pairs) - 1)
    return last



def moe_route(nc, t, x, wt_t, cond_t, wg_t):
    names = ["x_in", "w_in", "x_tr", "x_hi", "x_lo", "w_hl", "logits", "dve", "exp_in", "exp_out"]
    with tensors(nc) as (sb, ps):
        wt = sb("route_wt", [P, KD, E])
        wt_h, wt_l = (sb(f"route_wt_{n}", [P, KD, E], FR) for n in "hl")
        cond = sb("route_cond", [G, B])
        cond_b = sb("route_cond_b", [G, B, P])
        wg = sb("route_wg", [G, E])
        logits = sb("route_logits", [P, NTT, E])
        top = sb("route_top", [P, NTT, E])
        top_i = sb("route_top_i", [P, NTT, E], U32)
        top_f = sb("route_top_f", [P, NTT, E])
        shifted = sb("route_shifted", [P, NTT, E])
        score = sb("route_score", [P, NTT, E])
        chosen = sb("route_chosen", [P, NTT, E])
        other = sb("route_other", [P, NTT, E])
        total = sb("route_total", [P, NTT])
        inv = sb("route_inv", [P, NTT])
        tr = [ps(f"route_tr{n}", [P, KD * P]) for n in range(2)]
        lp = ps("route_lp", [P, NTT, E])
        with Phase(nc, t, names) as (block, s):
            @block.sync
            def _(eng):
                eng.dma_start(t["ident"][:], t["in_ident"]).then_inc(s["w_in"], 16)
                eng.dma_start(t["iota"][:], t["in_iota"]).then_inc(s["w_in"], 16)
                eng.dma_start(wt[:], wt_t.rearrange("(k p) e -> p k e", p=P)).then_inc(s["w_in"], 16)
                eng.dma_start(cond[:], cond_t).then_inc(s["w_in"], 16)
                eng.dma_start(wg[:], wg_t).then_inc(s["w_in"], 16)
                for n in range(4):
                    eng.dma_start(t["x"][:, 4 * n:4 * n + 4, :],
                                  x[512 * n:512 * n + 512, :].rearrange("(t p) d -> p t d", p=P)).then_inc(s["x_in"], 16)
                eng.wait_ge(s["w_in"], 80)
                eng.wait_ge(s["x_in"], 64)

            @block.tensor
            def _(eng):
                eng.wait_ge(s["w_in"], 80)
                eng.wait_ge(s["x_in"], 64)
                for n in range(NTT):
                    if n >= 2:
                        eng.wait_ge(s["x_lo"], n - 1)
                    for k in range(KD):
                        last = eng.transpose(tr[n % 2][:, k * P:(k + 1) * P],
                                             t["x"][:, n, k * P:(k + 1) * P], t["ident"][:])
                    last.then_inc(s["x_tr"], 1)
                eng.wait_ge(s["w_hl"], 1)
                eng.wait_ge(s["x_lo"], NTT)
                for n in range(NTT):
                    for k in range(KD):
                        left = [t[c][:, k, n * P:(n + 1) * P] for c in ("xt_h", "xt_l")]
                        three_products(eng, lp[:, n, :], left, [w[:, k, :] for w in (wt_h, wt_l)], k == 0, False)
                    last = eng.matmul(lp[:, n, :], cond_b[:, n // NT, :], wg[:], start=False, stop=True)
                last.then_inc(s["logits"], 1)

            @block.scalar
            def _(eng):
                for n in range(NTT):
                    eng.wait_ge(s["x_tr"], n + 1)
                    eng.activation(t["xt_h"][:, :, n * P:(n + 1) * P],
                                   tr[n % 2][:].rearrange("p (k i) -> p k i", k=KD), ACT.Copy).then_inc(s["x_hi"], 1)
                eng.wait_ge(s["exp_in"], 1)
                eng.activation(score[:], shifted[:], ACT.Exp).then_inc(s["exp_out"], 1)

            @block.vector
            def _(eng):
                own = Own(eng, s["dve"])
                eng.wait_ge(s["w_in"], 80)
                own.step(eng.tensor_copy(t["ident_r"][:], t["ident"][:]))
                own.step(eng.tensor_copy(wt_h[:], wt[:]))
                own.settle()
                own.step(eng.tensor_tensor(wt_l[:], wt[:], f32(wt_h[:]), ALU.subtract))
                eng.tensor_copy(cond_b[:], cond[:].unsqueeze(2).to_broadcast([G, B, P])).then_inc(s["w_hl"], 1)
                for n in range(NTT):
                    eng.wait_ge(s["x_hi"], n + 1)
                    eng.tensor_tensor(t["xt_l"][:, :, n * P:(n + 1) * P],
                                      tr[n % 2][:].rearrange("p (k i) -> p k i", k=KD),
                                      f32(t["xt_h"][:, :, n * P:(n + 1) * P]), ALU.subtract).then_inc(s["x_lo"], 1)
                eng.wait_ge(s["logits"], 1)
                own.step(eng.tensor_scalar(logits[:], lp[:], 0.5, None, ALU.mult))
                own.settle()
                for n in range(NTT):
                    own.step(eng.max(top[:, n, :], logits[:, n, :]))
                own.settle()
                for n in range(NTT):
                    own.step(eng.max_index(top_i[:, n, :], top[:, n, :], logits[:, n, :]))
                eng.tensor_tensor(shifted[:], logits[:], top[:, :, 0:1].to_broadcast([P, NTT, E]),
                                  ALU.subtract).then_inc(s["exp_in"], 1)
                own.settle()
                own.step(eng.tensor_copy(top_f[:], top_i[:]))
                own.settle()
                iota = t["iota"][:].unsqueeze(1).to_broadcast([P, NTT, E])
                own.step(eng.tensor_tensor(chosen[:], iota, top_f[:, :, 0:1].to_broadcast([P, NTT, E]), ALU.is_equal))
                own.step(eng.tensor_tensor(other[:], iota, top_f[:, :, 1:2].to_broadcast([P, NTT, E]), ALU.is_equal))
                own.settle()
                own.step(eng.tensor_tensor(chosen[:], chosen[:], other[:], ALU.add))
                eng.wait_ge(s["exp_out"], 1)

                def normalize(eps):
                    own.step(eng.tensor_reduce(total[:], score[:], AX.X, ALU.add))
                    own.settle()
                    if eps:
                        own.step(eng.tensor_scalar(total[:], total[:], eps, None, ALU.add))
                        own.settle()
                    own.step(eng.reciprocal(inv[:], total[:]))
                    own.settle()

                normalize(0.0)
                own.step(eng.tensor_tensor(score[:], score[:], inv[:].unsqueeze(2).to_broadcast([P, NTT, E]), ALU.mult))
                own.settle()
                own.step(eng.tensor_tensor(score[:], score[:], chosen[:], ALU.mult))
                own.settle()
                normalize(1e-20)
                own.step(eng.memset(t["expert_w"][:], 1.0))
                own.settle()
                own.step(eng.tensor_tensor(t["expert_w"][:, 0:E, :].rearrange("p e n -> p n e"), score[:],
                                           inv[:].unsqueeze(2).to_broadcast([P, NTT, E]), ALU.mult))
                own.settle()


def moe_experts(nc, t, w_gate, w_up, w_down):
    NC = 4
    PAR = 2
    TURN = PAR * NC
    TPC = NTT // NC
    WC = 2 * KD * M + D
    names = ["w_in0", "w_in1", "w_split", "gu", "slope", "dve", "hidden", "hid_hi", "hid_lo", "down", "added"]
    with tensors(nc) as (sb, ps):
        raw = sb("moe_raw", [P, PAR, WC])
        wh, wl = (sb(f"moe_w{n}", [P, PAR, WC], FR) for n in "hl")
        slope = sb("moe_slope", [P, 2, BANK])
        leaky = sb("moe_leaky", [P, 2, BANK])
        hid = sb("moe_hid", [P, 2, BANK])
        hid_h, hid_l = (sb(f"moe_hid_{n}", [P, 2, BANK], FR) for n in "hl")
        unit_w = sb("moe_unit_w", [P, PAR, NTT])
        gate = [ps(f"moe_gate{n}", [P, BANK]) for n in range(2)]
        up = [ps(f"moe_up{n}", [P, BANK]) for n in range(2)]
        down = [ps(f"moe_down{n}", [P, TPC, D]) for n in range(2)]

        def w_of(tile, q, kind, k):
            at = {"gate": 0, "up": KD * M}.get(kind, 2 * KD * M) + k * M
            return tile[:, q, at:at + (D if kind == "down" else M)]

        marks = dict(w_split=PAR, gu=TURN, slope=TURN, dve=2 * PAR + TURN, hidden=TURN, hid_hi=TURN, hid_lo=TURN,
                     down=TURN, added=TURN)
        with Phase(nc, t, names) as (block, s):
            def load(eng, unit, q):
                one = bass.ds(unit, 1)
                for src, at in ((w_gate, 0), (w_up, KD * M)):
                    eng.dma_start(raw[:, q, at:at + KD * M].rearrange("p (k m) -> p k m", k=KD),
                                  src[one, :, :].rearrange("o (k p) m -> p (o k) m", p=P)).then_inc(s[f"w_in{q}"], 16)
                eng.dma_start(raw[:, q, 2 * KD * M:WC],
                              w_down[one, :, :].rearrange("o p d -> p (o d)")).then_inc(s[f"w_in{q}"], 16)

            @block.sync
            def _(eng):
                with eng.Fori(0, NU // PAR) as it:
                    turn = Turns(s, it, marks)
                    for q in range(PAR):
                        turn.wait(eng, "w_split", q + 1 - PAR)
                        load(eng, it * PAR + q, q)
                for q in range(PAR):
                    eng.wait_ge(s[f"w_in{q}"], 48 * (NU // PAR))

            @block.tensor
            def _(eng):
                start(eng, s, marks, "gu", "down")
                with eng.Fori(0, NU // PAR) as it:
                    turn = Turns(s, it, marks)

                    def gate_up(c):
                        q, tok = c // NC, c % NC
                        if c % NC == 0:
                            turn.wait(eng, "w_split", q + 1)
                        turn.wait(eng, "hidden", c - 1)
                        for kind, out in (("gate", gate), ("up", up)):
                            for k in range(KD):
                                last = three_products(
                                    eng, out[c % 2][:], [w_of(w, q, kind, k) for w in (wh, wl)],
                                    [t[x][:, k, tok * BANK:(tok + 1) * BANK] for x in ("xt_h", "xt_l")],
                                    k == 0, k == KD - 1)
                        last.then_inc(s["gu"], 1)

                    def down_of(c):
                        q = c // NC
                        turn.wait(eng, "hid_lo", c + 1)
                        turn.wait(eng, "added", c - 1)
                        for i in range(TPC):
                            last = three_products(
                                eng, down[c % 2][:, i, :], [h[:, c % 2, i * P:(i + 1) * P] for h in (hid_h, hid_l)],
                                [w_of(w, q, "down", 0) for w in (wh, wl)], True, True)
                        last.then_inc(s["down"], 1)

                    gate_up(0)
                    for c in range(TURN):
                        if c + 1 < TURN:
                            gate_up(c + 1)
                        down_of(c)

            @block.scalar
            def _(eng):
                start(eng, s, marks, "slope", "hid_hi")
                with eng.Fori(0, NU // PAR) as it:
                    turn = Turns(s, it, marks)

                    def slope_of(c):
                        turn.wait(eng, "gu", c + 1)
                        turn.wait(eng, "hidden", c - 1)
                        eng.activation(slope[:, c % 2, :], gate[c % 2][:], ACT.Copy, scale=0.01).then_inc(s["slope"], 1)

                    slope_of(0)
                    for c in range(TURN):
                        if c + 1 < TURN:
                            slope_of(c + 1)
                        turn.wait(eng, "hidden", c + 1)
                        turn.wait(eng, "down", c - 1)
                        eng.activation(hid_h[:, c % 2, :], hid[:, c % 2, :], ACT.Copy).then_inc(s["hid_hi"], 1)

            @block.gpsimd
            def _(eng):
                start(eng, s, marks, "hid_lo")
                with eng.Fori(0, NU // PAR) as it:
                    turn = Turns(s, it, marks)
                    for c in range(TURN):
                        turn.wait(eng, "hid_hi", c + 1)
                        eng.tensor_tensor(hid_l[:, c % 2, :], hid[:, c % 2, :], f32(hid_h[:, c % 2, :]),
                                          ALU.subtract).then_inc(s["hid_lo"], 1)

            @block.vector
            def _(eng):
                start(eng, s, marks, "w_split", "hidden", "added")
                with eng.Fori(0, NU // PAR) as it:
                    turn = Turns(s, it, marks)
                    own = Own(eng, s["dve"], it * marks["dve"])

                    def split(q):
                        eng.wait_ge(s[f"w_in{q}"], it * 48 + 48)
                        turn.wait(eng, "down", (q + 1) * NC - TURN)
                        own.step(eng.tensor_copy(wh[:, q, :], raw[:, q, :]))
                        own.step(eng.tensor_copy(unit_w[:, q, :],
                                                 t["expert_w"][:, bass.ds(it * PAR + q, 1), :].rearrange("p o n -> p (o n)")))
                        own.settle()
                        eng.tensor_tensor(wl[:, q, :], raw[:, q, :], f32(wh[:, q, :]), ALU.subtract
                                          ).then_inc(s["w_split"], 1)

                    def add_down(c):
                        q = c // NC
                        turn.wait(eng, "down", c + 1)
                        turn.wait(eng, "added", c)
                        for i in range(TPC):
                            n = (c % NC) * TPC + i
                            last = eng.scalar_tensor_tensor(t["x"][:, n, :], down[c % 2][:, i, :], unit_w[:, q, n:n + 1],
                                                            t["x"][:, n, :], ALU.mult, ALU.add)
                        last.then_inc(s["added"], 1)

                    split(0)
                    for c in range(TURN):
                        turn.wait(eng, "slope", c + 1)
                        own.step(eng.tensor_tensor(leaky[:, c % 2, :], gate[c % 2][:], slope[:, c % 2, :], ALU.max))
                        if c >= 1:
                            add_down(c - 1)
                        if c == 1:
                            split(1)
                        own.settle()
                        turn.wait(eng, "hid_lo", c - 1)
                        eng.tensor_tensor(hid[:, c % 2, :], leaky[:, c % 2, :], up[c % 2][:], ALU.mult
                                          ).then_inc(s["hidden"], 1)
                    add_down(TURN - 1)
                    turn.wait(eng, "added", TURN)
                    assert own.n == marks["dve"]



def relative_bias(nc, t, w):
    names = ["in", "dve", "act_in", "act_out", "tr", "tr_free", "tr_hi", "mm", "pool_in", "pool_out", "out"]
    NS = 2
    with tensors(nc) as (sb, ps):
        vec = {n: sb(f"rb_{n}", [P, D]) for n in ("w0", "b0", "g0", "b1", "g1")}
        w1 = sb("rb_w1", [P, KD, D])
        w1h, w1l = (sb(f"rb_w1{n}", [P, KD, D], FR) for n in "hl")
        w2 = sb("rb_w2", [P, KD, P])
        w2h, w2l = (sb(f"rb_w2{n}", [P, KD, P], FR) for n in "hl")
        b2 = sb("rb_b2", [H, 1])
        h = sb("rb_h", [P, NT, D])
        e = sb("rb_e", [P, NT, D])
        stats = sb("rb_stats", [P, NT, 6])
        mv = sb("rb_mv", [P, NT, 2])
        rstd = sb("rb_rstd", [P, NT])
        hth, htl = (sb(f"rb_ht{n}", [P, KD, S], FR) for n in "hl")
        brow = sb("rb_brow", [H, BROW])
        tr = [ps(f"rb_tr{n}", [P, KD * P]) for n in range(2)]
        mm = ps("rb_mm", [P, NT, D])
        with Phase(nc, t, names) as (block, s):
            @block.sync
            def _(eng):
                eng.dma_start(t["dist"][:], t["in_dist"]).then_inc(s["in"], 16)
                for n in vec:
                    eng.dma_start(vec[n][:], rows(w[n])).then_inc(s["in"], 16)
                eng.dma_start(w1[:], w["w1"].rearrange("(k p) n -> p k n", p=P)).then_inc(s["in"], 16)
                eng.wait_ge(s["dve"], 1)
                eng.dma_start(w2[:, :, 0:H], w["w2"].rearrange("(k p) n -> p k n", p=P)).then_inc(s["in"], 16)
                eng.dma_start(b2[:], w["b2"].rearrange("(n o) -> n o", o=1)).then_inc(s["in"], 16)
                eng.wait_ge(s["in"], 16 * 9)
                eng.wait_ge(s["out"], 1)
                eng.dma_start(t["brow"], brow[:]).then_inc(s["in"], 16)
                eng.wait_ge(s["in"], 16 * 10)
                eng.dma_start(t["bands"], bass.AP(t["brow"].tensor, P - 1, [[BROW, H], [-1, P], [1, S]])
                              ).then_inc(t["bands_sem"], 16)

            @block.vector
            def _(eng):
                own = Own(eng, s["dve"])
                own.step(eng.memset(w2[:], 0.0))
                own.step(eng.memset(brow[:], -BIG))
                eng.wait_ge(s["in"], 16 * 9)
                own.settle()
                for full, hi in ((w1, w1h), (w2, w2h)):
                    own.step(eng.tensor_copy(hi[:], full[:]))
                own.settle()
                for full, hi, lo in ((w1, w1h, w1l), (w2, w2h, w2l)):
                    own.step(eng.tensor_tensor(lo[:], full[:], f32(hi[:]), ALU.subtract))
                for n in range(NT):
                    own.step(eng.scalar_tensor_tensor(h[:, n, :], vec["w0"][:], t["dist"][:, n:n + 1], vec["b0"][:],
                                                      ALU.mult, ALU.add))
                for layer in range(NS):
                    g = vec[f"g{layer}"]
                    if layer:
                        eng.wait_ge(s["mm"], 1)
                        own.step(eng.tensor_tensor(h[:], mm[:], vec["b1"][:].unsqueeze(1).to_broadcast([P, NT, D]),
                                                   ALU.add))
                    own.settle()
                    for n in range(NT):
                        own.step(eng.bn_stats(stats[:, n, :], h[:, n, :]))
                    own.settle()
                    for n in range(NT):
                        own.step(eng.bn_aggr(mv[:, n, :], stats[:, n, :]))
                    own.settle()
                    eng.tensor_scalar(rstd[:], mv[:, :, 1], EPS, None, ALU.add).then_inc(s["act_in"], 1)
                    eng.wait_ge(s["act_out"], 2 * layer + 1)
                    own.step(eng.reciprocal(rstd[:], rstd[:]))
                    own.settle()
                    for n in range(NT):
                        own.step(eng.tensor_scalar(h[:, n, :], h[:, n, :], mv[:, n, 0:1], rstd[:, n:n + 1],
                                                   ALU.subtract, ALU.mult))
                    own.settle()
                    eng.tensor_tensor(h[:], h[:], g[:].unsqueeze(1).to_broadcast([P, NT, D]), ALU.mult
                                      ).then_inc(s["act_in"], 1)
                    eng.wait_ge(s["act_out"], 2 * layer + 2)
                    own.step(eng.tensor_scalar(e[:], e[:], 1.0, None, ALU.add))
                    own.settle()
                    own.step(eng.reciprocal(e[:], e[:]))
                    own.settle()
                    eng.tensor_tensor(h[:], h[:], e[:], ALU.mult).then_inc(s["pool_out"], 1)
                    for n in range(NT):
                        eng.wait_ge(s["tr_hi"], NT * layer + n + 1)
                        eng.tensor_tensor(htl[:, :, n * P:(n + 1) * P], tr[n % 2][:].rearrange("p (k i) -> p k i", k=KD),
                                          f32(hth[:, :, n * P:(n + 1) * P]), ALU.subtract).then_inc(s["tr_free"], 1)
                eng.wait_ge(s["mm"], 2)
                eng.tensor_scalar(brow[:, 0:S], mm[0:H, 0:S // D, :].rearrange("p a b -> p (a b)"), b2[:], None, ALU.add
                                  ).then_inc(s["out"], 1)

            @block.scalar
            def _(eng):
                for layer in range(NS):
                    eng.wait_ge(s["act_in"], 2 * layer + 1)
                    eng.activation(rstd[:], rstd[:], ACT.Sqrt).then_inc(s["act_out"], 1)
                    eng.wait_ge(s["act_in"], 2 * layer + 2)
                    eng.activation(e[:], h[:], ACT.Exp, scale=-1.0).then_inc(s["act_out"], 1)
                    for n in range(NT):
                        if layer and n == 0:
                            eng.wait_ge(s["mm"], 1)
                        eng.wait_ge(s["tr"], NT * layer + n + 1)
                        eng.activation(hth[:, :, n * P:(n + 1) * P], tr[n % 2][:].rearrange("p (k i) -> p k i", k=KD),
                                       ACT.Copy).then_inc(s["tr_hi"], 1)

            @block.tensor
            def _(eng):
                for layer in range(NS):
                    eng.wait_ge(s["pool_out"], layer + 1)
                    for n in range(NT):
                        if NT * layer + n >= 2:
                            eng.wait_ge(s["tr_free"], NT * layer + n - 1)
                        for k in range(KD):
                            last = eng.transpose(tr[n % 2][:, k * P:(k + 1) * P], h[:, n, k * P:(k + 1) * P],
                                                 t["ident"][:])
                        last.then_inc(s["tr"], 1)
                    eng.wait_ge(s["tr_free"], NT * (layer + 1))
                    if layer == 0:
                        for n in range(NT):
                            for k in range(KD):
                                last = three_products(eng, mm[:, n, :], [x[:, k, n * P:(n + 1) * P] for x in (hth, htl)],
                                                      [x[:, k, :] for x in (w1h, w1l)], k == 0, k == KD - 1)
                    else:
                        for c in range(S // BANK):
                            for k in range(KD):
                                last = three_products(
                                    eng, mm[:, 2 * c:2 * c + 2, :].rearrange("p a b -> p (a b)"),
                                    [x[:, k, :] for x in (w2h, w2l)],
                                    [x[:, k, c * BANK:(c + 1) * BANK] for x in (hth, htl)], k == 0, k == KD - 1)
                    last.then_inc(s["mm"], 1)


def layer_weights(nc, t, w, cond, normed):
    names = ["in", "dve", "act", "fold", "null_mm", "pool"]
    with tensors(nc) as (sb, ps):
        wq = sb("lw_wq", [P, KD, H * DH])
        prod = sb("lw_prod", [P, KD, H * DH])
        wx = sb("lw_wx", [P, KD, 2 * DH + H])
        wo = sb("lw_wo", [P, NPAIR, D])
        gain = sb("lw_gain", [P, KD])
        k0 = sb("lw_k0", [P, DH])
        k0n = sb("lw_k0n", [P, DH])
        qs = sb("lw_qs", [P, DH])
        ss = sb("lw_ss", [P, 1])
        v0 = sb("lw_v0", [P, 1])
        v0m = sb("lw_v0m", [P, NPAIR * H])
        vps = ps("lw_vps", [H, D])
        n_in = 16 * (9 + 2 * normed)
        with Phase(nc, t, names) as (block, s):
            @block.sync
            def _(eng):
                def load(dst, src):
                    eng.dma_start(dst, src).then_inc(s["in"], 16)

                load(wq[:], w["Wq"].rearrange("(k p) n -> p k n", p=P))
                load(wx[:, :, 0:2 * DH], w["Wkv"].rearrange("(k p) n -> p k n", p=P))
                load(gain[:], w["g_norm"])
                load(k0[:], rows(cond[0, :]))
                for c in range(2):
                    load(v0[c * DH:(c + 1) * DH, :], cond[1, :].rearrange("(d o) -> d o", o=1))
                if normed:
                    load(t["kscale"][:], rows(w["k_scale"]))
                    load(qs[:], rows(w["q_scale"]))
                load(t["null_bias"][:], rows(w["null_attn_bias"]))
                load(t["gain_out"][:], rows(w["g_out"]))
                load(wo[:], w["Wout"].rearrange("(a p) n -> p a n", p=P))
                eng.wait_ge(s["in"], n_in)

            @block.vector
            def _(eng):
                own = Own(eng, s["dve"])
                own.step(eng.memset(v0m[:], 0.0))
                eng.wait_ge(s["in"], n_in)
                own.settle()
                for c in range(2):
                    last = eng.tensor_copy(v0m[c * DH:(c + 1) * DH, c:c + (H + 2) * (NPAIR - 1) + 1:H + 2],
                                           v0[c * DH:(c + 1) * DH, :].to_broadcast([DH, NPAIR]))
                last.then_inc(s["fold"], 1)
                for k in range(KD):
                    own.step(eng.tensor_scalar(wq[:, k, :], wq[:, k, :], gain[:, k:k + 1], None, ALU.mult))
                    own.step(eng.tensor_scalar(wx[:, k, 0:2 * DH], wx[:, k, 0:2 * DH], gain[:, k:k + 1], None, ALU.mult))
                if normed:
                    own.step(eng.scalar_tensor_tensor(t["kscale"][:], t["kscale"][:], 8.0, qs[:], ALU.mult, ALU.mult))
                    own.step(eng.tensor_tensor(k0n[:], k0[:], k0[:], ALU.mult))
                    own.settle()
                    own.step(eng.tensor_reduce(ss[:], k0n[:], AX.X, ALU.add))
                    own.settle()
                    eng.sem_inc(s["pool"], 1)
                    eng.wait_ge(s["act"], 1)
                    own.step(eng.tensor_scalar(ss[:], ss[:], 1e-12, None, ALU.max))
                    own.settle()
                    own.step(eng.reciprocal(ss[:], ss[:]))
                    own.settle()
                    own.step(eng.scalar_tensor_tensor(k0n[:], k0[:], ss[:, 0:1], t["kscale"][:], ALU.mult, ALU.mult))
                else:
                    own.step(eng.tensor_scalar(k0n[:], k0[:], DH ** -0.5, None, ALU.mult))
                own.settle()
                for k in range(KD):
                    own.step(eng.tensor_tensor(prod[:, k, :].rearrange("p (h d) -> p h d", h=H),
                                               wq[:, k, :].rearrange("p (h d) -> p h d", h=H),
                                               k0n[:].unsqueeze(1).to_broadcast([P, H, DH]), ALU.mult))
                own.settle()
                for k in range(KD):
                    own.step(eng.tensor_reduce(wx[:, k, 2 * DH:], prod[:, k, :].rearrange("p (h d) -> p h d", h=H),
                                               AX.X, ALU.add))
                own.settle()
                for full, hi in ((wq, "wq_h"), (wx, "wx_h"), (wo, "wo_h")):
                    own.step(eng.tensor_copy(t[hi][:], full[:]))
                own.settle()
                for full, hi, lo in ((wq, "wq_h", "wq_l"), (wx, "wx_h", "wx_l"), (wo, "wo_h", "wo_l")):
                    own.step(eng.tensor_tensor(t[lo][:], full[:], f32(t[hi][:]), ALU.subtract))
                eng.wait_ge(s["null_mm"], 1)
                own.step(eng.tensor_copy(t["null_out"][:], vps[:]))
                own.settle()

            @block.scalar
            def _(eng):
                if normed:
                    eng.wait_ge(s["pool"], 1)
                    eng.activation(ss[:], ss[:], ACT.Sqrt).then_inc(s["act"], 1)

            @block.tensor
            def _(eng):
                eng.wait_ge(s["in"], n_in)
                eng.wait_ge(s["fold"], 1)
                for a in range(NPAIR):
                    last = eng.matmul(vps[:], v0m[:, a * H:(a + 1) * H], wo[:, a, :], start=a == 0, stop=a == NPAIR - 1)
                last.then_inc(s["null_mm"], 1)


def project(nc, t, b, mask, normed):
    names = ["mask_in", "dve", "var", "std", "xn", "xtr", "xt_hi", "xt_lo", "q", "kv", "q_copy", "kv_copy", "sumsq",
             "norm", "q_ready", "q_hi", "q_lo", "k_ready", "tr", "out", "store0", "store1"]
    NG = 4
    GR = 1 + H // NG
    with tensors(nc) as (sb, ps):
        mask8 = sb("pj_mask8", [P, NT], U8)
        pen = sb("pj_pen", [P, NT])
        xb = sb("pj_xb", [P, NT, D])
        stats = sb("pj_stats", [P, NT, 6])
        mv = sb("pj_mv", [P, NT, 2])
        rstd = sb("pj_rstd", [P, NT])
        xth, xtl = (sb(f"pj_xt{n}", [P, KD, S], FR) for n in "hl")
        qs = sb("pj_qs", [P, 2, H * DH])
        sq = sb("pj_sq", [P, 2, H * DH])
        kvs = sb("pj_kvs", [P, 2, 2 * DH + H])
        ksq = sb("pj_ksq", [P, DH])
        ss = sb("pj_ss", [P, 2, H + 1])
        kn = sb("pj_kn", [P, DH])
        nul = sb("pj_nul", [P, H])
        qhl = sb("pj_qhl", [P, 2, H, 2 * DH], FR)
        khl = sb("pj_khl", [P, 2, 2 * P], FR)
        qt = sb("pj_qt", [P, 2, H, P], FR)
        xtr = ps("pj_xtr", [P, BANK])[:, 0:KD * P]
        qps = [ps(f"pj_q{n}", [P, H * DH]) for n in range(2)]
        kvp = ps("pj_kv", [P, BANK])
        trs = [ps(f"pj_tr{n}", [P, NG * P]) for n in range(2)]
        with Phase(nc, t, names) as (block, s):
            @block.sync
            def _(eng):
                eng.dma_start(mask8[:], mask[bass.ds(b, 1), :, :].rearrange("o p t -> p (o t)")
                              ).then_inc(s["mask_in"], 16)
                for n in range(NT):
                    eng.wait_ge(s["out"], GR * (n + 1))
                    eng.dma_start(t["q_dram"][:, :, n * P:(n + 1) * P].rearrange("h p i -> p h i"), f32(qt[:, n % 2, :, :])
                                  ).then_inc(s[f"store{n % 2}"], 16)
                eng.wait_ge(s["mask_in"], 16)
                eng.wait_ge(s["store0"], 16 * NT // 2)
                eng.wait_ge(s["store1"], 16 * NT // 2)

            @block.tensor
            def _(eng):
                def x_transpose(n):
                    eng.wait_ge(s["xn"], n + 1)
                    if n:
                        eng.wait_ge(s["xt_lo"], n)
                    for k in range(KD):
                        last = eng.transpose(xtr[:, k * P:(k + 1) * P], xb[:, n, k * P:(k + 1) * P], t["ident"][:])
                    last.then_inc(s["xtr"], 1)

                def projections(n):
                    eng.wait_ge(s["xt_lo"], n + 1)
                    if n >= 2:
                        eng.wait_ge(s["q_lo"], n - 1)
                    left = [[x[:, k, n * P:(n + 1) * P] for x in (xth, xtl)] for k in range(KD)]
                    for c in range(H * DH // BANK):
                        for k in range(KD):
                            last = three_products(eng, qps[n % 2][:, c * BANK:(c + 1) * BANK], left[k],
                                                  [t[x][:, k, c * BANK:(c + 1) * BANK] for x in ("wq_h", "wq_l")],
                                                  k == 0, k == KD - 1)
                    last.then_inc(s["q"], 1)
                    if n:
                        eng.wait_ge(s["kv_copy"], n)
                    for k in range(KD):
                        last = three_products(eng, kvp[:, 0:2 * DH + H], left[k], [t[x][:, k, :] for x in ("wx_h", "wx_l")],
                                              k == 0, k == KD - 1)
                    last.then_inc(s["kv"], 1)

                def head_transposes(n):
                    for g in range(GR):
                        m = n * GR + g
                        if g == 0:
                            eng.wait_ge(s["k_ready"], n + 1)
                            blocks = [khl[:, n % 2, c * P:(c + 1) * P] for c in range(2)]
                        else:
                            eng.wait_ge(s["q_lo"], n + 1)
                            blocks = [qhl[:, n % 2, (g - 1) * NG + c, :] for c in range(NG)]
                        if m >= 2:
                            eng.wait_ge(s["out"], m - 1)
                        for c, block in enumerate(blocks):
                            last = eng.transpose(trs[m % 2][:, c * P:(c + 1) * P].bitcast(FR), block, t["ident_r"][:])
                        last.then_inc(s["tr"], 1)

                x_transpose(0)
                for n in range(NT):
                    projections(n)
                    if n + 1 < NT:
                        x_transpose(n + 1)
                    if n:
                        head_transposes(n - 1)
                head_transposes(NT - 1)

            def evacuate(eng, n, g, copy):
                m = n * GR + g
                eng.wait_ge(s["tr"], m + 1)
                if m:
                    eng.wait_ge(s["out"], m)
                if g == 0:
                    copy(t["k_hh"][:, n * P:(n + 1) * P], trs[m % 2][:, 0:P])
                    copy(t["k_lp"][:, n * P:(n + 1) * P], trs[m % 2][:, P:2 * P]).then_inc(s["out"], 1)
                else:
                    if n >= 2:
                        eng.wait_ge(s[f"store{n % 2}"], 16 * (n // 2))
                    copy(qt[:, n % 2, (g - 1) * NG:g * NG, :].rearrange("p h i -> p (h i)"), trs[m % 2][:]
                         ).then_inc(s["out"], 1)

            @block.vector
            def _(eng):
                own = Own(eng, s["dve"])
                for tile in (0, 1):
                    own.step(eng.memset(f32(khl[:, tile, P:2 * P]), 0.0))
                own.step(eng.tensor_copy(xb[:], t["x"][:, bass.ds(b * NT, NT), :]))
                eng.wait_ge(s["mask_in"], 16)
                own.step(eng.tensor_copy(pen[:], mask8[:]))
                own.settle()
                own.step(eng.tensor_scalar(pen[:], pen[:], BIG, -BIG, ALU.mult, ALU.add))
                for n in range(NT):
                    own.step(eng.bn_stats(stats[:, n, :], xb[:, n, :]))
                own.settle()
                for n in range(NT):
                    own.step(eng.bn_aggr(mv[:, n, :], stats[:, n, :]))
                own.settle()
                eng.tensor_scalar(rstd[:], mv[:, :, 1], EPS, None, ALU.add).then_inc(s["var"], 1)
                eng.wait_ge(s["std"], 1)
                own.step(eng.reciprocal(rstd[:], rstd[:]))
                own.settle()
                for n in range(NT):
                    eng.tensor_scalar(xb[:, n, :], xb[:, n, :], mv[:, n, 0:1], rstd[:, n:n + 1],
                                      ALU.subtract, ALU.mult).then_inc(s["xn"], 1)

                def x_low(n):
                    eng.wait_ge(s["xt_hi"], n + 1)
                    eng.tensor_tensor(xtl[:, :, n * P:(n + 1) * P], xtr.rearrange("p (k i) -> p k i", k=KD),
                                      f32(xth[:, :, n * P:(n + 1) * P]), ALU.subtract).then_inc(s["xt_lo"], 1)

                x_low(0)
                for n in range(NT):
                    if n + 1 < NT:
                        x_low(n + 1)
                    c = n % 2
                    eng.wait_ge(s["kv_copy"], n + 1)
                    if n:
                        eng.wait_ge(s["k_ready"], n)
                    heads = sq[:, c, :].rearrange("p (h d) -> p h d", h=H)
                    if normed:
                        own.step(eng.tensor_tensor(ksq[:], kvs[:, c, 0:DH], kvs[:, c, 0:DH], ALU.mult))
                        own.settle()
                        own.step(eng.tensor_reduce(ss[:, c, H:H + 1], ksq[:], AX.X, ALU.add))
                        eng.wait_ge(s["q_copy"], n + 1)
                        own.step(eng.tensor_reduce(ss[:, c, 0:H], heads, AX.X, ALU.add))
                        own.settle()
                        eng.sem_inc(s["sumsq"], 1)
                        eng.wait_ge(s["norm"], n + 1)
                        own.step(eng.tensor_scalar(ss[:, c, :], ss[:, c, :], 1e-12, None, ALU.max))
                        own.settle()
                        own.step(eng.reciprocal(ss[:, c, :], ss[:, c, :]))
                        own.settle()
                        own.step(eng.scalar_tensor_tensor(kn[:], kvs[:, c, 0:DH], ss[:, c, H:H + 1], t["kscale"][:],
                                                          ALU.mult, ALU.mult))
                        own.step(eng.tensor_tensor(nul[:], kvs[:, c, 2 * DH:], ss[:, c, 0:H], ALU.mult))
                        eng.tensor_tensor(qs[:, c, :].rearrange("p (h d) -> p h d", h=H),
                                          qs[:, c, :].rearrange("p (h d) -> p h d", h=H),
                                          ss[:, c, 0:H].unsqueeze(2).to_broadcast([P, H, DH]), ALU.mult
                                          ).then_inc(s["q_ready"], 1)
                    else:
                        own.step(eng.tensor_scalar(kn[:], kvs[:, c, 0:DH], DH ** -0.5, None, ALU.mult))
                        own.step(eng.tensor_copy(nul[:], kvs[:, c, 2 * DH:]))
                    if n >= 2:
                        eng.wait_ge(s["tr"], GR * (n - 2) + 1)
                    own.settle()
                    own.step(eng.tensor_copy(khl[:, c, 0:DH], kn[:]))
                    own.step(eng.tensor_copy(khl[:, c, DH:2 * DH], kn[:]))
                    own.step(eng.tensor_copy(khl[:, c, 3 * DH:3 * DH + 1], pen[:, n:n + 1]))
                    own.step(eng.scalar_tensor_tensor(t["neg_null"][:, n, :], nul[:], -1.0, t["null_bias"][:],
                                                      ALU.mult, ALU.subtract))
                    own.settle()
                    eng.tensor_tensor(khl[:, c, 2 * DH:3 * DH], kn[:], f32(khl[:, c, 0:DH]), ALU.subtract
                                      ).then_inc(s["k_ready"], 1)
                    eng.wait_ge(s["q_hi"], n + 1)
                    source = (qs[:, c, :] if normed else qps[c][:]).rearrange("p (h d) -> p h d", h=H)
                    eng.tensor_tensor(qhl[:, c, :, DH:], source, f32(qhl[:, c, :, 0:DH]), ALU.subtract
                                      ).then_inc(s["q_lo"], 1)
                    if n:
                        for g in range(0, GR, 2):
                            evacuate(eng, n - 1, g, eng.tensor_copy)
                for g in range(0, GR, 2):
                    evacuate(eng, NT - 1, g, eng.tensor_copy)

            @block.scalar
            def _(eng):
                def copy(out, in_):
                    return eng.activation(out, in_, ACT.Copy)

                eng.wait_ge(s["var"], 1)
                eng.activation(rstd[:], rstd[:], ACT.Sqrt).then_inc(s["std"], 1)

                def x_high(n):
                    eng.wait_ge(s["xtr"], n + 1)
                    eng.activation(xth[:, :, n * P:(n + 1) * P], xtr.rearrange("p (k i) -> p k i", k=KD), ACT.Copy
                                   ).then_inc(s["xt_hi"], 1)

                x_high(0)
                for n in range(NT):
                    c = n % 2
                    if n + 1 < NT:
                        x_high(n + 1)
                    if n >= 2:
                        eng.wait_ge(s["q_lo"], n - 1)
                        eng.wait_ge(s["k_ready"], n - 1)
                    if normed:
                        eng.wait_ge(s["q"], n + 1)
                        eng.activation(qs[:, c, :], qps[c][:], ACT.Copy)
                        eng.activation(sq[:, c, :], qps[c][:], ACT.Square).then_inc(s["q_copy"], 1)
                    eng.wait_ge(s["kv"], n + 1)
                    eng.activation(t["v"][:, n, :], kvp[:, DH:2 * DH], ACT.Copy)
                    eng.activation(kvs[:, c, :], kvp[:, 0:2 * DH + H], ACT.Copy).then_inc(s["kv_copy"], 1)
                    if normed:
                        eng.wait_ge(s["sumsq"], n + 1)
                        eng.activation(ss[:, c, :], ss[:, c, :], ACT.Sqrt).then_inc(s["norm"], 1)
                        eng.wait_ge(s["q_ready"], n + 1)
                    else:
                        eng.wait_ge(s["q"], n + 1)
                    if n >= 2:
                        eng.wait_ge(s["tr"], GR * (n - 1))
                    source = (qs[:, c, :] if normed else qps[c][:]).rearrange("p (h d) -> p h d", h=H)
                    eng.activation(qhl[:, c, :, 0:DH], source, ACT.Copy).then_inc(s["q_hi"], 1)
                    if n:
                        for g in range(1, GR, 2):
                            evacuate(eng, n - 1, g, copy)
                for g in range(1, GR, 2):
                    evacuate(eng, NT - 1, g, copy)


def attend(nc, t, bias):
    HP = 2
    U = HP * NT * 2
    GU = 8
    NGRP = U // GU
    TURNS = NPAIR // HP
    NBIAS = 4
    VSTEPS = 4
    SKEW = VSTEPS + 1
    toeplitz = bias is None
    n_bias = HP * 2 if toeplitz else U

    pieces, starts = [], []
    for u in range(U):
        n = (u // 2) % NT + 1
        starts.append(len(pieces))
        pieces += [(at, min(4, n - at)) for at in range(0, n, 4)]
    NPC = len(pieces)
    assert NPC % 2 == 0 and U % NBIAS == 0 and NGRP % 2 == 0

    def first(u):
        return u // U * NPC + starts[u % U]

    marks = dict(qk=U, biased=U, exp=U, tr=NPC, ev_a=NPC // 2, ev_d=NPC // 2, pv=NGRP, null_d=NGRP, null_e=NGRP,
                 inv_b=NGRP, bc=NGRP, bc_s=NGRP, out=NGRP, diag=U, nulls=HP, sums=3 * NGRP)
    names = list(marks) + ["q0", "q1", "ones", "gate"] + [f"bias{n}" for n in range(NBIAS)]

    NARROW = BANK - P

    def weights_at(g, j):
        full = 4 * (g % 2)
        return min(j, full) * BANK + max(0, j - full) * NARROW

    def unit(u):
        tile = (u // 2) % NT
        return u % U // (2 * NT), tile, u % 2, (tile + 1) * P

    def run(eng, step):
        def steps(it, at, to, has):
            for u in range(at, to):
                step(it, u, has)

        def peeled(it):
            return lambda n, per: 0 <= it * per + n < TURNS * per

        steps(-1, U - 2, U + SKEW, peeled(-1))
        with eng.Fori(0, TURNS - 1) as it:
            steps(it, SKEW, U + SKEW, lambda n, per: True)
        steps(TURNS - 1, SKEW, U + SKEW, peeled(TURNS - 1))

    with tensors(nc) as (sb, ps):
        q_hl = sb("at_q_hl", [P, HP, 2, S], FR)
        q_h1 = sb("at_q_h1", [P, HP, 2, S], FR)
        bt = sb("at_bias", [P, NBIAS, S])
        neg = sb("at_neg", [P, 2, S])
        prob = sb("at_prob", [P, 2, S])
        pt = [sb(f"at_pt{n}", [P, 2, 4 * n * BANK + 3 * NARROW + BANK]) for n in range(2)]
        nmax, rsum, nd, p0, inv = (sb(f"at_{n}", [P, 2, GU]) for n in ("nmax", "rsum", "nd", "p0", "inv"))
        inv_b = sb("at_inv_b", [P, GU, DH])
        bc_s = sb("at_bc_s", [P, BANK])
        nn = sb("at_nn", [P, NT, 2 * HP])
        s_ps = [ps(f"at_s{n}", [P, S]) for n in range(2)]
        t_ps = [ps(f"at_t{n}", [P, BANK]) for n in range(2)]
        o_ps = ps("at_o", [P, BANK])
        b_ps = ps("at_b", [P, BANK])

        def evacuate(eng, turn, u, n, copy, parity, name):
            m = first(u) + n
            if m >= first(u + 1) or m % 2 != parity:
                return
            turn.wait(eng, "tr", m + 1)
            turn.wait(eng, "pv", u // GU - 1)
            at, blocks = pieces[m % NPC]
            col = ((u // 2) % 4) * P
            g = u // GU % 2
            here = weights_at(g, at) + col
            one = pt[g][:, u % 2, here:here + P]
            pitch = BANK if at < 4 * g else NARROW
            copy(bass.AP(one.tensor, one.offset, [one.ap[0], [pitch, blocks], [1, P]]),
                 t_ps[parity][:, 0:blocks * P].rearrange("p (c i) -> p c i", i=P)).then_inc(s[name], 1)

        with Phase(nc, t, names) as (block, s):
            @block.sync
            def _(eng):
                if toeplitz:
                    eng.wait_ge(t["bands_sem"], t["bands_n"])
                with eng.Fori(0, TURNS) as it:
                    turn = Turns(s, it, marks)

                    def queries(p):
                        turn.wait(eng, "qk", (p + 1) * 2 * NT - U)
                        two = bass.ds(it * 2 * HP + 2 * p, 2)
                        eng.dma_start(f32(q_hl[:, p, :, :]), t["q_dram"][two, :, :].rearrange("h p i -> p h i")
                                      ).then_inc(s[f"q{p}"], 16)
                        eng.dma_start(f32(q_h1[0:DH, p, :, :]), t["q_dram"][two, 0:DH, :].rearrange("h p i -> p h i")
                                      ).then_inc(s[f"q{p}"], 16)

                    for n in range(n_bias):
                        if n % (n_bias // HP) == 0:
                            queries(n // (n_bias // HP))
                        slot = n % NBIAS
                        if toeplitz:
                            turn.wait(eng, "biased", (n // 2) * 2 * NT + 2 * (NT - 1) + n % 2 + 1 - U)
                            head = bass.ds(it * 2 * HP + n, 1)
                            eng.dma_start(bt[:, slot, :], t["bands"][head, :, :].rearrange("o p c -> p (o c)")
                                          ).then_inc(s[f"bias{slot}"], 16)
                        else:
                            p, tile, side, width = unit(n)
                            turn.wait(eng, "biased", n + 1 - NBIAS)
                            head = bass.ds(it * 2 * HP + 2 * p + side, 1)
                            eng.dma_start(bt[:, slot, 0:width],
                                          bias[head, tile * P:(tile + 1) * P, 0:width].rearrange("o p c -> p (o c)")
                                          ).then_inc(s[f"bias{slot}"], 16)
                for p in range(HP):
                    eng.wait_ge(s[f"q{p}"], 32 * TURNS)
                for n in range(NBIAS):
                    eng.wait_ge(s[f"bias{n}"], 16 * TURNS * n_bias // NBIAS)

            @block.tensor
            def _(eng):
                def logits(it, u):
                    turn = Turns(s, it, marks)
                    p, tile, side, width = unit(u)
                    if u % (2 * NT) == 0:
                        eng.wait_ge(s[f"q{p}"], it * 32 + 32 * (u // U + 1))
                    turn.wait(eng, "biased", u - 1)
                    at = slice(tile * P, (tile + 1) * P)
                    for c in range(0, width, BANK):
                        n = min(BANK, width - c)
                        out = s_ps[u % 2][:, c:c + n]
                        eng.matmul(out, q_hl[:, p, side, at], t["k_hh"][:, c:c + n], start=True, stop=False)
                        last = eng.matmul(out, q_h1[0:DH + 1, p, side, at], t["k_lp"][0:DH + 1, c:c + n],
                                          start=False, stop=True)
                    last.then_inc(s["qk"], 1)

                def transposes(turn, u, n):
                    m = first(u) + n
                    if m >= first(u + 1):
                        return
                    turn.wait(eng, "exp", u + 1)
                    turn.wait(eng, ("ev_a", "ev_d")[m % 2], m // 2)
                    at, blocks = pieces[m % NPC]
                    for c in range(blocks):
                        last = eng.transpose(t_ps[m % 2][:, c * P:(c + 1) * P],
                                             prob[:, u % 2, (at + c) * P:(at + c + 1) * P], t["ident"][:])
                    last.then_inc(s["tr"], 1)

                def values(turn, g, part):
                    m = first(GU * (g + 1))
                    turn.wait(eng, "ev_a", m // 2)
                    turn.wait(eng, "ev_d", m // 2)
                    turn.wait(eng, "out", g)
                    blocks = 4 * (g % 2) + 4
                    share = blocks // VSTEPS
                    for j in range(part * share, (part + 1) * share):
                        i0 = max(0, j - (blocks - 4)) * P
                        at = weights_at(g, j)
                        for side in range(2):
                            last = eng.matmul(o_ps[side * DH:(side + 1) * DH, i0:BANK], t["v"][:, j, :],
                                              pt[g % 2][:, side, at + i0:at + BANK], start=j == 0, stop=j == blocks - 1)
                    if part == VSTEPS - 1:
                        last.then_inc(s["pv"], 1)

                def broadcast(turn, g):
                    turn.wait(eng, "inv_b", g + 1)
                    turn.wait(eng, "bc_s", g)
                    for c in range(4):
                        last = eng.transpose(b_ps[:, c * P:(c + 1) * P],
                                             inv_b[:, 2 * c:2 * c + 2, :].rearrange("p s d -> p (s d)"), t["ident"][:])
                    last.then_inc(s["bc"], 1)

                def step(it, u, has):
                    turn = Turns(s, it, marks)
                    if has(u + 2, U):
                        logits(it, u + 2)
                    if has(u, U):
                        transposes(turn, u, 0)
                        transposes(turn, u, 1)
                    g = u // GU - 1
                    if u % GU < VSTEPS and has(g, NGRP):
                        values(turn, g, u % GU)
                    if u % GU == 2 and has(g, NGRP):
                        broadcast(turn, g)

                start(eng, s, marks, "qk", "tr", "pv", "bc")
                eng.wait_ge(s["ones"], 1)
                run(eng, step)

            @block.vector
            def _(eng):
                start(eng, s, marks, "biased", "ev_d", "null_d", "nulls", "sums", "inv_b", "out")
                for p in range(HP):
                    for side in range(2):
                        last = eng.memset(f32(q_h1[DH:DH + 1, p, side, :]), 1.0)
                last.then_inc(s["ones"], 1)

                def null_logits(turn, it, pair):
                    p = pair % HP
                    turn.wait(eng, "null_d", 2 * (pair - HP) + 2)
                    eng.sem_inc(s["gate"], 1)
                    eng.tensor_copy(nn[:, :, 2 * p:2 * p + 2], t["neg_null"][:, :, bass.ds(it * 2 * HP + 2 * pair, 2)]
                                    ).then_inc(s["nulls"], 1)
                    turn.wait(eng, "nulls", pair + 1)

                def add_bias(turn, it, u):
                    p, tile, side, width = unit(u)
                    turn.wait(eng, "qk", u + 1)
                    turn.wait(eng, "exp", u - 1)
                    slot, lo = (2 * p + side, S - width) if toeplitz else (u % NBIAS, 0)
                    if not toeplitz:
                        turn.wait(eng, "diag", u + 1)
                    elif tile == 0:
                        eng.wait_ge(s[f"bias{slot}"], it * 16 + 16 * (u // U + 1))
                    eng.sem_inc(s["gate"], 1)
                    eng.tensor_tensor_reduce(
                        out=neg[:, u % 2, 0:width], in0=s_ps[u % 2][:, 0:width], in1=bt[:, slot, lo:lo + width],
                        scale=-1.0, scalar=nn[:, tile, 2 * p + side:2 * p + side + 1], op0=ALU.add, op1=ALU.min,
                        accum_out=nmax[:, (u // GU) % 2, u % GU:u % GU + 1]).then_inc(s["biased"], 1)

                def per_tile(x, g):
                    return x[:, g % 2, :].rearrange("p (t s) -> p t s", s=2)

                def tiles(g):
                    return slice(4 * (g % 2), 4 * (g % 2) + 4)

                def null_shift(turn, g):
                    p = g // 2 % HP
                    turn.wait(eng, "exp", GU * (g + 1))
                    turn.wait(eng, "null_e", g - 1)
                    eng.tensor_tensor(per_tile(nd, g), per_tile(nmax, g), nn[:, tiles(g), 2 * p:2 * p + 2], ALU.subtract
                                      ).then_inc(s["null_d"], 1)

                def sums(turn, it, g):
                    turn.wait(eng, "null_e", g + 1)
                    turn.wait(eng, "inv_b", g - 1)
                    c = g % 2
                    eng.tensor_tensor(inv[:, c, :], p0[:, c, :], rsum[:, c, :], ALU.add).then_inc(s["sums"], 1)
                    turn.wait(eng, "sums", 3 * g + 1)
                    eng.reciprocal(inv[:, c, :], inv[:, c, :]).then_inc(s["sums"], 1)
                    turn.wait(eng, "sums", 3 * g + 2)
                    eng.tensor_tensor(t["null_w"][:, tiles(g), bass.ds(it * 2 * HP + 2 * (g // 2), 2)],
                                      per_tile(p0, g), per_tile(inv, g), ALU.mult).then_inc(s["sums"], 1)
                    turn.wait(eng, "bc", g)
                    eng.tensor_copy(inv_b[:], inv[:, c, :].unsqueeze(2).to_broadcast([P, GU, DH])
                                    ).then_inc(s["inv_b"], 1)

                def output(turn, it, g):
                    turn.wait(eng, "bc_s", g + 1)
                    turn.wait(eng, "pv", g + 1)
                    at = (g % 2) * BANK
                    eng.tensor_tensor(t["o_t"][:, bass.ds(it * HP + g // 2, 1), at:at + BANK
                                               ].rearrange("p o i -> p (o i)"),
                                      o_ps[:], bc_s[:], ALU.mult).then_inc(s["out"], 1)

                def step(it, u, has):
                    turn = Turns(s, it, marks)
                    if has(u + 2, U):
                        if (u + 2) % (2 * NT) == 0:
                            null_logits(turn, it, (u + 2) // (2 * NT))
                        add_bias(turn, it, u + 2)
                    if has(u, U):
                        evacuate(eng, turn, u, 0, eng.tensor_copy, 1, "ev_d")
                        evacuate(eng, turn, u, 1, eng.tensor_copy, 1, "ev_d")
                        if u % GU == GU - 1:
                            null_shift(turn, u // GU)
                    g = u // GU - 1
                    if u % GU == 0 and has(g, NGRP):
                        sums(turn, it, g)
                    if u % GU == VSTEPS and has(g, NGRP):
                        output(turn, it, g)

                run(eng, step)
                eng.wait_ge(s["out"], NGRP * (TURNS + 1))

            @block.scalar
            def _(eng):
                def copy(out, in_):
                    return eng.activation(out, in_, ACT.Copy)

                def exponent(turn, u):
                    width = unit(u)[3]
                    c, i = (u // GU) % 2, u % GU
                    turn.wait(eng, "biased", u + 1)
                    turn.wait(eng, "tr", first(u - 1))
                    turn.wait(eng, "inv_b", u // GU - 1)
                    eng.activation(prob[:, u % 2, 0:width], neg[:, u % 2, 0:width], ACT.Exp, scale=-1.0,
                                   bias=nmax[:, c, i:i + 1], accum_out=rsum[:, c, i:i + 1]).then_inc(s["exp"], 1)

                def null_exponent(turn, g):
                    turn.wait(eng, "null_d", g + 1)
                    turn.wait(eng, "inv_b", g - 1)
                    eng.activation(p0[:, g % 2, :], nd[:, g % 2, :], ACT.Exp).then_inc(s["null_e"], 1)

                def copy_broadcast(turn, g):
                    turn.wait(eng, "bc", g + 1)
                    turn.wait(eng, "out", g)
                    copy(bc_s[:], b_ps[:]).then_inc(s["bc_s"], 1)

                def step(it, u, has):
                    turn = Turns(s, it, marks)
                    if has(u + 1, U):
                        exponent(turn, u + 1)
                    g = u // GU - 1
                    if u % GU == VSTEPS and has(g, NGRP):
                        copy_broadcast(turn, g)
                    if has(u, U):
                        evacuate(eng, turn, u, 0, copy, 0, "ev_a")
                        evacuate(eng, turn, u, 1, copy, 0, "ev_a")
                        if u % GU == GU - 1:
                            null_exponent(turn, u // GU)

                start(eng, s, marks, "exp", "ev_a", "null_e", "bc_s")
                run(eng, step)

            if not toeplitz:
                @block.gpsimd
                def _(eng):
                    start(eng, s, marks, "diag")
                    with eng.Fori(0, TURNS) as it:
                        for u in range(U):
                            tile, width = unit(u)[1], unit(u)[3]
                            slot = u % NBIAS
                            eng.wait_ge(s[f"bias{slot}"], it * (16 * U // NBIAS) + 16 * (u // NBIAS + 1))
                            eng.sem_inc(s["gate"], 1)
                            corner = bt[:, slot, tile * P:width]
                            eng.affine_select(out=corner, in_=corner, compare_op=ALU.is_ge, fill=-BIG, base=0,
                                              pattern=[[-1, P]], channel_multiplier=1).then_inc(s["diag"], 1)


def close_layer(nc, t, b, out):
    names = ["o_hi", "o_lo", "n_tr", "n_copy", "y", "y_copy", "var", "std", "dve", "scaled", "added", "stored"]
    with tensors(nc) as (sb, ps):
        oh, ol = (sb(f"cl_o{n}", [P, 2, NPAIR, P], FR) for n in "hl")
        nwt = sb("cl_nwt", [H, 2, P])
        y = sb("cl_y", [P, NT, D])
        stats = sb("cl_stats", [P, NT, 6])
        mv = sb("cl_mv", [P, NT, 2])
        rstd = sb("cl_rstd", [P, NT])
        yps = [ps(f"cl_y{n}", [P, BANK]) for n in range(2)]
        nps = [ps(f"cl_n{n}", [H, BANK]) for n in range(2)]
        with Phase(nc, t, names) as (block, s):
            @block.scalar
            def _(eng):
                for n in range(NT):
                    if n >= 2:
                        eng.wait_ge(s["y"], n - 1)
                    eng.activation(oh[:, n % 2, :, :], t["o_t"][:, :, n * P:(n + 1) * P], ACT.Copy).then_inc(s["o_hi"], 1)
                    eng.wait_ge(s["n_tr"], n + 1)
                    eng.activation(nwt[:, n % 2, :], nps[n % 2][:, 0:P], ACT.Copy).then_inc(s["n_copy"], 1)
                    if n:
                        eng.wait_ge(s["y"], n)
                        eng.activation(y[:, n - 1, :], yps[(n - 1) % 2][:, 0:D], ACT.Copy).then_inc(s["y_copy"], 1)
                eng.wait_ge(s["y"], NT)
                eng.activation(y[:, NT - 1, :], yps[(NT - 1) % 2][:, 0:D], ACT.Copy).then_inc(s["y_copy"], 1)
                eng.wait_ge(s["var"], 1)
                eng.activation(rstd[:], rstd[:], ACT.Sqrt).then_inc(s["std"], 1)

            @block.tensor
            def _(eng):
                for n in range(NT):
                    if n >= 2:
                        eng.wait_ge(s["n_copy"], n - 1)
                    eng.transpose(nps[n % 2][:, 0:P], t["null_w"][:, n, :], t["ident"][:]).then_inc(s["n_tr"], 1)
                    eng.wait_ge(s["o_lo"], n + 1)
                    if n >= 2:
                        eng.wait_ge(s["y_copy"], n - 1)
                    out_ = yps[n % 2][:, 0:D]
                    for a in range(NPAIR):
                        three_products(eng, out_, [x[:, n % 2, a, :] for x in (oh, ol)],
                                       [t[x][:, a, :] for x in ("wo_h", "wo_l")], a == 0, False)
                    eng.wait_ge(s["n_copy"], n + 1)
                    eng.matmul(out_, nwt[:, n % 2, :], t["null_out"][:], start=False, stop=True).then_inc(s["y"], 1)

            @block.vector
            def _(eng):
                own = Own(eng, s["dve"])
                for n in range(NT):
                    eng.wait_ge(s["o_hi"], n + 1)
                    eng.tensor_tensor(ol[:, n % 2, :, :], t["o_t"][:, :, n * P:(n + 1) * P], f32(oh[:, n % 2, :, :]),
                                      ALU.subtract).then_inc(s["o_lo"], 1)
                    if n:
                        eng.wait_ge(s["y_copy"], n)
                        own.step(eng.bn_stats(stats[:, n - 1, :], y[:, n - 1, :]))
                eng.wait_ge(s["y_copy"], NT)
                own.step(eng.bn_stats(stats[:, NT - 1, :], y[:, NT - 1, :]))
                own.settle()
                for n in range(NT):
                    own.step(eng.bn_aggr(mv[:, n, :], stats[:, n, :]))
                own.settle()
                eng.tensor_scalar(rstd[:], mv[:, :, 1], EPS, None, ALU.add).then_inc(s["var"], 1)
                eng.wait_ge(s["std"], 1)
                own.step(eng.reciprocal(rstd[:], rstd[:]))
                own.settle()
                for n in range(NT):
                    own.step(eng.tensor_scalar(y[:, n, :], y[:, n, :], mv[:, n, 0:1], rstd[:, n:n + 1],
                                               ALU.subtract, ALU.mult))
                own.settle()
                own.step(eng.tensor_tensor(y[:], y[:], t["gain_out"][:].unsqueeze(1).to_broadcast([P, NT, D]), ALU.mult))
                own.settle()
                x = t["x"][:, bass.ds(b * NT, NT), :]
                if out is None:
                    own.step(eng.tensor_tensor(x, x, y[:], ALU.add))
                    own.settle()
                else:
                    eng.tensor_tensor(y[:], x, y[:], ALU.add).then_inc(s["added"], 1)

            if out is not None:
                @block.sync
                def _(eng):
                    eng.wait_ge(s["added"], 1)
                    eng.dma_start(out[bass.ds(b, 1), :, :].rearrange("o (t p) d -> p (o t) d", p=P), y[:]
                                  ).then_inc(s["stored"], 16)
                    eng.wait_ge(s["stored"], 16)


def program(nc, a, out):
    q_dram = nc.dram_tensor("q_dram", [H, P, S], F32, kind="Internal").ap()
    brow = nc.dram_tensor("brow_dram", [H, BROW], F32, kind="Internal").ap()
    with ExitStack() as stack, tensors(nc) as (sb, _):
        bands = nc.dram_tensor("bands_dram", [H, P, S], F32, kind="Internal").ap()
        t = {"in_ident": a["ident"], "in_iota": a["iota"], "in_dist": a["dist"], "q_dram": q_dram, "brow": brow,
             "bands": bands, "bands_sem": stack.enter_context(nc.semaphore("bands")), "bands_n": 0}
        t["pool"] = [stack.enter_context(nc.semaphore(f"phase{n}")) for n in range(Phase.POOL)]
        assert t["pool"][-1].num - t["pool"][0].num == Phase.POOL - 1
        t["x"] = sb("x", [P, NTT, D])
        t["ident"] = sb("ident", [P, P])
        t["ident_r"] = sb("ident_r", [P, P], FR)
        t["iota"] = sb("iota", [P, E])
        t["dist"] = sb("dist", [P, NT])
        with tensors(nc) as (sb0, _):
            t["xt_h"] = sb0("xt_h", [P, KD, NTT * P], FR)
            t["xt_l"] = sb0("xt_l", [P, KD, NTT * P], FR)
            t["expert_w"] = sb0("expert_w", [P, NU, NTT])
            moe_route(nc, t, a["x"].rearrange("b s d -> (b s) d"), a["wt_t"], a["cond_t"], a["wg_t"])
            moe_experts(nc, t, a["w_gate"], a["w_up"], a["w_down"])
        for layer, normed in ((1, True), (2, False), (3, True)):
            w = {n: a[f"L{layer}_{n}"] for n in WEIGHTS[layer]}
            if not normed:
                w = {{"g_in": "g_norm", "Wo": "Wout"}.get(n, n): ap for n, ap in w.items()}
            if normed:
                t["bands_n"] += 16
                relative_bias(nc, t, w)
            with tensors(nc) as (sbl, _):
                for part in "hl":
                    t[f"wq_{part}"] = sbl(f"wq_{part}", [P, KD, H * DH], FR)
                    t[f"wx_{part}"] = sbl(f"wx_{part}", [P, KD, 2 * DH + H], FR)
                    t[f"wo_{part}"] = sbl(f"wo_{part}", [P, NPAIR, D], FR)
                t["kscale"] = sbl("kscale", [P, DH])
                t["null_bias"] = sbl("null_bias", [P, H])
                t["gain_out"] = sbl("gain_out", [P, D])
                t["null_out"] = sbl("null_out", [H, D])
                t["k_hh"] = sbl("k_hh", [P, S], FR)
                t["k_lp"] = sbl("k_lp", [P, S], FR)
                t["v"] = sbl("v", [P, NT, DH])
                t["neg_null"] = sbl("neg_null", [P, NT, H])
                t["null_w"] = sbl("null_w", [P, NT, H])
                t["o_t"] = sbl("o_t", [P, NPAIR, S])
                layer_weights(nc, t, w, a["cond"], normed)
                with nc.Fori(0, B) as b:
                    project(nc, t, b, a["mask_f"] if normed else a["mask_k"], normed)
                    attend(nc, t, None if normed else a["fside"])
                    close_layer(nc, t, b, out if layer == 3 else None)


RELATIVE = ["g_norm", "Wq", "Wkv", "q_scale", "k_scale", "null_attn_bias", "w0", "b0", "g0", "w1", "b1", "g1", "w2", "b2",
            "Wout", "g_out"]
WEIGHTS = {1: RELATIVE, 2: ["g_in", "null_attn_bias", "Wq", "Wkv", "Wo", "g_out"], 3: RELATIVE}


def kernel(**inputs):
    import numpy as _np
    import concourse.bacc as _bacc
    from concourse import mybir as _mybir
    from concourse.bass_utils import run_bass_kernel_spmd as _run

    raw = {n: _np.asarray(v) for n, v in inputs.items()}
    arrays = {
        "x": raw["x"], "cond": raw["cond_64"], "cond_t": raw["cond_64"].T, "fside": raw["fside_16xSxS_0"],
        "mask_f": raw["mask_BxS_bf1"].reshape(B, NT, P).transpose(0, 2, 1),
        "mask_k": raw["mask_BxS_bk0"].reshape(B, NT, P).transpose(0, 2, 1),
        "wt_t": raw["L0_cond_wt"].T, "wg_t": raw["L0_cond_wg"].T,
        "w_gate": _np.concatenate([raw["L0_cond_w_gate"], raw["L0_cond_sw_gate"].reshape(D, 2, M).transpose(1, 0, 2)]),
        "w_up": _np.concatenate([raw["L0_cond_w_up"], raw["L0_cond_sw_up"].reshape(D, 2, M).transpose(1, 0, 2)]),
        "w_down": _np.concatenate([raw["L0_cond_w_down"], raw["L0_cond_sw_down"].reshape(2, M, D)]),
        "ident": _np.eye(P, dtype=_np.float32),
        "iota": _np.tile(_np.arange(E, dtype=_np.float32), (P, 1)),
        "dist": (S - 1 - _np.arange(S, dtype=_np.float32)).reshape(NT, P).T,
    }
    for layer, names in WEIGHTS.items():
        for n in names:
            arrays[f"L{layer}_{n}"] = raw[f"L{layer}_cond_{n}"]
            if n in ("g_norm", "g_in"):
                arrays[f"L{layer}_{n}"] = arrays[f"L{layer}_{n}"].reshape(KD, P).T
    arrays = {f"in_{n}": _np.ascontiguousarray(v) for n, v in arrays.items()}

    nc = _bacc.Bacc("TRN2", target_bir_lowering=False, num_devices=1)
    aps = {n[3:]: nc.dram_tensor(n, v.shape, _mybir.dt.from_np(v.dtype), kind="ExternalInput").ap()
           for n, v in arrays.items()}
    out = nc.dram_tensor("out", (B, S, D), F32, kind="ExternalOutput").ap()
    program(nc, aps, out)
    result = _run(nc, [arrays], core_ids=[0])
    return result.results[0]["out"]
```

```python
from contextlib import ExitStack, contextmanager
from itertools import count

import numpy as np

import concourse.bass as bass
from concourse import mybir

F32 = mybir.dt.float32
FR = mybir.dt.float32r
U8 = mybir.dt.uint8
U32 = mybir.dt.uint32
ALU = mybir.AluOpType
ACT = mybir.ActivationFunctionType
AX = mybir.AxisListType

P = 128
B, S, D = 2, 1024, 256
NT = S // P
NTT = B * NT
KD = D // P
H, DH = 16, 64
NPAIR = H // 2
E, TOPK, M = 8, 2, 128
NU = E + 2
G = 64
BANK = 512
BIG = 1e30
EPS = 1e-5
BROW = S + P


SERIAL = count()


class Phase:

    POOL = 40

    def __init__(self, nc, t, names):
        self.nc, self.pool, self.names = nc, t["pool"], names

    def __enter__(self):
        self.stack = ExitStack()
        self.block = self.stack.enter_context(self.nc.Block())
        assert len(self.names) <= self.POOL
        return self.block, dict(zip(self.names, self.pool))

    def __exit__(self, *exc):
        self.stack.close()
        if exc[0] is None:
            self.nc.all_engine_barrier(sems_to_clear=range(self.pool[0].num, self.pool[len(self.names) - 1].num + 1))


class Own:

    def __init__(self, eng, sem, start=0):
        self.eng, self.sem, self.start, self.n = eng, sem, start, 0

    def step(self, instruction):
        instruction.then_inc(self.sem, 1)
        self.n += 1

    def settle(self):
        self.eng.wait_ge(self.sem, self.start + self.n)


class Turns:

    def __init__(self, sems, turn, marks):
        self.sems, self.turn, self.marks = sems, turn, marks

    def wait(self, eng, name, n):
        eng.wait_ge(self.sems[name], self.turn * self.marks[name] + (self.marks[name] + n))


def start(eng, sems, marks, *names):
    for name in names:
        eng.sem_inc(sems[name], marks[name])


def run(eng, step, turns, size, early, late):
    def steps(turn, at, to, has):
        for n in range(at, to):
            step(turn, n, has)

    def peeled(turn):
        return lambda n, per: 0 <= turn * per + n < turns * per

    steps(-1, size - early, size + late, peeled(-1))
    with eng.Fori(0, turns - 1) as turn:
        steps(turn, late, size + late, lambda n, per: True)
    steps(turns - 1, late, size + late, peeled(turns - 1))


@contextmanager
def tensors(nc):
    serial = next(SERIAL)
    with ExitStack() as stack:
        def sb(name, shape, dt=F32):
            return stack.enter_context(nc.sbuf_tensor(f"{name}_{serial}", shape, dt))

        def ps(name, shape, dt=F32):
            return stack.enter_context(nc.psum_tensor(f"{name}_{serial}", shape, dt))

        yield sb, ps


def rows(vector, n=P):
    return bass.AP(vector.tensor, vector.offset, [[0, n], [1, vector.shape[-1]]])


def f32(ap):
    return ap.bitcast(F32)


def three_products(eng, out, left, right, start, stop):
    pairs = ((0, 0), (0, 1), (1, 0))
    for n, (a, b) in enumerate(pairs):
        last = eng.matmul(out, left[a], right[b], start=start and n == 0, stop=stop and n == len(pairs) - 1)
    return last



def moe_route(nc, t, x, wt_t, cond_t, wg_t):
    names = ["x_in", "w_in", "x_tr", "x_hi", "x_lo", "w_hl", "logits", "dve", "exp_in", "exp_out"]
    with tensors(nc) as (sb, ps):
        wt = sb("route_wt", [P, KD, E])
        wt_h, wt_l = (sb(f"route_wt_{n}", [P, KD, E], FR) for n in "hl")
        cond = sb("route_cond", [G, B])
        cond_b = sb("route_cond_b", [G, B, P])
        wg = sb("route_wg", [G, E])
        logits = sb("route_logits", [P, NTT, E])
        top = sb("route_top", [P, NTT, E])
        top_i = sb("route_top_i", [P, NTT, E], U32)
        top_f = sb("route_top_f", [P, NTT, E])
        shifted = sb("route_shifted", [P, NTT, E])
        score = sb("route_score", [P, NTT, E])
        chosen = sb("route_chosen", [P, NTT, E])
        other = sb("route_other", [P, NTT, E])
        total = sb("route_total", [P, NTT])
        inv = sb("route_inv", [P, NTT])
        tr = [ps(f"route_tr{n}", [P, KD * P]) for n in range(2)]
        lp = ps("route_lp", [P, NTT, E])
        with Phase(nc, t, names) as (block, s):
            @block.sync
            def _(eng):
                eng.dma_start(t["ident"][:], t["in_ident"]).then_inc(s["w_in"], 16)
                eng.dma_start(t["iota"][:], t["in_iota"]).then_inc(s["w_in"], 16)
                eng.dma_start(wt[:], wt_t.rearrange("(k p) e -> p k e", p=P)).then_inc(s["w_in"], 16)
                eng.dma_start(cond[:], cond_t).then_inc(s["w_in"], 16)
                eng.dma_start(wg[:], wg_t).then_inc(s["w_in"], 16)
                for n in range(4):
                    eng.dma_start(t["x"][:, 4 * n:4 * n + 4, :],
                                  x[512 * n:512 * n + 512, :].rearrange("(t p) d -> p t d", p=P)).then_inc(s["x_in"], 16)
                eng.wait_ge(s["w_in"], 80)
                eng.wait_ge(s["x_in"], 64)

            @block.tensor
            def _(eng):
                eng.wait_ge(s["w_in"], 80)
                eng.wait_ge(s["x_in"], 64)
                for n in range(NTT):
                    if n >= 2:
                        eng.wait_ge(s["x_lo"], n - 1)
                    for k in range(KD):
                        last = eng.transpose(tr[n % 2][:, k * P:(k + 1) * P],
                                             t["x"][:, n, k * P:(k + 1) * P], t["ident"][:])
                    last.then_inc(s["x_tr"], 1)
                eng.wait_ge(s["w_hl"], 1)
                eng.wait_ge(s["x_lo"], NTT)
                for n in range(NTT):
                    for k in range(KD):
                        left = [t[c][:, k, n * P:(n + 1) * P] for c in ("xt_h", "xt_l")]
                        three_products(eng, lp[:, n, :], left, [w[:, k, :] for w in (wt_h, wt_l)], k == 0, False)
                    last = eng.matmul(lp[:, n, :], cond_b[:, n // NT, :], wg[:], start=False, stop=True)
                last.then_inc(s["logits"], 1)

            @block.scalar
            def _(eng):
                for n in range(NTT):
                    eng.wait_ge(s["x_tr"], n + 1)
                    eng.activation(t["xt_h"][:, :, n * P:(n + 1) * P],
                                   tr[n % 2][:].rearrange("p (k i) -> p k i", k=KD), ACT.Copy).then_inc(s["x_hi"], 1)
                eng.wait_ge(s["exp_in"], 1)
                eng.activation(score[:], shifted[:], ACT.Exp).then_inc(s["exp_out"], 1)

            @block.vector
            def _(eng):
                own = Own(eng, s["dve"])
                eng.wait_ge(s["w_in"], 80)
                own.step(eng.tensor_copy(t["ident_r"][:], t["ident"][:]))
                own.step(eng.tensor_copy(wt_h[:], wt[:]))
                own.settle()
                own.step(eng.tensor_tensor(wt_l[:], wt[:], f32(wt_h[:]), ALU.subtract))
                eng.tensor_copy(cond_b[:], cond[:].unsqueeze(2).to_broadcast([G, B, P])).then_inc(s["w_hl"], 1)
                for n in range(NTT):
                    eng.wait_ge(s["x_hi"], n + 1)
                    eng.tensor_tensor(t["xt_l"][:, :, n * P:(n + 1) * P],
                                      tr[n % 2][:].rearrange("p (k i) -> p k i", k=KD),
                                      f32(t["xt_h"][:, :, n * P:(n + 1) * P]), ALU.subtract).then_inc(s["x_lo"], 1)
                eng.wait_ge(s["logits"], 1)
                own.step(eng.tensor_scalar(logits[:], lp[:], 0.5, None, ALU.mult))
                own.settle()
                for n in range(NTT):
                    own.step(eng.max(top[:, n, :], logits[:, n, :]))
                own.settle()
                for n in range(NTT):
                    own.step(eng.max_index(top_i[:, n, :], top[:, n, :], logits[:, n, :]))
                eng.tensor_tensor(shifted[:], logits[:], top[:, :, 0:1].to_broadcast([P, NTT, E]),
                                  ALU.subtract).then_inc(s["exp_in"], 1)
                own.settle()
                own.step(eng.tensor_copy(top_f[:], top_i[:]))
                own.settle()
                iota = t["iota"][:].unsqueeze(1).to_broadcast([P, NTT, E])
                own.step(eng.tensor_tensor(chosen[:], iota, top_f[:, :, 0:1].to_broadcast([P, NTT, E]), ALU.is_equal))
                own.step(eng.tensor_tensor(other[:], iota, top_f[:, :, 1:2].to_broadcast([P, NTT, E]), ALU.is_equal))
                own.settle()
                own.step(eng.tensor_tensor(chosen[:], chosen[:], other[:], ALU.add))
                eng.wait_ge(s["exp_out"], 1)

                def normalize(eps):
                    own.step(eng.tensor_reduce(total[:], score[:], AX.X, ALU.add))
                    own.settle()
                    if eps:
                        own.step(eng.tensor_scalar(total[:], total[:], eps, None, ALU.add))
                        own.settle()
                    own.step(eng.reciprocal(inv[:], total[:]))
                    own.settle()

                normalize(0.0)
                own.step(eng.tensor_tensor(score[:], score[:], inv[:].unsqueeze(2).to_broadcast([P, NTT, E]), ALU.mult))
                own.settle()
                own.step(eng.tensor_tensor(score[:], score[:], chosen[:], ALU.mult))
                own.settle()
                normalize(1e-20)
                own.step(eng.memset(t["expert_w"][:], 1.0))
                own.settle()
                own.step(eng.tensor_tensor(t["expert_w"][:, 0:E, :].rearrange("p e n -> p n e"), score[:],
                                           inv[:].unsqueeze(2).to_broadcast([P, NTT, E]), ALU.mult))
                own.settle()


def moe_experts(nc, t, w_gate, w_up, w_down):
    NC = 4
    PAR = 2
    TURN = PAR * NC
    TPC = NTT // NC
    WC = 2 * KD * M + D
    RUN = (NU // PAR, TURN, 2, 2)
    names = ["w_in0", "w_in1", "gate", "w_split", "w_hi", "gu", "slope", "leaky", "hidden", "hid_hi", "hid_lo", "down",
             "added"]
    with tensors(nc) as (sb, ps):
        raw = sb("moe_raw", [P, PAR, WC])
        wh, wl = (sb(f"moe_w{n}", [P, PAR, WC], FR) for n in "hl")
        slope = sb("moe_slope", [P, 2, BANK])
        leaky = sb("moe_leaky", [P, 2, BANK])
        hid = sb("moe_hid", [P, 2, BANK])
        hid_h, hid_l = (sb(f"moe_hid_{n}", [P, 2, BANK], FR) for n in "hl")
        unit_w = sb("moe_unit_w", [P, PAR, NTT])
        gate = [ps(f"moe_gate{n}", [P, BANK]) for n in range(2)]
        up = [ps(f"moe_up{n}", [P, BANK]) for n in range(2)]
        down = [ps(f"moe_down{n}", [P, TPC, D]) for n in range(2)]

        def w_of(tile, q, kind, k):
            at = {"gate": 0, "up": KD * M}.get(kind, 2 * KD * M) + k * M
            return tile[:, q, at:at + (D if kind == "down" else M)]

        marks = dict(w_split=PAR, gu=TURN, slope=TURN, w_hi=2 * PAR, leaky=TURN, hidden=TURN, hid_hi=TURN, hid_lo=TURN,
                     down=TURN, added=TURN)
        with Phase(nc, t, names) as (block, s):
            def load(eng, unit, q):
                one = bass.ds(unit, 1)
                for src, at in ((w_gate, 0), (w_up, KD * M)):
                    eng.dma_start(raw[:, q, at:at + KD * M].rearrange("p (k m) -> p k m", k=KD),
                                  src[one, :, :].rearrange("o (k p) m -> p (o k) m", p=P)).then_inc(s[f"w_in{q}"], 16)
                eng.dma_start(raw[:, q, 2 * KD * M:WC],
                              w_down[one, :, :].rearrange("o p d -> p (o d)")).then_inc(s[f"w_in{q}"], 16)

            @block.sync
            def _(eng):
                with eng.Fori(0, NU // PAR) as it:
                    turn = Turns(s, it, marks)
                    for q in range(PAR):
                        turn.wait(eng, "w_split", q + 1 - PAR)
                        load(eng, it * PAR + q, q)
                for q in range(PAR):
                    eng.wait_ge(s[f"w_in{q}"], 48 * (NU // PAR))

            @block.tensor
            def _(eng):
                def gate_up(turn, c):
                    q, tok = c // NC % PAR, c % NC
                    if c % NC == 0:
                        turn.wait(eng, "w_split", c // NC + 1)
                    turn.wait(eng, "hidden", c - 1)
                    for kind, out in (("gate", gate), ("up", up)):
                        for k in range(KD):
                            last = three_products(
                                eng, out[c % 2][:], [w_of(w, q, kind, k) for w in (wh, wl)],
                                [t[x][:, k, tok * BANK:(tok + 1) * BANK] for x in ("xt_h", "xt_l")],
                                k == 0, k == KD - 1)
                    last.then_inc(s["gu"], 1)

                def down_of(turn, c):
                    q = c // NC % PAR
                    turn.wait(eng, "hid_lo", c + 1)
                    turn.wait(eng, "added", c - 1)
                    for i in range(TPC):
                        last = three_products(
                            eng, down[c % 2][:, i, :], [h[:, c % 2, i * P:(i + 1) * P] for h in (hid_h, hid_l)],
                            [w_of(w, q, "down", 0) for w in (wh, wl)], True, True)
                    last.then_inc(s["down"], 1)

                def step(it, c, has):
                    turn = Turns(s, it, marks)
                    if has(c + 1, TURN):
                        gate_up(turn, c + 1)
                    if has(c - 1, TURN):
                        down_of(turn, c - 1)

                start(eng, s, marks, "gu", "down")
                run(eng, step, *RUN)

            @block.scalar
            def _(eng):
                def step(it, c, has):
                    if not has(c, TURN):
                        return
                    turn = Turns(s, it, marks)
                    turn.wait(eng, "gu", c + 1)
                    turn.wait(eng, "hidden", c - 1)
                    eng.activation(slope[:, c % 2, :], gate[c % 2][:], ACT.Copy, scale=0.01).then_inc(s["slope"], 1)
                    turn.wait(eng, "hidden", c + 1)
                    turn.wait(eng, "down", c - 1)
                    eng.activation(hid_h[:, c % 2, :], hid[:, c % 2, :], ACT.Copy).then_inc(s["hid_hi"], 1)

                start(eng, s, marks, "slope", "hid_hi")
                run(eng, step, *RUN)

            @block.gpsimd
            def _(eng):
                start(eng, s, marks, "hid_lo")
                with eng.Fori(0, NU // PAR) as it:
                    turn = Turns(s, it, marks)
                    for c in range(TURN):
                        turn.wait(eng, "hid_hi", c + 1)
                        eng.tensor_tensor(hid_l[:, c % 2, :], hid[:, c % 2, :], f32(hid_h[:, c % 2, :]),
                                          ALU.subtract).then_inc(s["hid_lo"], 1)

            @block.vector
            def _(eng):
                def split(turn, it, unit):
                    q = unit % PAR
                    eng.wait_ge(s[f"w_in{q}"], it * 48 + 48 * (unit // PAR + 1))
                    turn.wait(eng, "down", (unit - PAR + 1) * NC)
                    turn.wait(eng, "added", (unit - PAR + 1) * NC)
                    eng.sem_inc(s["gate"], 1)
                    eng.tensor_copy(wh[:, q, :], raw[:, q, :]).then_inc(s["w_hi"], 1)
                    eng.tensor_copy(unit_w[:, q, :],
                                    t["expert_w"][:, bass.ds(it * PAR + unit, 1), :].rearrange("p o n -> p (o n)")
                                    ).then_inc(s["w_hi"], 1)
                    turn.wait(eng, "w_hi", 2 * unit + 2)
                    eng.tensor_tensor(wl[:, q, :], raw[:, q, :], f32(wh[:, q, :]), ALU.subtract
                                      ).then_inc(s["w_split"], 1)

                def hidden(turn, c):
                    turn.wait(eng, "slope", c + 1)
                    eng.tensor_tensor(leaky[:, c % 2, :], gate[c % 2][:], slope[:, c % 2, :], ALU.max
                                      ).then_inc(s["leaky"], 1)
                    turn.wait(eng, "leaky", c + 1)
                    turn.wait(eng, "hid_lo", c - 1)
                    eng.tensor_tensor(hid[:, c % 2, :], leaky[:, c % 2, :], up[c % 2][:], ALU.mult
                                      ).then_inc(s["hidden"], 1)

                def add_down(turn, c):
                    q = c // NC % PAR
                    turn.wait(eng, "down", c + 1)
                    turn.wait(eng, "added", c)
                    for i in range(TPC):
                        n = (c % NC) * TPC + i
                        last = eng.scalar_tensor_tensor(t["x"][:, n, :], down[c % 2][:, i, :], unit_w[:, q, n:n + 1],
                                                        t["x"][:, n, :], ALU.mult, ALU.add)
                    last.then_inc(s["added"], 1)

                def step(it, c, has):
                    turn = Turns(s, it, marks)
                    if has(c, TURN):
                        hidden(turn, c)
                    if has(c - 2, TURN):
                        add_down(turn, c - 2)
                    if c % NC == 2 and has(c // NC + 1, PAR):
                        split(turn, it, c // NC + 1)

                start(eng, s, marks, "w_split", "leaky", "w_hi", "hidden", "added")
                run(eng, step, *RUN)
                eng.wait_ge(s["added"], TURN * (NU // PAR + 1))



def relative_bias(nc, t, w):
    names = ["in", "dve", "act_in", "act_out", "tr", "tr_free", "tr_hi", "mm", "pool_in", "pool_out", "out"]
    NS = 2
    with tensors(nc) as (sb, ps):
        vec = {n: sb(f"rb_{n}", [P, D]) for n in ("w0", "b0", "g0", "b1", "g1")}
        w1 = sb("rb_w1", [P, KD, D])
        w1h, w1l = (sb(f"rb_w1{n}", [P, KD, D], FR) for n in "hl")
        w2 = sb("rb_w2", [P, KD, P])
        w2h, w2l = (sb(f"rb_w2{n}", [P, KD, P], FR) for n in "hl")
        b2 = sb("rb_b2", [H, 1])
        h = sb("rb_h", [P, NT, D])
        e = sb("rb_e", [P, NT, D])
        stats = sb("rb_stats", [P, NT, 6])
        mv = sb("rb_mv", [P, NT, 2])
        rstd = sb("rb_rstd", [P, NT])
        hth, htl = (sb(f"rb_ht{n}", [P, KD, S], FR) for n in "hl")
        brow = sb("rb_brow", [H, BROW])
        tr = [ps(f"rb_tr{n}", [P, KD * P]) for n in range(2)]
        mm = ps("rb_mm", [P, NT, D])
        with Phase(nc, t, names) as (block, s):
            @block.sync
            def _(eng):
                eng.dma_start(t["dist"][:], t["in_dist"]).then_inc(s["in"], 16)
                for n in vec:
                    eng.dma_start(vec[n][:], rows(w[n])).then_inc(s["in"], 16)
                eng.dma_start(w1[:], w["w1"].rearrange("(k p) n -> p k n", p=P)).then_inc(s["in"], 16)
                eng.wait_ge(s["dve"], 1)
                eng.dma_start(w2[:, :, 0:H], w["w2"].rearrange("(k p) n -> p k n", p=P)).then_inc(s["in"], 16)
                eng.dma_start(b2[:], w["b2"].rearrange("(n o) -> n o", o=1)).then_inc(s["in"], 16)
                eng.wait_ge(s["in"], 16 * 9)
                eng.wait_ge(s["out"], 1)
                eng.dma_start(t["brow"], brow[:]).then_inc(s["in"], 16)
                eng.wait_ge(s["in"], 16 * 10)
                eng.dma_start(t["bands"], bass.AP(t["brow"].tensor, P - 1, [[BROW, H], [-1, P], [1, S]])
                              ).then_inc(t["bands_sem"], 16)

            @block.vector
            def _(eng):
                own = Own(eng, s["dve"])
                own.step(eng.memset(w2[:], 0.0))
                own.step(eng.memset(brow[:], -BIG))
                eng.wait_ge(s["in"], 16 * 9)
                own.settle()
                for full, hi in ((w1, w1h), (w2, w2h)):
                    own.step(eng.tensor_copy(hi[:], full[:]))
                own.settle()
                for full, hi, lo in ((w1, w1h, w1l), (w2, w2h, w2l)):
                    own.step(eng.tensor_tensor(lo[:], full[:], f32(hi[:]), ALU.subtract))
                for n in range(NT):
                    own.step(eng.scalar_tensor_tensor(h[:, n, :], vec["w0"][:], t["dist"][:, n:n + 1], vec["b0"][:],
                                                      ALU.mult, ALU.add))
                for layer in range(NS):
                    g = vec[f"g{layer}"]
                    if layer:
                        eng.wait_ge(s["mm"], 1)
                        own.step(eng.tensor_tensor(h[:], mm[:], vec["b1"][:].unsqueeze(1).to_broadcast([P, NT, D]),
                                                   ALU.add))
                    own.settle()
                    for n in range(NT):
                        own.step(eng.bn_stats(stats[:, n, :], h[:, n, :]))
                    own.settle()
                    for n in range(NT):
                        own.step(eng.bn_aggr(mv[:, n, :], stats[:, n, :]))
                    own.settle()
                    eng.tensor_scalar(rstd[:], mv[:, :, 1], EPS, None, ALU.add).then_inc(s["act_in"], 1)
                    eng.wait_ge(s["act_out"], 2 * layer + 1)
                    own.step(eng.reciprocal(rstd[:], rstd[:]))
                    own.settle()
                    for n in range(NT):
                        own.step(eng.tensor_scalar(h[:, n, :], h[:, n, :], mv[:, n, 0:1], rstd[:, n:n + 1],
                                                   ALU.subtract, ALU.mult))
                    own.settle()
                    eng.tensor_tensor(h[:], h[:], g[:].unsqueeze(1).to_broadcast([P, NT, D]), ALU.mult
                                      ).then_inc(s["act_in"], 1)
                    eng.wait_ge(s["act_out"], 2 * layer + 2)
                    own.step(eng.tensor_scalar(e[:], e[:], 1.0, None, ALU.add))
                    own.settle()
                    own.step(eng.reciprocal(e[:], e[:]))
                    own.settle()
                    eng.tensor_tensor(h[:], h[:], e[:], ALU.mult).then_inc(s["pool_out"], 1)
                    for n in range(NT):
                        eng.wait_ge(s["tr_hi"], NT * layer + n + 1)
                        eng.tensor_tensor(htl[:, :, n * P:(n + 1) * P], tr[n % 2][:].rearrange("p (k i) -> p k i", k=KD),
                                          f32(hth[:, :, n * P:(n + 1) * P]), ALU.subtract).then_inc(s["tr_free"], 1)
                eng.wait_ge(s["mm"], 2)
                eng.tensor_scalar(brow[:, 0:S], mm[0:H, 0:S // D, :].rearrange("p a b -> p (a b)"), b2[:], None, ALU.add
                                  ).then_inc(s["out"], 1)

            @block.scalar
            def _(eng):
                for layer in range(NS):
                    eng.wait_ge(s["act_in"], 2 * layer + 1)
                    eng.activation(rstd[:], rstd[:], ACT.Sqrt).then_inc(s["act_out"], 1)
                    eng.wait_ge(s["act_in"], 2 * layer + 2)
                    eng.activation(e[:], h[:], ACT.Exp, scale=-1.0).then_inc(s["act_out"], 1)
                    for n in range(NT):
                        if layer and n == 0:
                            eng.wait_ge(s["mm"], 1)
                        eng.wait_ge(s["tr"], NT * layer + n + 1)
                        eng.activation(hth[:, :, n * P:(n + 1) * P], tr[n % 2][:].rearrange("p (k i) -> p k i", k=KD),
                                       ACT.Copy).then_inc(s["tr_hi"], 1)

            @block.tensor
            def _(eng):
                for layer in range(NS):
                    eng.wait_ge(s["pool_out"], layer + 1)
                    for n in range(NT):
                        if NT * layer + n >= 2:
                            eng.wait_ge(s["tr_free"], NT * layer + n - 1)
                        for k in range(KD):
                            last = eng.transpose(tr[n % 2][:, k * P:(k + 1) * P], h[:, n, k * P:(k + 1) * P],
                                                 t["ident"][:])
                        last.then_inc(s["tr"], 1)
                    eng.wait_ge(s["tr_free"], NT * (layer + 1))
                    if layer == 0:
                        for n in range(NT):
                            for k in range(KD):
                                last = three_products(eng, mm[:, n, :], [x[:, k, n * P:(n + 1) * P] for x in (hth, htl)],
                                                      [x[:, k, :] for x in (w1h, w1l)], k == 0, k == KD - 1)
                    else:
                        for c in range(S // BANK):
                            for k in range(KD):
                                last = three_products(
                                    eng, mm[:, 2 * c:2 * c + 2, :].rearrange("p a b -> p (a b)"),
                                    [x[:, k, :] for x in (w2h, w2l)],
                                    [x[:, k, c * BANK:(c + 1) * BANK] for x in (hth, htl)], k == 0, k == KD - 1)
                    last.then_inc(s["mm"], 1)


def layer_weights(nc, t, w, cond, normed):
    names = ["in", "dve", "act", "fold", "null_mm", "pool"]
    with tensors(nc) as (sb, ps):
        wq = sb("lw_wq", [P, KD, H * DH])
        prod = sb("lw_prod", [P, KD, H * DH])
        wx = sb("lw_wx", [P, KD, 2 * DH + H])
        wo = sb("lw_wo", [P, NPAIR, D])
        gain = sb("lw_gain", [P, KD])
        k0 = sb("lw_k0", [P, DH])
        k0n = sb("lw_k0n", [P, DH])
        qs = sb("lw_qs", [P, DH])
        ss = sb("lw_ss", [P, 1])
        v0 = sb("lw_v0", [P, 1])
        v0m = sb("lw_v0m", [P, NPAIR * H])
        vps = ps("lw_vps", [H, D])
        n_in = 16 * (9 + 2 * normed)
        with Phase(nc, t, names) as (block, s):
            @block.sync
            def _(eng):
                def load(dst, src):
                    eng.dma_start(dst, src).then_inc(s["in"], 16)

                load(wq[:], w["Wq"].rearrange("(k p) n -> p k n", p=P))
                load(wx[:, :, 0:2 * DH], w["Wkv"].rearrange("(k p) n -> p k n", p=P))
                load(gain[:], w["g_norm"])
                load(k0[:], rows(cond[0, :]))
                for c in range(2):
                    load(v0[c * DH:(c + 1) * DH, :], cond[1, :].rearrange("(d o) -> d o", o=1))
                if normed:
                    load(t["kscale"][:], rows(w["k_scale"]))
                    load(qs[:], rows(w["q_scale"]))
                load(t["null_bias"][:], rows(w["null_attn_bias"]))
                load(t["gain_out"][:], rows(w["g_out"]))
                load(wo[:], w["Wout"].rearrange("(a p) n -> p a n", p=P))
                eng.wait_ge(s["in"], n_in)

            @block.vector
            def _(eng):
                own = Own(eng, s["dve"])
                own.step(eng.memset(v0m[:], 0.0))
                eng.wait_ge(s["in"], n_in)
                own.settle()
                for c in range(2):
                    last = eng.tensor_copy(v0m[c * DH:(c + 1) * DH, c:c + (H + 2) * (NPAIR - 1) + 1:H + 2],
                                           v0[c * DH:(c + 1) * DH, :].to_broadcast([DH, NPAIR]))
                last.then_inc(s["fold"], 1)
                for k in range(KD):
                    own.step(eng.tensor_scalar(wq[:, k, :], wq[:, k, :], gain[:, k:k + 1], None, ALU.mult))
                    own.step(eng.tensor_scalar(wx[:, k, 0:2 * DH], wx[:, k, 0:2 * DH], gain[:, k:k + 1], None, ALU.mult))
                if normed:
                    own.step(eng.scalar_tensor_tensor(t["kscale"][:], t["kscale"][:], 8.0, qs[:], ALU.mult, ALU.mult))
                    own.step(eng.tensor_tensor(k0n[:], k0[:], k0[:], ALU.mult))
                    own.settle()
                    own.step(eng.tensor_reduce(ss[:], k0n[:], AX.X, ALU.add))
                    own.settle()
                    eng.sem_inc(s["pool"], 1)
                    eng.wait_ge(s["act"], 1)
                    own.step(eng.tensor_scalar(ss[:], ss[:], 1e-12, None, ALU.max))
                    own.settle()
                    own.step(eng.reciprocal(ss[:], ss[:]))
                    own.settle()
                    own.step(eng.scalar_tensor_tensor(k0n[:], k0[:], ss[:, 0:1], t["kscale"][:], ALU.mult, ALU.mult))
                else:
                    own.step(eng.tensor_scalar(k0n[:], k0[:], DH ** -0.5, None, ALU.mult))
                own.settle()
                for k in range(KD):
                    own.step(eng.tensor_tensor(prod[:, k, :].rearrange("p (h d) -> p h d", h=H),
                                               wq[:, k, :].rearrange("p (h d) -> p h d", h=H),
                                               k0n[:].unsqueeze(1).to_broadcast([P, H, DH]), ALU.mult))
                own.settle()
                for k in range(KD):
                    own.step(eng.tensor_reduce(wx[:, k, 2 * DH:], prod[:, k, :].rearrange("p (h d) -> p h d", h=H),
                                               AX.X, ALU.add))
                own.settle()
                for full, hi in ((wq, "wq_h"), (wx, "wx_h"), (wo, "wo_h")):
                    own.step(eng.tensor_copy(t[hi][:], full[:]))
                own.settle()
                for full, hi, lo in ((wq, "wq_h", "wq_l"), (wx, "wx_h", "wx_l"), (wo, "wo_h", "wo_l")):
                    own.step(eng.tensor_tensor(t[lo][:], full[:], f32(t[hi][:]), ALU.subtract))
                eng.wait_ge(s["null_mm"], 1)
                own.step(eng.tensor_copy(t["null_out"][:], vps[:]))
                own.settle()

            @block.scalar
            def _(eng):
                if normed:
                    eng.wait_ge(s["pool"], 1)
                    eng.activation(ss[:], ss[:], ACT.Sqrt).then_inc(s["act"], 1)

            @block.tensor
            def _(eng):
                eng.wait_ge(s["in"], n_in)
                eng.wait_ge(s["fold"], 1)
                for a in range(NPAIR):
                    last = eng.matmul(vps[:], v0m[:, a * H:(a + 1) * H], wo[:, a, :], start=a == 0, stop=a == NPAIR - 1)
                last.then_inc(s["null_mm"], 1)


def project(nc, t, b, mask, normed):
    names = ["mask_in", "dve", "var", "std", "xn", "xtr", "xt_hi", "xt_lo", "q", "kv", "q_copy", "kv_copy", "sumsq",
             "norm", "q_ready", "q_hi", "q_lo", "k_ready", "tr", "out", "store0", "store1"]
    NG = 4
    GR = 1 + H // NG
    BY_DVE, BY_ACT = (0, 3), (1, 2, 4)
    LAG = 2
    AHEAD = 2
    NQ = 3
    with tensors(nc) as (sb, ps):
        mask8 = sb("pj_mask8", [P, NT], U8)
        pen = sb("pj_pen", [P, NT])
        xb = sb("pj_xb", [P, NT, D])
        stats = sb("pj_stats", [P, NT, 6])
        mv = sb("pj_mv", [P, NT, 2])
        rstd = sb("pj_rstd", [P, NT])
        xth, xtl = (sb(f"pj_xt{n}", [P, KD, S], FR) for n in "hl")
        qs = sb("pj_qs", [P, NQ, H * DH])
        sq = sb("pj_sq", [P, 2, H * DH])
        kvs = sb("pj_kvs", [P, 2, 2 * DH + H])
        ksq = sb("pj_ksq", [P, DH])
        ss = sb("pj_ss", [P, 2, H + 1])
        kn = sb("pj_kn", [P, DH])
        nul = sb("pj_nul", [P, H])
        qhl = sb("pj_qhl", [P, 2, H, 2 * DH], FR)
        khl = sb("pj_khl", [P, 2, 2 * P], FR)
        qt = sb("pj_qt", [P, 2, H, P], FR)
        xtr = ps("pj_xtr", [P, BANK])[:, 0:KD * P]
        qps = [ps(f"pj_q{n}", [P, H * DH]) for n in range(2)]
        kvp = ps("pj_kv", [P, BANK])
        trs = [ps(f"pj_tr{n}", [P, NG * P]) for n in range(2)]
        with Phase(nc, t, names) as (block, s):
            @block.sync
            def _(eng):
                eng.dma_start(mask8[:], mask[bass.ds(b, 1), :, :].rearrange("o p t -> p (o t)")
                              ).then_inc(s["mask_in"], 16)
                for n in range(NT):
                    eng.wait_ge(s["out"], GR * (n + 1))
                    eng.dma_start(t["q_dram"][:, :, n * P:(n + 1) * P].rearrange("h p i -> p h i"), f32(qt[:, n % 2, :, :])
                                  ).then_inc(s[f"store{n % 2}"], 16)
                eng.wait_ge(s["mask_in"], 16)
                eng.wait_ge(s["store0"], 16 * NT // 2)
                eng.wait_ge(s["store1"], 16 * NT // 2)

            @block.tensor
            def _(eng):
                def x_transpose(n):
                    eng.wait_ge(s["xn"], n + 1)
                    if n:
                        eng.wait_ge(s["xt_lo"], n)
                    for k in range(KD):
                        last = eng.transpose(xtr[:, k * P:(k + 1) * P], xb[:, n, k * P:(k + 1) * P], t["ident"][:])
                    last.then_inc(s["xtr"], 1)

                def left(n, k):
                    return [x[:, k, n * P:(n + 1) * P] for x in (xth, xtl)]

                def queries(n, c):
                    if c == 0:
                        eng.wait_ge(s["xt_lo"], n + 1)
                        if n >= 2:
                            eng.wait_ge(s["q_copy"], n - 1)
                    for k in range(KD):
                        last = three_products(eng, qps[n % 2][:, c * BANK:(c + 1) * BANK], left(n, k),
                                              [t[x][:, k, c * BANK:(c + 1) * BANK] for x in ("wq_h", "wq_l")],
                                              k == 0, k == KD - 1)
                    if c == H * DH // BANK - 1:
                        last.then_inc(s["q"], 1)

                def keys_values(n):
                    if n:
                        eng.wait_ge(s["kv_copy"], n)
                    for k in range(KD):
                        last = three_products(eng, kvp[:, 0:2 * DH + H], left(n, k), [t[x][:, k, :] for x in ("wx_h", "wx_l")],
                                              k == 0, k == KD - 1)
                    last.then_inc(s["kv"], 1)

                def head_transposes(n, *groups):
                    for g in groups:
                        m = n * GR + g
                        if g == 0:
                            eng.wait_ge(s["k_ready"], n + 1)
                            blocks = [khl[:, n % 2, c * P:(c + 1) * P] for c in range(2)]
                        else:
                            eng.wait_ge(s["q_lo"], n + 1)
                            blocks = [qhl[:, n % 2, (g - 1) * NG + c, :] for c in range(NG)]
                        if m >= 2:
                            eng.wait_ge(s["out"], m - 1)
                        for c, block in enumerate(blocks):
                            last = eng.transpose(trs[m % 2][:, c * P:(c + 1) * P].bitcast(FR), block, t["ident_r"][:])
                        last.then_inc(s["tr"], 1)

                for n in range(AHEAD):
                    x_transpose(n)
                for n in range(NT + LAG):
                    if n + AHEAD < NT:
                        x_transpose(n + AHEAD)
                    if n < NT:
                        queries(n, 0)
                    if n >= LAG:
                        head_transposes(n - LAG, 0, 1)
                    if n < NT:
                        queries(n, 1)
                    if n >= LAG:
                        head_transposes(n - LAG, 2, 3)
                    if n < NT:
                        keys_values(n)
                    if n >= LAG:
                        head_transposes(n - LAG, 4)

            def heads(n):
                return qs[:, n % NQ, :].rearrange("p (h d) -> p h d", h=H)

            def evacuate(eng, n, g, copy):
                m = n * GR + g
                eng.wait_ge(s["tr"], m + 1)
                if m:
                    eng.wait_ge(s["out"], m)
                if g == 0:
                    copy(t["k_hh"][:, n * P:(n + 1) * P], trs[m % 2][:, 0:P])
                    copy(t["k_lp"][:, n * P:(n + 1) * P], trs[m % 2][:, P:2 * P]).then_inc(s["out"], 1)
                else:
                    if n >= 2:
                        eng.wait_ge(s[f"store{n % 2}"], 16 * (n // 2))
                    copy(qt[:, n % 2, (g - 1) * NG:g * NG, :].rearrange("p h i -> p (h i)"), trs[m % 2][:]
                         ).then_inc(s["out"], 1)

            @block.vector
            def _(eng):
                own = Own(eng, s["dve"])
                for tile in (0, 1):
                    own.step(eng.memset(f32(khl[:, tile, P:2 * P]), 0.0))
                own.step(eng.tensor_copy(xb[:], t["x"][:, bass.ds(b * NT, NT), :]))
                eng.wait_ge(s["mask_in"], 16)
                own.step(eng.tensor_copy(pen[:], mask8[:]))
                own.settle()
                own.step(eng.tensor_scalar(pen[:], pen[:], BIG, -BIG, ALU.mult, ALU.add))
                for n in range(NT):
                    own.step(eng.bn_stats(stats[:, n, :], xb[:, n, :]))
                own.settle()
                for n in range(NT):
                    own.step(eng.bn_aggr(mv[:, n, :], stats[:, n, :]))
                own.settle()
                eng.tensor_scalar(rstd[:], mv[:, :, 1], EPS, None, ALU.add).then_inc(s["var"], 1)
                eng.wait_ge(s["std"], 1)
                own.step(eng.reciprocal(rstd[:], rstd[:]))
                own.settle()
                for n in range(NT):
                    eng.tensor_scalar(xb[:, n, :], xb[:, n, :], mv[:, n, 0:1], rstd[:, n:n + 1],
                                      ALU.subtract, ALU.mult).then_inc(s["xn"], 1)

                def x_low(n):
                    eng.wait_ge(s["xt_hi"], n + 1)
                    eng.tensor_tensor(xtl[:, :, n * P:(n + 1) * P], xtr.rearrange("p (k i) -> p k i", k=KD),
                                      f32(xth[:, :, n * P:(n + 1) * P]), ALU.subtract).then_inc(s["xt_lo"], 1)

                def sum_squares(n):
                    eng.wait_ge(s["kv_copy"], n + 1)
                    eng.wait_ge(s["q_copy"], n + 1)
                    if n:
                        eng.wait_ge(s["sumsq"], n)
                    own.step(eng.tensor_tensor(ksq[:], kvs[:, n % 2, 0:DH], kvs[:, n % 2, 0:DH], ALU.mult))
                    own.step(eng.tensor_reduce(ss[:, n % 2, 0:H], sq[:, n % 2, :].rearrange("p (h d) -> p h d", h=H),
                                               AX.X, ALU.add))
                    own.settle()
                    eng.tensor_reduce(ss[:, n % 2, H:H + 1], ksq[:], AX.X, ALU.add).then_inc(s["sumsq"], 1)

                def keys(n):
                    c = n % 2
                    if n:
                        eng.wait_ge(s["k_ready"], n)
                    if normed:
                        eng.wait_ge(s["norm"], n + 1)
                        own.step(eng.tensor_scalar(ss[:, c, :], ss[:, c, :], 1e-12, None, ALU.max))
                        own.settle()
                        own.step(eng.reciprocal(ss[:, c, :], ss[:, c, :]))
                        own.settle()
                        eng.tensor_tensor(heads(n), heads(n), ss[:, c, 0:H].unsqueeze(2).to_broadcast([P, H, DH]), ALU.mult
                                          ).then_inc(s["q_ready"], 1)
                        own.step(eng.scalar_tensor_tensor(kn[:], kvs[:, c, 0:DH], ss[:, c, H:H + 1], t["kscale"][:],
                                                          ALU.mult, ALU.mult))
                        own.step(eng.tensor_tensor(nul[:], kvs[:, c, 2 * DH:], ss[:, c, 0:H], ALU.mult))
                    else:
                        eng.wait_ge(s["kv_copy"], n + 1)
                        own.step(eng.tensor_scalar(kn[:], kvs[:, c, 0:DH], DH ** -0.5, None, ALU.mult))
                        own.step(eng.tensor_copy(nul[:], kvs[:, c, 2 * DH:]))
                    if n >= 2:
                        eng.wait_ge(s["tr"], GR * (n - 2) + 1)
                    own.settle()
                    own.step(eng.tensor_copy(khl[:, c, 0:DH], kn[:]))
                    own.step(eng.tensor_copy(khl[:, c, DH:2 * DH], kn[:]))
                    own.step(eng.tensor_copy(khl[:, c, 3 * DH:3 * DH + 1], pen[:, n:n + 1]))
                    own.step(eng.scalar_tensor_tensor(t["neg_null"][:, n, :], nul[:], -1.0, t["null_bias"][:],
                                                      ALU.mult, ALU.subtract))
                    own.settle()
                    eng.tensor_tensor(khl[:, c, 2 * DH:3 * DH], kn[:], f32(khl[:, c, 0:DH]), ALU.subtract
                                      ).then_inc(s["k_ready"], 1)

                def q_low(n):
                    eng.wait_ge(s["q_hi"], n + 1)
                    eng.tensor_tensor(qhl[:, n % 2, :, DH:], heads(n), f32(qhl[:, n % 2, :, 0:DH]), ALU.subtract
                                      ).then_inc(s["q_lo"], 1)

                for n in range(AHEAD):
                    x_low(n)
                for n in range(NT + LAG):
                    if n >= LAG:
                        q_low(n - LAG)
                    if normed and 1 <= n <= NT:
                        sum_squares(n - 1)
                    if n + AHEAD < NT:
                        x_low(n + AHEAD)
                    if n >= LAG:
                        for g in BY_DVE:
                            evacuate(eng, n - LAG, g, eng.tensor_copy)
                    if 1 <= n <= NT:
                        keys(n - 1)

            @block.scalar
            def _(eng):
                def copy(out, in_):
                    return eng.activation(out, in_, ACT.Copy)

                eng.wait_ge(s["var"], 1)
                eng.activation(rstd[:], rstd[:], ACT.Sqrt).then_inc(s["std"], 1)

                def x_high(n):
                    eng.wait_ge(s["xtr"], n + 1)
                    eng.activation(xth[:, :, n * P:(n + 1) * P], xtr.rearrange("p (k i) -> p k i", k=KD), ACT.Copy
                                   ).then_inc(s["xt_hi"], 1)

                def copies(n):
                    c = n % 2
                    eng.wait_ge(s["q"], n + 1)
                    if n >= NQ:
                        eng.wait_ge(s["q_lo"], n - NQ + 1)
                    q_copied = eng.activation(qs[:, n % NQ, :], qps[c][:], ACT.Copy)
                    if normed:
                        if n >= 2:
                            eng.wait_ge(s["sumsq"], n - 1)
                        q_copied = eng.activation(sq[:, c, :], qps[c][:], ACT.Square)
                    q_copied.then_inc(s["q_copy"], 1)
                    eng.wait_ge(s["kv"], n + 1)
                    if n >= 2:
                        eng.wait_ge(s["k_ready"], n - 1)
                    eng.activation(t["v"][:, n, :], kvp[:, DH:2 * DH], ACT.Copy)
                    eng.activation(kvs[:, c, :], kvp[:, 0:2 * DH + H], ACT.Copy).then_inc(s["kv_copy"], 1)

                def norms(n):
                    eng.wait_ge(s["sumsq"], n + 1)
                    eng.activation(ss[:, n % 2, :], ss[:, n % 2, :], ACT.Sqrt).then_inc(s["norm"], 1)

                def q_high(n):
                    if normed:
                        eng.wait_ge(s["q_ready"], n + 1)
                    if n >= 2:
                        eng.wait_ge(s["tr"], GR * (n - 1))
                    eng.activation(qhl[:, n % 2, :, 0:DH], heads(n), ACT.Copy).then_inc(s["q_hi"], 1)

                for n in range(AHEAD):
                    x_high(n)
                for n in range(NT + LAG):
                    if n >= LAG:
                        q_high(n - LAG)
                    if normed and 1 <= n <= NT:
                        norms(n - 1)
                    if n + AHEAD < NT:
                        x_high(n + AHEAD)
                    if n >= LAG:
                        for g in BY_ACT[:-1]:
                            evacuate(eng, n - LAG, g, copy)
                    if n < NT:
                        copies(n)
                    if n >= LAG:
                        evacuate(eng, n - LAG, BY_ACT[-1], copy)


def attend(nc, t, bias):
    HP = 2
    U = HP * NT * 2
    GU = 8
    NGRP = U // GU
    TURNS = NPAIR // HP
    NBIAS = 4
    VSTEPS = 4
    SKEW = VSTEPS + 1
    toeplitz = bias is None
    n_bias = HP * 2 if toeplitz else U

    pieces, starts = [], []
    for u in range(U):
        n = (u // 2) % NT + 1
        starts.append(len(pieces))
        pieces += [(at, min(4, n - at)) for at in range(0, n, 4)]
    NPC = len(pieces)
    assert NPC % 2 == 0 and U % NBIAS == 0 and NGRP % 2 == 0

    def first(u):
        return u // U * NPC + starts[u % U]

    marks = dict(qk=U, biased=U, exp=U, tr=NPC, ev_a=NPC // 2, ev_d=NPC // 2, pv=NGRP, null_d=NGRP, null_e=NGRP,
                 inv_b=NGRP, bc=NGRP, bc_s=NGRP, out=NGRP, diag=U, nulls=HP, sums=3 * NGRP)
    names = list(marks) + ["q0", "q1", "ones", "gate"] + [f"bias{n}" for n in range(NBIAS)]

    NARROW = BANK - P

    def weights_at(g, j):
        full = 4 * (g % 2)
        return min(j, full) * BANK + max(0, j - full) * NARROW

    def unit(u):
        tile = (u // 2) % NT
        return u % U // (2 * NT), tile, u % 2, (tile + 1) * P

    with tensors(nc) as (sb, ps):
        q_hl = sb("at_q_hl", [P, HP, 2, S], FR)
        q_h1 = sb("at_q_h1", [P, HP, 2, S], FR)
        bt = sb("at_bias", [P, NBIAS, S])
        neg = sb("at_neg", [P, 2, S])
        prob = sb("at_prob", [P, 2, S])
        pt = [sb(f"at_pt{n}", [P, 2, 4 * n * BANK + 3 * NARROW + BANK]) for n in range(2)]
        nmax, rsum, nd, p0, inv = (sb(f"at_{n}", [P, 2, GU]) for n in ("nmax", "rsum", "nd", "p0", "inv"))
        inv_b = sb("at_inv_b", [P, GU, DH])
        bc_s = sb("at_bc_s", [P, BANK])
        nn = sb("at_nn", [P, NT, 2 * HP])
        s_ps = [ps(f"at_s{n}", [P, S]) for n in range(2)]
        t_ps = [ps(f"at_t{n}", [P, BANK]) for n in range(2)]
        o_ps = ps("at_o", [P, BANK])
        b_ps = ps("at_b", [P, BANK])

        def evacuate(eng, turn, u, n, copy, parity, name):
            m = first(u) + n
            if m >= first(u + 1) or m % 2 != parity:
                return
            turn.wait(eng, "tr", m + 1)
            turn.wait(eng, "pv", u // GU - 1)
            at, blocks = pieces[m % NPC]
            col = ((u // 2) % 4) * P
            g = u // GU % 2
            here = weights_at(g, at) + col
            one = pt[g][:, u % 2, here:here + P]
            pitch = BANK if at < 4 * g else NARROW
            copy(bass.AP(one.tensor, one.offset, [one.ap[0], [pitch, blocks], [1, P]]),
                 t_ps[parity][:, 0:blocks * P].rearrange("p (c i) -> p c i", i=P)).then_inc(s[name], 1)

        with Phase(nc, t, names) as (block, s):
            @block.sync
            def _(eng):
                if toeplitz:
                    eng.wait_ge(t["bands_sem"], t["bands_n"])
                with eng.Fori(0, TURNS) as it:
                    turn = Turns(s, it, marks)

                    def queries(p):
                        turn.wait(eng, "qk", (p + 1) * 2 * NT - U)
                        two = bass.ds(it * 2 * HP + 2 * p, 2)
                        eng.dma_start(f32(q_hl[:, p, :, :]), t["q_dram"][two, :, :].rearrange("h p i -> p h i")
                                      ).then_inc(s[f"q{p}"], 16)
                        eng.dma_start(f32(q_h1[0:DH, p, :, :]), t["q_dram"][two, 0:DH, :].rearrange("h p i -> p h i")
                                      ).then_inc(s[f"q{p}"], 16)

                    for n in range(n_bias):
                        if n % (n_bias // HP) == 0:
                            queries(n // (n_bias // HP))
                        slot = n % NBIAS
                        if toeplitz:
                            turn.wait(eng, "biased", (n // 2) * 2 * NT + 2 * (NT - 1) + n % 2 + 1 - U)
                            head = bass.ds(it * 2 * HP + n, 1)
                            eng.dma_start(bt[:, slot, :], t["bands"][head, :, :].rearrange("o p c -> p (o c)")
                                          ).then_inc(s[f"bias{slot}"], 16)
                        else:
                            p, tile, side, width = unit(n)
                            turn.wait(eng, "biased", n + 1 - NBIAS)
                            head = bass.ds(it * 2 * HP + 2 * p + side, 1)
                            eng.dma_start(bt[:, slot, 0:width],
                                          bias[head, tile * P:(tile + 1) * P, 0:width].rearrange("o p c -> p (o c)")
                                          ).then_inc(s[f"bias{slot}"], 16)
                for p in range(HP):
                    eng.wait_ge(s[f"q{p}"], 32 * TURNS)
                for n in range(NBIAS):
                    eng.wait_ge(s[f"bias{n}"], 16 * TURNS * n_bias // NBIAS)

            @block.tensor
            def _(eng):
                def logits(it, u):
                    turn = Turns(s, it, marks)
                    p, tile, side, width = unit(u)
                    if u % (2 * NT) == 0:
                        eng.wait_ge(s[f"q{p}"], it * 32 + 32 * (u // U + 1))
                    turn.wait(eng, "biased", u - 1)
                    at = slice(tile * P, (tile + 1) * P)
                    for c in range(0, width, BANK):
                        n = min(BANK, width - c)
                        out = s_ps[u % 2][:, c:c + n]
                        eng.matmul(out, q_hl[:, p, side, at], t["k_hh"][:, c:c + n], start=True, stop=False)
                        last = eng.matmul(out, q_h1[0:DH + 1, p, side, at], t["k_lp"][0:DH + 1, c:c + n],
                                          start=False, stop=True)
                    last.then_inc(s["qk"], 1)

                def transposes(turn, u, n):
                    m = first(u) + n
                    if m >= first(u + 1):
                        return
                    turn.wait(eng, "exp", u + 1)
                    turn.wait(eng, ("ev_a", "ev_d")[m % 2], m // 2)
                    at, blocks = pieces[m % NPC]
                    for c in range(blocks):
                        last = eng.transpose(t_ps[m % 2][:, c * P:(c + 1) * P],
                                             prob[:, u % 2, (at + c) * P:(at + c + 1) * P], t["ident"][:])
                    last.then_inc(s["tr"], 1)

                def values(turn, g, part):
                    m = first(GU * (g + 1))
                    turn.wait(eng, "ev_a", m // 2)
                    turn.wait(eng, "ev_d", m // 2)
                    turn.wait(eng, "out", g)
                    blocks = 4 * (g % 2) + 4
                    share = blocks // VSTEPS
                    for j in range(part * share, (part + 1) * share):
                        i0 = max(0, j - (blocks - 4)) * P
                        at = weights_at(g, j)
                        for side in range(2):
                            last = eng.matmul(o_ps[side * DH:(side + 1) * DH, i0:BANK], t["v"][:, j, :],
                                              pt[g % 2][:, side, at + i0:at + BANK], start=j == 0, stop=j == blocks - 1)
                    if part == VSTEPS - 1:
                        last.then_inc(s["pv"], 1)

                def broadcast(turn, g):
                    turn.wait(eng, "inv_b", g + 1)
                    turn.wait(eng, "bc_s", g)
                    for c in range(4):
                        last = eng.transpose(b_ps[:, c * P:(c + 1) * P],
                                             inv_b[:, 2 * c:2 * c + 2, :].rearrange("p s d -> p (s d)"), t["ident"][:])
                    last.then_inc(s["bc"], 1)

                def step(it, u, has):
                    turn = Turns(s, it, marks)
                    if has(u + 2, U):
                        logits(it, u + 2)
                    if has(u, U):
                        transposes(turn, u, 0)
                        transposes(turn, u, 1)
                    g = u // GU - 1
                    if u % GU < VSTEPS and has(g, NGRP):
                        values(turn, g, u % GU)
                    if u % GU == 2 and has(g, NGRP):
                        broadcast(turn, g)

                start(eng, s, marks, "qk", "tr", "pv", "bc")
                eng.wait_ge(s["ones"], 1)
                run(eng, step, TURNS, U, 2, SKEW)

            @block.vector
            def _(eng):
                start(eng, s, marks, "biased", "ev_d", "null_d", "nulls", "sums", "inv_b", "out")
                for p in range(HP):
                    for side in range(2):
                        last = eng.memset(f32(q_h1[DH:DH + 1, p, side, :]), 1.0)
                last.then_inc(s["ones"], 1)

                def null_logits(turn, it, pair):
                    p = pair % HP
                    turn.wait(eng, "null_d", 2 * (pair - HP) + 2)
                    eng.sem_inc(s["gate"], 1)
                    eng.tensor_copy(nn[:, :, 2 * p:2 * p + 2], t["neg_null"][:, :, bass.ds(it * 2 * HP + 2 * pair, 2)]
                                    ).then_inc(s["nulls"], 1)
                    turn.wait(eng, "nulls", pair + 1)

                def add_bias(turn, it, u):
                    p, tile, side, width = unit(u)
                    turn.wait(eng, "qk", u + 1)
                    turn.wait(eng, "exp", u - 1)
                    slot, lo = (2 * p + side, S - width) if toeplitz else (u % NBIAS, 0)
                    if not toeplitz:
                        turn.wait(eng, "diag", u + 1)
                    elif tile == 0:
                        eng.wait_ge(s[f"bias{slot}"], it * 16 + 16 * (u // U + 1))
                    eng.sem_inc(s["gate"], 1)
                    eng.tensor_tensor_reduce(
                        out=neg[:, u % 2, 0:width], in0=s_ps[u % 2][:, 0:width], in1=bt[:, slot, lo:lo + width],
                        scale=-1.0, scalar=nn[:, tile, 2 * p + side:2 * p + side + 1], op0=ALU.add, op1=ALU.min,
                        accum_out=nmax[:, (u // GU) % 2, u % GU:u % GU + 1]).then_inc(s["biased"], 1)

                def per_tile(x, g):
                    return x[:, g % 2, :].rearrange("p (t s) -> p t s", s=2)

                def tiles(g):
                    return slice(4 * (g % 2), 4 * (g % 2) + 4)

                def null_shift(turn, g):
                    p = g // 2 % HP
                    turn.wait(eng, "exp", GU * (g + 1))
                    turn.wait(eng, "null_e", g - 1)
                    eng.tensor_tensor(per_tile(nd, g), per_tile(nmax, g), nn[:, tiles(g), 2 * p:2 * p + 2], ALU.subtract
                                      ).then_inc(s["null_d"], 1)

                def sums(turn, it, g):
                    turn.wait(eng, "null_e", g + 1)
                    turn.wait(eng, "inv_b", g - 1)
                    c = g % 2
                    eng.tensor_tensor(inv[:, c, :], p0[:, c, :], rsum[:, c, :], ALU.add).then_inc(s["sums"], 1)
                    turn.wait(eng, "sums", 3 * g + 1)
                    eng.reciprocal(inv[:, c, :], inv[:, c, :]).then_inc(s["sums"], 1)
                    turn.wait(eng, "sums", 3 * g + 2)
                    eng.tensor_tensor(t["null_w"][:, tiles(g), bass.ds(it * 2 * HP + 2 * (g // 2), 2)],
                                      per_tile(p0, g), per_tile(inv, g), ALU.mult).then_inc(s["sums"], 1)
                    turn.wait(eng, "bc", g)
                    eng.tensor_copy(inv_b[:], inv[:, c, :].unsqueeze(2).to_broadcast([P, GU, DH])
                                    ).then_inc(s["inv_b"], 1)

                def output(turn, it, g):
                    turn.wait(eng, "bc_s", g + 1)
                    turn.wait(eng, "pv", g + 1)
                    at = (g % 2) * BANK
                    eng.tensor_tensor(t["o_t"][:, bass.ds(it * HP + g // 2, 1), at:at + BANK
                                               ].rearrange("p o i -> p (o i)"),
                                      o_ps[:], bc_s[:], ALU.mult).then_inc(s["out"], 1)

                def step(it, u, has):
                    turn = Turns(s, it, marks)
                    if has(u + 2, U):
                        if (u + 2) % (2 * NT) == 0:
                            null_logits(turn, it, (u + 2) // (2 * NT))
                        add_bias(turn, it, u + 2)
                    if has(u, U):
                        evacuate(eng, turn, u, 0, eng.tensor_copy, 1, "ev_d")
                        evacuate(eng, turn, u, 1, eng.tensor_copy, 1, "ev_d")
                        if u % GU == GU - 1:
                            null_shift(turn, u // GU)
                    g = u // GU - 1
                    if u % GU == 0 and has(g, NGRP):
                        sums(turn, it, g)
                    if u % GU == VSTEPS and has(g, NGRP):
                        output(turn, it, g)

                run(eng, step, TURNS, U, 2, SKEW)
                eng.wait_ge(s["out"], NGRP * (TURNS + 1))

            @block.scalar
            def _(eng):
                def copy(out, in_):
                    return eng.activation(out, in_, ACT.Copy)

                def exponent(turn, u):
                    width = unit(u)[3]
                    c, i = (u // GU) % 2, u % GU
                    turn.wait(eng, "biased", u + 1)
                    turn.wait(eng, "tr", first(u - 1))
                    turn.wait(eng, "inv_b", u // GU - 1)
                    eng.activation(prob[:, u % 2, 0:width], neg[:, u % 2, 0:width], ACT.Exp, scale=-1.0,
                                   bias=nmax[:, c, i:i + 1], accum_out=rsum[:, c, i:i + 1]).then_inc(s["exp"], 1)

                def null_exponent(turn, g):
                    turn.wait(eng, "null_d", g + 1)
                    turn.wait(eng, "inv_b", g - 1)
                    eng.activation(p0[:, g % 2, :], nd[:, g % 2, :], ACT.Exp).then_inc(s["null_e"], 1)

                def copy_broadcast(turn, g):
                    turn.wait(eng, "bc", g + 1)
                    turn.wait(eng, "out", g)
                    copy(bc_s[:], b_ps[:]).then_inc(s["bc_s"], 1)

                def step(it, u, has):
                    turn = Turns(s, it, marks)
                    if has(u + 1, U):
                        exponent(turn, u + 1)
                    g = u // GU - 1
                    if u % GU == VSTEPS and has(g, NGRP):
                        copy_broadcast(turn, g)
                    if has(u, U):
                        evacuate(eng, turn, u, 0, copy, 0, "ev_a")
                        evacuate(eng, turn, u, 1, copy, 0, "ev_a")
                        if u % GU == GU - 1:
                            null_exponent(turn, u // GU)

                start(eng, s, marks, "exp", "ev_a", "null_e", "bc_s")
                run(eng, step, TURNS, U, 2, SKEW)

            if not toeplitz:
                @block.gpsimd
                def _(eng):
                    start(eng, s, marks, "diag")
                    with eng.Fori(0, TURNS) as it:
                        for u in range(U):
                            tile, width = unit(u)[1], unit(u)[3]
                            slot = u % NBIAS
                            eng.wait_ge(s[f"bias{slot}"], it * (16 * U // NBIAS) + 16 * (u // NBIAS + 1))
                            eng.sem_inc(s["gate"], 1)
                            corner = bt[:, slot, tile * P:width]
                            eng.affine_select(out=corner, in_=corner, compare_op=ALU.is_ge, fill=-BIG, base=0,
                                              pattern=[[-1, P]], channel_multiplier=1).then_inc(s["diag"], 1)


def close_layer(nc, t, b, out):
    names = ["o_hi", "o_lo", "n_tr", "n_copy", "y", "y_copy", "var", "std", "dve", "scaled", "added", "stored"]
    with tensors(nc) as (sb, ps):
        oh, ol = (sb(f"cl_o{n}", [P, 2, NPAIR, P], FR) for n in "hl")
        nwt = sb("cl_nwt", [H, 2, P])
        y = sb("cl_y", [P, NT, D])
        stats = sb("cl_stats", [P, NT, 6])
        mv = sb("cl_mv", [P, NT, 2])
        rstd = sb("cl_rstd", [P, NT])
        yps = [ps(f"cl_y{n}", [P, BANK]) for n in range(2)]
        nps = [ps(f"cl_n{n}", [H, BANK]) for n in range(2)]
        with Phase(nc, t, names) as (block, s):
            @block.scalar
            def _(eng):
                for n in range(NT):
                    if n >= 2:
                        eng.wait_ge(s["y"], n - 1)
                    eng.activation(oh[:, n % 2, :, :], t["o_t"][:, :, n * P:(n + 1) * P], ACT.Copy).then_inc(s["o_hi"], 1)
                    eng.wait_ge(s["n_tr"], n + 1)
                    eng.activation(nwt[:, n % 2, :], nps[n % 2][:, 0:P], ACT.Copy).then_inc(s["n_copy"], 1)
                    if n:
                        eng.wait_ge(s["y"], n)
                        eng.activation(y[:, n - 1, :], yps[(n - 1) % 2][:, 0:D], ACT.Copy).then_inc(s["y_copy"], 1)
                eng.wait_ge(s["y"], NT)
                eng.activation(y[:, NT - 1, :], yps[(NT - 1) % 2][:, 0:D], ACT.Copy).then_inc(s["y_copy"], 1)
                eng.wait_ge(s["var"], 1)
                eng.activation(rstd[:], rstd[:], ACT.Sqrt).then_inc(s["std"], 1)

            @block.tensor
            def _(eng):
                for n in range(NT):
                    if n >= 2:
                        eng.wait_ge(s["n_copy"], n - 1)
                    eng.transpose(nps[n % 2][:, 0:P], t["null_w"][:, n, :], t["ident"][:]).then_inc(s["n_tr"], 1)
                    eng.wait_ge(s["o_lo"], n + 1)
                    if n >= 2:
                        eng.wait_ge(s["y_copy"], n - 1)
                    out_ = yps[n % 2][:, 0:D]
                    for a in range(NPAIR):
                        three_products(eng, out_, [x[:, n % 2, a, :] for x in (oh, ol)],
                                       [t[x][:, a, :] for x in ("wo_h", "wo_l")], a == 0, False)
                    eng.wait_ge(s["n_copy"], n + 1)
                    eng.matmul(out_, nwt[:, n % 2, :], t["null_out"][:], start=False, stop=True).then_inc(s["y"], 1)

            @block.vector
            def _(eng):
                own = Own(eng, s["dve"])
                for n in range(NT):
                    eng.wait_ge(s["o_hi"], n + 1)
                    eng.tensor_tensor(ol[:, n % 2, :, :], t["o_t"][:, :, n * P:(n + 1) * P], f32(oh[:, n % 2, :, :]),
                                      ALU.subtract).then_inc(s["o_lo"], 1)
                    if n:
                        eng.wait_ge(s["y_copy"], n)
                        own.step(eng.bn_stats(stats[:, n - 1, :], y[:, n - 1, :]))
                eng.wait_ge(s["y_copy"], NT)
                own.step(eng.bn_stats(stats[:, NT - 1, :], y[:, NT - 1, :]))
                own.settle()
                for n in range(NT):
                    own.step(eng.bn_aggr(mv[:, n, :], stats[:, n, :]))
                own.settle()
                eng.tensor_scalar(rstd[:], mv[:, :, 1], EPS, None, ALU.add).then_inc(s["var"], 1)
                eng.wait_ge(s["std"], 1)
                own.step(eng.reciprocal(rstd[:], rstd[:]))
                own.settle()
                for n in range(NT):
                    own.step(eng.tensor_scalar(y[:, n, :], y[:, n, :], mv[:, n, 0:1], rstd[:, n:n + 1],
                                               ALU.subtract, ALU.mult))
                own.settle()
                own.step(eng.tensor_tensor(y[:], y[:], t["gain_out"][:].unsqueeze(1).to_broadcast([P, NT, D]), ALU.mult))
                own.settle()
                x = t["x"][:, bass.ds(b * NT, NT), :]
                if out is None:
                    own.step(eng.tensor_tensor(x, x, y[:], ALU.add))
                    own.settle()
                else:
                    eng.tensor_tensor(y[:], x, y[:], ALU.add).then_inc(s["added"], 1)

            if out is not None:
                @block.sync
                def _(eng):
                    eng.wait_ge(s["added"], 1)
                    eng.dma_start(out[bass.ds(b, 1), :, :].rearrange("o (t p) d -> p (o t) d", p=P), y[:]
                                  ).then_inc(s["stored"], 16)
                    eng.wait_ge(s["stored"], 16)


def program(nc, a, out):
    q_dram = nc.dram_tensor("q_dram", [H, P, S], F32, kind="Internal").ap()
    brow = nc.dram_tensor("brow_dram", [H, BROW], F32, kind="Internal").ap()
    with ExitStack() as stack, tensors(nc) as (sb, _):
        bands = nc.dram_tensor("bands_dram", [H, P, S], F32, kind="Internal").ap()
        t = {"in_ident": a["ident"], "in_iota": a["iota"], "in_dist": a["dist"], "q_dram": q_dram, "brow": brow,
             "bands": bands, "bands_sem": stack.enter_context(nc.semaphore("bands")), "bands_n": 0}
        t["pool"] = [stack.enter_context(nc.semaphore(f"phase{n}")) for n in range(Phase.POOL)]
        assert t["pool"][-1].num - t["pool"][0].num == Phase.POOL - 1
        t["x"] = sb("x", [P, NTT, D])
        t["ident"] = sb("ident", [P, P])
        t["ident_r"] = sb("ident_r", [P, P], FR)
        t["iota"] = sb("iota", [P, E])
        t["dist"] = sb("dist", [P, NT])
        with tensors(nc) as (sb0, _):
            t["xt_h"] = sb0("xt_h", [P, KD, NTT * P], FR)
            t["xt_l"] = sb0("xt_l", [P, KD, NTT * P], FR)
            t["expert_w"] = sb0("expert_w", [P, NU, NTT])
            moe_route(nc, t, a["x"].rearrange("b s d -> (b s) d"), a["wt_t"], a["cond_t"], a["wg_t"])
            moe_experts(nc, t, a["w_gate"], a["w_up"], a["w_down"])
        for layer, normed in ((1, True), (2, False), (3, True)):
            w = {n: a[f"L{layer}_{n}"] for n in WEIGHTS[layer]}
            if not normed:
                w = {{"g_in": "g_norm", "Wo": "Wout"}.get(n, n): ap for n, ap in w.items()}
            if normed:
                t["bands_n"] += 16
                relative_bias(nc, t, w)
            with tensors(nc) as (sbl, _):
                for part in "hl":
                    t[f"wq_{part}"] = sbl(f"wq_{part}", [P, KD, H * DH], FR)
                    t[f"wx_{part}"] = sbl(f"wx_{part}", [P, KD, 2 * DH + H], FR)
                    t[f"wo_{part}"] = sbl(f"wo_{part}", [P, NPAIR, D], FR)
                t["kscale"] = sbl("kscale", [P, DH])
                t["null_bias"] = sbl("null_bias", [P, H])
                t["gain_out"] = sbl("gain_out", [P, D])
                t["null_out"] = sbl("null_out", [H, D])
                t["k_hh"] = sbl("k_hh", [P, S], FR)
                t["k_lp"] = sbl("k_lp", [P, S], FR)
                t["v"] = sbl("v", [P, NT, DH])
                t["neg_null"] = sbl("neg_null", [P, NT, H])
                t["null_w"] = sbl("null_w", [P, NT, H])
                t["o_t"] = sbl("o_t", [P, NPAIR, S])
                layer_weights(nc, t, w, a["cond"], normed)
                with nc.Fori(0, B) as b:
                    project(nc, t, b, a["mask_f"] if normed else a["mask_k"], normed)
                    attend(nc, t, None if normed else a["fside"])
                    close_layer(nc, t, b, out if layer == 3 else None)


RELATIVE = ["g_norm", "Wq", "Wkv", "q_scale", "k_scale", "null_attn_bias", "w0", "b0", "g0", "w1", "b1", "g1", "w2", "b2",
            "Wout", "g_out"]
WEIGHTS = {1: RELATIVE, 2: ["g_in", "null_attn_bias", "Wq", "Wkv", "Wo", "g_out"], 3: RELATIVE}


def kernel(**inputs):
    import numpy as _np
    import concourse.bacc as _bacc
    from concourse import mybir as _mybir
    from concourse.bass_utils import run_bass_kernel_spmd as _run

    raw = {n: _np.asarray(v) for n, v in inputs.items()}
    arrays = {
        "x": raw["x"], "cond": raw["cond_64"], "cond_t": raw["cond_64"].T, "fside": raw["fside_16xSxS_0"],
        "mask_f": raw["mask_BxS_bf1"].reshape(B, NT, P).transpose(0, 2, 1),
        "mask_k": raw["mask_BxS_bk0"].reshape(B, NT, P).transpose(0, 2, 1),
        "wt_t": raw["L0_cond_wt"].T, "wg_t": raw["L0_cond_wg"].T,
        "w_gate": _np.concatenate([raw["L0_cond_w_gate"], raw["L0_cond_sw_gate"].reshape(D, 2, M).transpose(1, 0, 2)]),
        "w_up": _np.concatenate([raw["L0_cond_w_up"], raw["L0_cond_sw_up"].reshape(D, 2, M).transpose(1, 0, 2)]),
        "w_down": _np.concatenate([raw["L0_cond_w_down"], raw["L0_cond_sw_down"].reshape(2, M, D)]),
        "ident": _np.eye(P, dtype=_np.float32),
        "iota": _np.tile(_np.arange(E, dtype=_np.float32), (P, 1)),
        "dist": (S - 1 - _np.arange(S, dtype=_np.float32)).reshape(NT, P).T,
    }
    for layer, names in WEIGHTS.items():
        for n in names:
            arrays[f"L{layer}_{n}"] = raw[f"L{layer}_cond_{n}"]
            if n in ("g_norm", "g_in"):
                arrays[f"L{layer}_{n}"] = arrays[f"L{layer}_{n}"].reshape(KD, P).T
    arrays = {f"in_{n}": _np.ascontiguousarray(v) for n, v in arrays.items()}

    nc = _bacc.Bacc("TRN2", target_bir_lowering=False, num_devices=1)
    aps = {n[3:]: nc.dram_tensor(n, v.shape, _mybir.dt.from_np(v.dtype), kind="ExternalInput").ap()
           for n, v in arrays.items()}
    out = nc.dram_tensor("out", (B, S, D), F32, kind="ExternalOutput").ap()
    program(nc, aps, out)
    result = _run(nc, [arrays], core_ids=[0])
    return result.results[0]["out"]
```

```python
from contextlib import ExitStack, contextmanager
from itertools import count

import numpy as np

import concourse.bass as bass
from concourse import mybir

F32 = mybir.dt.float32
FR = mybir.dt.float32r
U8 = mybir.dt.uint8
U32 = mybir.dt.uint32
ALU = mybir.AluOpType
ACT = mybir.ActivationFunctionType
AX = mybir.AxisListType

P = 128
B, S, D = 2, 1024, 256
NT = S // P
NTT = B * NT
KD = D // P
H, DH = 16, 64
NPAIR = H // 2
E, TOPK, M = 8, 2, 128
NU = E + 2
G = 64
BANK = 512
BIG = 1e30
EPS = 1e-5
BROW = S + P


SERIAL = count()


class Phase:

    POOL = 40

    def __init__(self, nc, t, names):
        self.nc, self.pool, self.names = nc, t["pool"], names

    def __enter__(self):
        self.stack = ExitStack()
        self.block = self.stack.enter_context(self.nc.Block())
        assert len(self.names) <= self.POOL
        return self.block, dict(zip(self.names, self.pool))

    def __exit__(self, *exc):
        self.stack.close()
        if exc[0] is None:
            self.nc.all_engine_barrier(sems_to_clear=range(self.pool[0].num, self.pool[len(self.names) - 1].num + 1))


class Own:

    def __init__(self, eng, sem):
        self.eng, self.sem, self.n = eng, sem, 0

    def step(self, instruction):
        instruction.then_inc(self.sem, 1)
        self.n += 1

    def settle(self):
        self.eng.wait_ge(self.sem, self.n)


class Turns:

    def __init__(self, sems, turn, marks):
        self.sems, self.turn, self.marks = sems, turn, marks

    def wait(self, eng, name, n):
        eng.wait_ge(self.sems[name], self.turn * self.marks[name] + (self.marks[name] + n))


def start(eng, sems, marks, *names):
    for name in names:
        eng.sem_inc(sems[name], marks[name])


def run(eng, step, turns, size, early, late):
    def steps(turn, at, to, has):
        for n in range(at, to):
            step(turn, n, has)

    def peeled(turn):
        return lambda n, per: 0 <= turn * per + n < turns * per

    steps(-1, size - early, size + late, peeled(-1))
    with eng.Fori(0, turns - 1) as turn:
        steps(turn, late, size + late, lambda n, per: True)
    steps(turns - 1, late, size + late, peeled(turns - 1))


@contextmanager
def tensors(nc):
    serial = next(SERIAL)
    with ExitStack() as stack:
        def sb(name, shape, dt=F32):
            return stack.enter_context(nc.sbuf_tensor(f"{name}_{serial}", shape, dt))

        def ps(name, shape, dt=F32):
            return stack.enter_context(nc.psum_tensor(f"{name}_{serial}", shape, dt))

        yield sb, ps


def rows(vector, n=P):
    return bass.AP(vector.tensor, vector.offset, [[0, n], [1, vector.shape[-1]]])


def f32(ap):
    return ap.bitcast(F32)


def three_products(eng, out, left, right, start, stop):
    pairs = ((0, 0), (0, 1), (1, 0))
    for n, (a, b) in enumerate(pairs):
        last = eng.matmul(out, left[a], right[b], start=start and n == 0, stop=stop and n == len(pairs) - 1)
    return last



def moe_route(nc, t, x, wt_t, cond_t, wg_t):
    CH = B * S // BANK
    TPC = NTT // CH
    NTR = 4
    names = ["w_in", "x_tr", "x_hi", "x_lo", "w_hl", "cond_mm", "lt", "lt_copy", "logits", "dve", "exp_in", "exp_out"]
    names += [f"x_in{c}" for c in range(CH)]
    with tensors(nc) as (sb, ps):
        wt = sb("route_wt", [P, KD, E])
        wt_h, wt_l = (sb(f"route_wt_{n}", [P, KD, P], FR) for n in "hl")
        cond = sb("route_cond", [G, B])
        cond_l = sb("route_cond_l", [E, B])
        lts = sb("route_lts", [E, B * S])
        wg = sb("route_wg", [G, E])
        logits = sb("route_logits", [P, NTT, E])
        top = sb("route_top", [P, NTT, E])
        top_i = sb("route_top_i", [P, NTT, E], U32)
        top_f = sb("route_top_f", [P, NTT, E])
        shifted = sb("route_shifted", [P, NTT, E])
        score = sb("route_score", [P, NTT, E])
        chosen = sb("route_chosen", [P, NTT, E])
        other = sb("route_other", [P, NTT, E])
        total = sb("route_total", [P, NTT])
        inv = sb("route_inv", [P, NTT])
        tr = [ps(f"route_tr{n}", [P, BANK])[:, 0:KD * P] for n in range(NTR)]
        lt = [ps(f"route_lt{n}", [P, BANK]) for n in range(2)]
        cp = ps("route_cp", [E, BANK])[:, 0:B]
        lp = ps("route_lp", [P, BANK])[:, 0:NTT * E].rearrange("p (n e) -> p n e", e=E)
        with Phase(nc, t, names) as (block, s):
            @block.sync
            def _(eng):
                eng.dma_start(t["ident"][:], t["in_ident"]).then_inc(s["w_in"], 16)
                eng.dma_start(t["iota"][:], t["in_iota"]).then_inc(s["w_in"], 16)
                eng.dma_start(wt[:], wt_t.rearrange("(k p) e -> p k e", p=P)).then_inc(s["w_in"], 16)
                eng.dma_start(cond[:], cond_t).then_inc(s["w_in"], 16)
                eng.dma_start(wg[:], wg_t).then_inc(s["w_in"], 16)
                for c in range(CH):
                    eng.dma_start(t["x"][:, TPC * c:TPC * (c + 1), :],
                                  x[BANK * c:BANK * (c + 1), :].rearrange("(t p) d -> p t d", p=P)
                                  ).then_inc(s[f"x_in{c}"], 16)
                eng.wait_ge(s["w_in"], 80)
                for c in range(CH):
                    eng.wait_ge(s[f"x_in{c}"], 16)

            @block.tensor
            def _(eng):
                eng.wait_ge(s["w_in"], 80)
                eng.matmul(cp[:], wg[:], cond[:], start=True, stop=True).then_inc(s["cond_mm"], 1)

                def chunk_logits(c):
                    eng.wait_ge(s["w_hl"], 1)
                    eng.wait_ge(s["x_lo"], TPC * (c + 1))
                    if c >= 2:
                        eng.wait_ge(s["lt_copy"], c - 1)
                    for k in range(KD):
                        last = three_products(eng, lt[c % 2][:], [w[:, k, :] for w in (wt_h, wt_l)],
                                              [t[x][:, k, c * BANK:(c + 1) * BANK] for x in ("xt_h", "xt_l")],
                                              k == 0, k == KD - 1)
                    last.then_inc(s["lt"], 1)

                for n in range(NTT):
                    if n % TPC == 0:
                        eng.wait_ge(s[f"x_in{n // TPC}"], 16)
                    if n >= NTR:
                        eng.wait_ge(s["x_lo"], n - NTR + 1)
                    for k in range(KD):
                        last = eng.transpose(tr[n % NTR][:, k * P:(k + 1) * P],
                                             t["x"][:, n, k * P:(k + 1) * P], t["ident"][:])
                    last.then_inc(s["x_tr"], 1)
                    if n % TPC == 1 and n > TPC:
                        chunk_logits(n // TPC - 1)
                chunk_logits(CH - 1)
                for n in range(NTT):
                    eng.wait_ge(s["lt_copy"], n // TPC + 1)
                    last = eng.transpose(lp[:, n, :], lts[:, n * P:(n + 1) * P], t["ident"][0:E, 0:E])
                last.then_inc(s["logits"], 1)

            @block.scalar
            def _(eng):
                for n in range(NTT):
                    eng.wait_ge(s["x_tr"], n + 1)
                    eng.activation(t["xt_h"][:, :, n * P:(n + 1) * P],
                                   tr[n % NTR].rearrange("p (k i) -> p k i", k=KD), ACT.Copy).then_inc(s["x_hi"], 1)
                eng.wait_ge(s["exp_in"], 1)
                eng.activation(score[:], shifted[:], ACT.Exp).then_inc(s["exp_out"], 1)

            @block.vector
            def _(eng):
                own = Own(eng, s["dve"])
                eng.wait_ge(s["w_in"], 80)
                own.step(eng.tensor_copy(t["ident_r"][:], t["ident"][:]))
                for w in (wt_h, wt_l):
                    own.step(eng.memset(f32(w[:]), 0.0))
                own.settle()
                own.step(eng.tensor_copy(wt_h[:, :, 0:E], wt[:]))
                own.settle()
                eng.tensor_tensor(wt_l[:, :, 0:E], wt[:], f32(wt_h[:, :, 0:E]), ALU.subtract).then_inc(s["w_hl"], 1)
                eng.wait_ge(s["cond_mm"], 1)
                own.step(eng.tensor_copy(cond_l[:], cp[:]))
                own.settle()

                def mean_logits(c):
                    eng.wait_ge(s["lt"], c + 1)
                    b = c * BANK // S
                    eng.tensor_scalar(lts[:, c * BANK:(c + 1) * BANK], lt[c % 2][0:E, :], cond_l[:, b:b + 1], 0.5,
                                      ALU.add, ALU.mult).then_inc(s["lt_copy"], 1)

                for n in range(NTT):
                    eng.wait_ge(s["x_hi"], n + 1)
                    eng.tensor_tensor(t["xt_l"][:, :, n * P:(n + 1) * P],
                                      tr[n % NTR].rearrange("p (k i) -> p k i", k=KD),
                                      f32(t["xt_h"][:, :, n * P:(n + 1) * P]), ALU.subtract).then_inc(s["x_lo"], 1)
                    if n % TPC == TPC - 1 and n > TPC:
                        mean_logits(n // TPC - 1)
                mean_logits(CH - 1)
                eng.wait_ge(s["logits"], 1)
                own.step(eng.tensor_copy(logits[:], lp[:]))
                own.settle()
                for n in range(NTT):
                    own.step(eng.max(top[:, n, :], logits[:, n, :]))
                own.settle()
                for n in range(NTT):
                    own.step(eng.max_index(top_i[:, n, :], top[:, n, :], logits[:, n, :]))
                eng.tensor_tensor(shifted[:], logits[:], top[:, :, 0:1].to_broadcast([P, NTT, E]),
                                  ALU.subtract).then_inc(s["exp_in"], 1)
                own.settle()
                own.step(eng.tensor_copy(top_f[:], top_i[:]))
                own.settle()
                iota = t["iota"][:].unsqueeze(1).to_broadcast([P, NTT, E])
                own.step(eng.tensor_tensor(chosen[:], iota, top_f[:, :, 0:1].to_broadcast([P, NTT, E]), ALU.is_equal))
                own.step(eng.tensor_tensor(other[:], iota, top_f[:, :, 1:2].to_broadcast([P, NTT, E]), ALU.is_equal))
                own.settle()
                own.step(eng.tensor_tensor(chosen[:], chosen[:], other[:], ALU.add))
                eng.wait_ge(s["exp_out"], 1)

                def normalize(eps):
                    own.step(eng.tensor_reduce(total[:], score[:], AX.X, ALU.add))
                    own.settle()
                    if eps:
                        own.step(eng.tensor_scalar(total[:], total[:], eps, None, ALU.add))
                        own.settle()
                    own.step(eng.reciprocal(inv[:], total[:]))
                    own.settle()

                normalize(0.0)
                own.step(eng.tensor_tensor(score[:], score[:], inv[:].unsqueeze(2).to_broadcast([P, NTT, E]), ALU.mult))
                own.settle()
                own.step(eng.tensor_tensor(score[:], score[:], chosen[:], ALU.mult))
                own.settle()
                normalize(1e-20)
                own.step(eng.memset(t["expert_w"][:], 1.0))
                own.settle()
                own.step(eng.tensor_tensor(t["expert_w"][:, 0:E, :].rearrange("p e n -> p n e"), score[:],
                                           inv[:].unsqueeze(2).to_broadcast([P, NTT, E]), ALU.mult))
                own.settle()


def moe_experts(nc, t, w_gate, w_up, w_down):
    NC = 4
    PAR = 2
    TURN = PAR * NC
    TPC = NTT // NC
    WC = 2 * KD * M + D
    RUN = (NU // PAR, TURN, 2, 2)
    names = ["w_in0", "w_in1", "gate", "w_split", "w_hi", "gu", "slope", "leaky", "hidden", "hid_hi", "hid_lo", "down",
             "added"]
    with tensors(nc) as (sb, ps):
        raw = sb("moe_raw", [P, PAR, WC])
        wh, wl = (sb(f"moe_w{n}", [P, PAR, WC], FR) for n in "hl")
        slope = sb("moe_slope", [P, 2, BANK])
        leaky = sb("moe_leaky", [P, 2, BANK])
        hid = sb("moe_hid", [P, 2, BANK])
        hid_h, hid_l = (sb(f"moe_hid_{n}", [P, 2, BANK], FR) for n in "hl")
        unit_w = sb("moe_unit_w", [P, PAR, NTT])
        gate = [ps(f"moe_gate{n}", [P, BANK]) for n in range(2)]
        up = [ps(f"moe_up{n}", [P, BANK]) for n in range(2)]
        down = [ps(f"moe_down{n}", [P, TPC, D]) for n in range(2)]

        def w_of(tile, q, kind, k):
            at = {"gate": 0, "up": KD * M}.get(kind, 2 * KD * M) + k * M
            return tile[:, q, at:at + (D if kind == "down" else M)]

        marks = dict(w_split=PAR, gu=TURN, slope=TURN, w_hi=2 * PAR, leaky=TURN, hidden=TURN, hid_hi=TURN, hid_lo=TURN,
                     down=TURN, added=TURN)
        with Phase(nc, t, names) as (block, s):
            def load(eng, unit, q):
                one = bass.ds(unit, 1)
                for src, at in ((w_gate, 0), (w_up, KD * M)):
                    eng.dma_start(raw[:, q, at:at + KD * M].rearrange("p (k m) -> p k m", k=KD),
                                  src[one, :, :].rearrange("o (k p) m -> p (o k) m", p=P)).then_inc(s[f"w_in{q}"], 16)
                eng.dma_start(raw[:, q, 2 * KD * M:WC],
                              w_down[one, :, :].rearrange("o p d -> p (o d)")).then_inc(s[f"w_in{q}"], 16)

            @block.sync
            def _(eng):
                with eng.Fori(0, NU // PAR) as it:
                    turn = Turns(s, it, marks)
                    for q in range(PAR):
                        turn.wait(eng, "w_split", q + 1 - PAR)
                        load(eng, it * PAR + q, q)
                for q in range(PAR):
                    eng.wait_ge(s[f"w_in{q}"], 48 * (NU // PAR))

            @block.tensor
            def _(eng):
                def gate_up(turn, c):
                    q, tok = c // NC % PAR, c % NC
                    if c % NC == 0:
                        turn.wait(eng, "w_split", c // NC + 1)
                    turn.wait(eng, "hidden", c - 1)
                    for kind, out in (("gate", gate), ("up", up)):
                        for k in range(KD):
                            last = three_products(
                                eng, out[c % 2][:], [w_of(w, q, kind, k) for w in (wh, wl)],
                                [t[x][:, k, tok * BANK:(tok + 1) * BANK] for x in ("xt_h", "xt_l")],
                                k == 0, k == KD - 1)
                    last.then_inc(s["gu"], 1)

                def down_of(turn, c):
                    q = c // NC % PAR
                    turn.wait(eng, "hid_lo", c + 1)
                    turn.wait(eng, "added", c - 1)
                    for i in range(TPC):
                        last = three_products(
                            eng, down[c % 2][:, i, :], [h[:, c % 2, i * P:(i + 1) * P] for h in (hid_h, hid_l)],
                            [w_of(w, q, "down", 0) for w in (wh, wl)], True, True)
                    last.then_inc(s["down"], 1)

                def step(it, c, has):
                    turn = Turns(s, it, marks)
                    if has(c + 1, TURN):
                        gate_up(turn, c + 1)
                    if has(c - 1, TURN):
                        down_of(turn, c - 1)

                start(eng, s, marks, "gu", "down")
                run(eng, step, *RUN)

            @block.scalar
            def _(eng):
                def step(it, c, has):
                    if not has(c, TURN):
                        return
                    turn = Turns(s, it, marks)
                    turn.wait(eng, "gu", c + 1)
                    turn.wait(eng, "hidden", c - 1)
                    eng.activation(slope[:, c % 2, :], gate[c % 2][:], ACT.Copy, scale=0.01).then_inc(s["slope"], 1)
                    turn.wait(eng, "hidden", c + 1)
                    turn.wait(eng, "down", c - 1)
                    eng.activation(hid_h[:, c % 2, :], hid[:, c % 2, :], ACT.Copy).then_inc(s["hid_hi"], 1)

                start(eng, s, marks, "slope", "hid_hi")
                run(eng, step, *RUN)

            @block.gpsimd
            def _(eng):
                start(eng, s, marks, "hid_lo")
                with eng.Fori(0, NU // PAR) as it:
                    turn = Turns(s, it, marks)
                    for c in range(TURN):
                        turn.wait(eng, "hid_hi", c + 1)
                        eng.tensor_tensor(hid_l[:, c % 2, :], hid[:, c % 2, :], f32(hid_h[:, c % 2, :]),
                                          ALU.subtract).then_inc(s["hid_lo"], 1)

            @block.vector
            def _(eng):
                def split(turn, it, unit):
                    q = unit % PAR
                    eng.wait_ge(s[f"w_in{q}"], it * 48 + 48 * (unit // PAR + 1))
                    turn.wait(eng, "down", (unit - PAR + 1) * NC)
                    turn.wait(eng, "added", (unit - PAR + 1) * NC)
                    eng.sem_inc(s["gate"], 1)
                    eng.tensor_copy(wh[:, q, :], raw[:, q, :]).then_inc(s["w_hi"], 1)
                    eng.tensor_copy(unit_w[:, q, :],
                                    t["expert_w"][:, bass.ds(it * PAR + unit, 1), :].rearrange("p o n -> p (o n)")
                                    ).then_inc(s["w_hi"], 1)
                    turn.wait(eng, "w_hi", 2 * unit + 2)
                    eng.tensor_tensor(wl[:, q, :], raw[:, q, :], f32(wh[:, q, :]), ALU.subtract
                                      ).then_inc(s["w_split"], 1)

                def hidden(turn, c):
                    turn.wait(eng, "slope", c + 1)
                    eng.tensor_tensor(leaky[:, c % 2, :], gate[c % 2][:], slope[:, c % 2, :], ALU.max
                                      ).then_inc(s["leaky"], 1)
                    turn.wait(eng, "leaky", c + 1)
                    turn.wait(eng, "hid_lo", c - 1)
                    eng.tensor_tensor(hid[:, c % 2, :], leaky[:, c % 2, :], up[c % 2][:], ALU.mult
                                      ).then_inc(s["hidden"], 1)

                def add_down(turn, c):
                    q = c // NC % PAR
                    turn.wait(eng, "down", c + 1)
                    turn.wait(eng, "added", c)
                    for i in range(TPC):
                        n = (c % NC) * TPC + i
                        last = eng.scalar_tensor_tensor(t["x"][:, n, :], down[c % 2][:, i, :], unit_w[:, q, n:n + 1],
                                                        t["x"][:, n, :], ALU.mult, ALU.add)
                    last.then_inc(s["added"], 1)

                def step(it, c, has):
                    turn = Turns(s, it, marks)
                    if has(c, TURN):
                        hidden(turn, c)
                    if has(c - 2, TURN):
                        add_down(turn, c - 2)
                    if c % NC == 2 and has(c // NC + 1, PAR):
                        split(turn, it, c // NC + 1)

                start(eng, s, marks, "w_split", "leaky", "w_hi", "hidden", "added")
                run(eng, step, *RUN)
                eng.wait_ge(s["added"], TURN * (NU // PAR + 1))



def prepare_layer(nc, t, w, cond, mask, normed):
    names = ["wide_in", "small_in", "dve", "norm_in", "norm", "v0_in", "folded", "k0n", "prod", "hi", "lo", "null_mm"]
    names += ["rb_in", "rb_dve", "act_in", "act_out", "tr", "tr_free", "tr_hi", "mm", "silu", "out"]
    NS, HALF = 2, NT // 2
    HALVES = range(NT // HALF)
    with tensors(nc) as (sb, ps):
        wq = sb("lw_wq", [P, KD, H * DH])
        prod = sb("lw_prod", [P, KD, H * DH])
        wx = sb("lw_wx", [P, KD, 2 * DH + H])
        wo = sb("lw_wo", [P, NPAIR, D])
        gain = sb("lw_gain", [P, KD])
        k0 = sb("lw_k0", [P, DH])
        k0n = sb("lw_k0n", [P, DH])
        qs = sb("lw_qs", [P, DH])
        ss = sb("lw_ss", [P, 1])
        v0 = sb("lw_v0", [P, 1])
        mask8 = sb("lw_mask8", [P, B, NT], U8)
        v0m = sb("lw_v0m", [P, NPAIR * H])
        vps = ps("lw_vps", [H, D])
        n_small, n_in = 16 * (8 + 2 * normed), 16 * 2
        parts = ((wq, "wq_h", "wq_l"), (wx, "wx_h", "wx_l"), (wo, "wo_h", "wo_l"))
        if normed:
            vec = {n: sb(f"rb_{n}", [P, D]) for n in ("w0", "b0", "g0", "b1", "g1")}
            w1 = sb("rb_w1", [P, KD, D])
            w1h, w1l = (sb(f"rb_w1{n}", [P, KD, D], FR) for n in "hl")
            w2 = sb("rb_w2", [P, KD, P])
            w2h, w2l = (sb(f"rb_w2{n}", [P, KD, P], FR) for n in "hl")
            b2 = sb("rb_b2", [H, 1])
            h = sb("rb_h", [P, NT, D])
            e = sb("rb_e", [P, NT, D])
            stats = sb("rb_stats", [P, NT, 6])
            mv = sb("rb_mv", [P, NT, 2])
            rstd = sb("rb_rstd", [P, NT])
            hth, htl = (sb(f"rb_ht{n}", [P, KD, S], FR) for n in "hl")
            brow = sb("rb_brow", [H, BROW])
            tr = [ps(f"rb_tr{n}", [P, BANK])[:, 0:KD * P] for n in range(2)]
            mm = ps("rb_mm", [P, NT, D])

        with Phase(nc, t, names) as (block, s):
            @block.sync
            def _(eng):
                def load(name, dst, src):
                    eng.dma_start(dst, src).then_inc(s[name], 16)

                if normed:
                    load("rb_in", t["dist"][:], t["in_dist"])
                    for n in vec:
                        load("rb_in", vec[n][:], rows(w[n]))
                    load("rb_in", w1[:], w["w1"].rearrange("(k p) n -> p k n", p=P))
                    eng.wait_ge(s["rb_dve"], 1)
                    load("rb_in", w2[:, :, 0:H], w["w2"].rearrange("(k p) n -> p k n", p=P))
                    load("rb_in", b2[:], w["b2"].rearrange("(n o) -> n o", o=1))
                load("small_in", gain[:], w["g_norm"])
                load("small_in", mask8[:], mask.rearrange("b p t -> p b t"))
                load("small_in", wx[:, :, 0:2 * DH], w["Wkv"].rearrange("(k p) n -> p k n", p=P))
                load("small_in", k0[:], rows(cond[0, :]))
                for c in range(2):
                    load("small_in", v0[c * DH:(c + 1) * DH, :], cond[1, :].rearrange("(d o) -> d o", o=1))
                if normed:
                    load("small_in", t["kscale"][:], rows(w["k_scale"]))
                    load("small_in", qs[:], rows(w["q_scale"]))
                load("small_in", t["null_bias"][:], rows(w["null_attn_bias"]))
                load("small_in", t["gain_out"][:], rows(w["g_out"]))
                load("wide_in", wq[:], w["Wq"].rearrange("(k p) n -> p k n", p=P))
                load("wide_in", wo[:], w["Wout"].rearrange("(a p) n -> p a n", p=P))
                if normed:
                    eng.wait_ge(s["rb_in"], 16 * 9)
                    eng.wait_ge(s["out"], 1)
                    load("rb_in", t["brow"], brow[:])
                    eng.wait_ge(s["rb_in"], 16 * 10)
                    eng.dma_start(t["bands"], bass.AP(t["brow"].tensor, P - 1, [[BROW, H], [-1, P], [1, S]])
                                  ).then_inc(t["bands_sem"], 16)
                eng.wait_ge(s["small_in"], n_small)
                eng.wait_ge(s["wide_in"], n_in)

            def null_products(eng):
                eng.wait_ge(s["folded"], 1)
                eng.wait_ge(s["k0n"], 1)
                for k in range(KD):
                    last = eng.tensor_tensor(prod[:, k, :].rearrange("p (h d) -> p h d", h=H),
                                             wq[:, k, :].rearrange("p (h d) -> p h d", h=H),
                                             k0n[:].unsqueeze(1).to_broadcast([P, H, DH]), ALU.mult)
                last.then_inc(s["prod"], 1)

            def low_part(eng, n):
                full, hi, lo = (parts[0], parts[2])[n]
                eng.wait_ge(s["hi"], n + 1)
                eng.tensor_tensor(t[lo][:], full[:], f32(t[hi][:]), ALU.subtract).then_inc(s["lo"], 1)

            @block.gpsimd
            def _(eng):
                if normed:
                    null_products(eng)
                    low_part(eng, 0)
                    low_part(eng, 1)
                eng.wait_ge(s["lo"], 2)

            @block.vector
            def _(eng):
                own = Own(eng, s["dve"])
                rb = Own(eng, s["rb_dve"])

                def null_key():
                    eng.wait_ge(s["small_in"], n_small)
                    own.step(eng.tensor_copy(t["penalty"][:], mask8[:]))
                    own.settle()
                    own.step(eng.tensor_scalar(t["penalty"][:], t["penalty"][:], BIG, -BIG, ALU.mult, ALU.add))
                    for c in range(2):
                        last = eng.tensor_copy(v0m[c * DH:(c + 1) * DH, c:c + (H + 2) * (NPAIR - 1) + 1:H + 2],
                                               v0[c * DH:(c + 1) * DH, :].to_broadcast([DH, NPAIR]))
                    last.then_inc(s["v0_in"], 1)
                    for k in range(KD):
                        own.step(eng.tensor_scalar(wx[:, k, 0:2 * DH], wx[:, k, 0:2 * DH], gain[:, k:k + 1], None, ALU.mult))
                    if not normed:
                        eng.tensor_scalar(k0n[:], k0[:], DH ** -0.5, None, ALU.mult).then_inc(s["k0n"], 1)
                        return
                    own.step(eng.scalar_tensor_tensor(t["kscale"][:], t["kscale"][:], 8.0, qs[:], ALU.mult, ALU.mult))
                    own.step(eng.tensor_tensor(k0n[:], k0[:], k0[:], ALU.mult))
                    own.settle()
                    eng.tensor_reduce(ss[:], k0n[:], AX.X, ALU.add).then_inc(s["norm_in"], 1)
                    eng.wait_ge(s["norm"], 1)
                    own.step(eng.tensor_scalar(ss[:], ss[:], 1e-12, None, ALU.max))
                    own.settle()
                    own.step(eng.reciprocal(ss[:], ss[:]))
                    own.settle()
                    eng.scalar_tensor_tensor(k0n[:], k0[:], ss[:, 0:1], t["kscale"][:], ALU.mult, ALU.mult
                                             ).then_inc(s["k0n"], 1)

                def null_columns():
                    eng.wait_ge(s["prod"], 1)
                    for k in range(KD):
                        own.step(eng.tensor_reduce(wx[:, k, 2 * DH:], prod[:, k, :].rearrange("p (h d) -> p h d", h=H),
                                                   AX.X, ALU.add))
                    own.settle()
                    own.step(eng.tensor_copy(t["wx_h"][:], wx[:]))
                    own.settle()
                    own.step(eng.tensor_tensor(t["wx_l"][:], wx[:], f32(t["wx_h"][:]), ALU.subtract))
                    eng.wait_ge(s["null_mm"], 1)
                    own.step(eng.tensor_copy(t["null_out"][:], vps[:]))
                    own.settle()

                def spread(x):
                    return x[:].unsqueeze(1).to_broadcast([P, HALF, D])

                def distance_layer(layer):
                    def tiles(i):
                        return range(i * HALF, (i + 1) * HALF)

                    def half(x, i):
                        return x[:, i * HALF:(i + 1) * HALF]

                    for i in HALVES:
                        if layer:
                            eng.wait_ge(s["mm"], i + 1)
                            rb.step(eng.tensor_tensor(half(h, i), half(mm, i), spread(vec["b1"]), ALU.add))
                        else:
                            for n in tiles(i):
                                rb.step(eng.scalar_tensor_tensor(h[:, n, :], vec["w0"][:], t["dist"][:, n:n + 1],
                                                                 vec["b0"][:], ALU.mult, ALU.add))
                        rb.settle()
                        for n in tiles(i):
                            rb.step(eng.bn_stats(stats[:, n, :], h[:, n, :]))
                        rb.settle()
                        for n in tiles(i):
                            rb.step(eng.bn_aggr(mv[:, n, :], stats[:, n, :]))
                        rb.settle()
                        eng.tensor_scalar(half(rstd, i), mv[:, i * HALF:(i + 1) * HALF, 1], EPS, None, ALU.add
                                          ).then_inc(s["act_in"], 1)
                    for i in HALVES:
                        eng.wait_ge(s["act_out"], 4 * layer + i + 1)
                        rb.step(eng.reciprocal(half(rstd, i), half(rstd, i)))
                        rb.settle()
                        for n in tiles(i):
                            rb.step(eng.tensor_scalar(h[:, n, :], h[:, n, :], mv[:, n, 0:1], rstd[:, n:n + 1],
                                                      ALU.subtract, ALU.mult))
                        rb.settle()
                        eng.tensor_tensor(half(h, i), half(h, i), spread(vec[f"g{layer}"]), ALU.mult
                                          ).then_inc(s["act_in"], 1)
                    for i in HALVES:
                        eng.wait_ge(s["act_out"], 4 * layer + i + 3)
                        rb.step(eng.tensor_scalar(half(e, i), half(e, i), 1.0, None, ALU.add))
                        rb.settle()
                        rb.step(eng.reciprocal(half(e, i), half(e, i)))
                        rb.settle()
                        eng.tensor_tensor(half(h, i), half(h, i), half(e, i), ALU.mult).then_inc(s["silu"], 1)
                    for n in range(NT):
                        eng.wait_ge(s["tr_hi"], NT * layer + n + 1)
                        eng.tensor_tensor(htl[:, :, n * P:(n + 1) * P], tr[n % 2].rearrange("p (k i) -> p k i", k=KD),
                                          f32(hth[:, :, n * P:(n + 1) * P]), ALU.subtract).then_inc(s["tr_free"], 1)

                if normed:
                    rb.step(eng.memset(w2[:], 0.0))
                    rb.step(eng.memset(brow[:], -BIG))
                own.step(eng.memset(v0m[:], 0.0))
                if not normed:
                    null_key()
                    null_products(eng)
                    low_part(eng, 0)
                    null_columns()
                    low_part(eng, 1)
                    return
                eng.wait_ge(s["rb_in"], 16 * 9)
                rb.settle()
                for full, hi in ((w1, w1h), (w2, w2h)):
                    rb.step(eng.tensor_copy(hi[:], full[:]))
                rb.settle()
                for full, hi, lo in ((w1, w1h, w1l), (w2, w2h, w2l)):
                    rb.step(eng.tensor_tensor(lo[:], full[:], f32(hi[:]), ALU.subtract))
                distance_layer(0)
                null_key()
                distance_layer(1)
                null_columns()
                eng.wait_ge(s["mm"], len(HALVES) + 1)
                eng.tensor_scalar(brow[:, 0:S], mm[0:H, 0:S // D, :].rearrange("p a b -> p (a b)"), b2[:], None, ALU.add
                                  ).then_inc(s["out"], 1)

            @block.scalar
            def _(eng):
                def fold():
                    if normed:
                        eng.wait_ge(s["norm_in"], 1)
                        eng.activation(ss[:], ss[:], ACT.Sqrt).then_inc(s["norm"], 1)
                    eng.wait_ge(s["small_in"], n_small)
                    eng.wait_ge(s["wide_in"], n_in)
                    for k in range(KD):
                        last = eng.activation(wq[:, k, :], wq[:, k, :], ACT.Copy, scale=gain[:, k:k + 1])
                    last.then_inc(s["folded"], 1)
                    eng.wait_ge(s["folded"], 1)
                    for full, hi, _ in (parts[0], parts[2]):
                        eng.activation(t[hi][:], full[:], ACT.Copy).then_inc(s["hi"], 1)

                if not normed:
                    fold()
                    eng.wait_ge(s["hi"], 2)
                    return
                for layer in range(NS):
                    for i in HALVES:
                        at = slice(i * HALF, (i + 1) * HALF)
                        eng.wait_ge(s["act_in"], 4 * layer + i + 1)
                        eng.activation(rstd[:, at], rstd[:, at], ACT.Sqrt).then_inc(s["act_out"], 1)
                    for i in HALVES:
                        at = slice(i * HALF, (i + 1) * HALF)
                        eng.wait_ge(s["act_in"], 4 * layer + i + 3)
                        eng.activation(e[:, at, :], h[:, at, :], ACT.Exp, scale=-1.0).then_inc(s["act_out"], 1)
                    for n in range(NT):
                        if layer and n % HALF == 0:
                            eng.wait_ge(s["mm"], n // HALF + 1)
                        eng.wait_ge(s["tr"], NT * layer + n + 1)
                        eng.activation(hth[:, :, n * P:(n + 1) * P], tr[n % 2].rearrange("p (k i) -> p k i", k=KD),
                                       ACT.Copy).then_inc(s["tr_hi"], 1)
                    if layer == 0:
                        fold()

            @block.tensor
            def _(eng):
                def null_values():
                    eng.wait_ge(s["wide_in"], n_in)
                    eng.wait_ge(s["v0_in"], 1)
                    for a in range(NPAIR):
                        last = eng.matmul(vps[:], v0m[:, a * H:(a + 1) * H], wo[:, a, :], start=a == 0,
                                          stop=a == NPAIR - 1)
                    last.then_inc(s["null_mm"], 1)

                if not normed:
                    null_values()
                    return
                for layer in range(NS):
                    for n in range(NT):
                        if n % HALF == 0:
                            eng.wait_ge(s["silu"], len(HALVES) * layer + n // HALF + 1)
                        if NT * layer + n >= 2:
                            eng.wait_ge(s["tr_free"], NT * layer + n - 1)
                        for k in range(KD):
                            last = eng.transpose(tr[n % 2][:, k * P:(k + 1) * P], h[:, n, k * P:(k + 1) * P],
                                                 t["ident"][:])
                        last.then_inc(s["tr"], 1)
                    if layer == 0:
                        for i in HALVES:
                            eng.wait_ge(s["tr_free"], HALF * (i + 1))
                            for n in range(i * HALF, (i + 1) * HALF):
                                for k in range(KD):
                                    last = three_products(
                                        eng, mm[:, n, :], [x[:, k, n * P:(n + 1) * P] for x in (hth, htl)],
                                        [x[:, k, :] for x in (w1h, w1l)], k == 0, k == KD - 1)
                            last.then_inc(s["mm"], 1)
                null_values()
                eng.wait_ge(s["tr_free"], NT * NS)
                for c in range(S // BANK):
                    for k in range(KD):
                        last = three_products(
                            eng, mm[:, 2 * c:2 * c + 2, :].rearrange("p a b -> p (a b)"),
                            [x[:, k, :] for x in (w2h, w2l)],
                            [x[:, k, c * BANK:(c + 1) * BANK] for x in (hth, htl)], k == 0, k == KD - 1)
                last.then_inc(s["mm"], 1)


def project(nc, t, b, normed):
    names = ["dve", "var", "std", "xn", "xtr", "xt_hi", "xt_lo", "q", "kv", "q_copy", "kv_copy", "sumsq",
             "norm", "q_ready", "q_hi", "q_lo", "k_ready", "tr", "out_d", "out_a", "store0", "store1"]
    NG = 4
    GR = 1 + H // NG
    BY_DVE, BY_ACT = (0, 3), (1, 2, 4)
    TILE_D, TILE_A = len(BY_DVE), len(BY_ACT)
    LAG = 2
    AHEAD = 2
    NQ = 3
    with tensors(nc) as (sb, ps):
        pen = sb("pj_pen", [P, NT])
        xb = sb("pj_xb", [P, NT, D])
        stats = sb("pj_stats", [P, NT, 6])
        mv = sb("pj_mv", [P, NT, 2])
        rstd = sb("pj_rstd", [P, NT])
        xth, xtl = (sb(f"pj_xt{n}", [P, KD, S], FR) for n in "hl")
        qs = sb("pj_qs", [P, NQ, H * DH])
        sq = sb("pj_sq", [P, 2, H * DH])
        kvs = sb("pj_kvs", [P, 2, 2 * DH + H])
        ksq = sb("pj_ksq", [P, DH])
        ss = sb("pj_ss", [P, 2, H + 1])
        kn = sb("pj_kn", [P, DH])
        nul = sb("pj_nul", [P, H])
        qhl = sb("pj_qhl", [P, 2, H, 2 * DH], FR)
        khl = sb("pj_khl", [P, 2, 2 * P], FR)
        qt = sb("pj_qt", [P, 2, H, P], FR)
        xtr = ps("pj_xtr", [P, BANK])[:, 0:KD * P]
        qps = [ps(f"pj_q{n}", [P, H * DH]) for n in range(2)]
        kvp = ps("pj_kv", [P, BANK])
        trs = [ps(f"pj_tr{n}", [P, NG * P]) for n in range(2)]
        with Phase(nc, t, names) as (block, s):
            def copied(eng, m):
                n, g = m // GR, m % GR
                if g in BY_DVE:
                    eng.wait_ge(s["out_d"], TILE_D * n + BY_DVE.index(g) + 1)
                else:
                    eng.wait_ge(s["out_a"], TILE_A * n + BY_ACT.index(g) + 1)

            @block.sync
            def _(eng):
                for n in range(NT):
                    eng.wait_ge(s["out_d"], TILE_D * (n + 1))
                    eng.wait_ge(s["out_a"], TILE_A * (n + 1))
                    eng.dma_start(t["q_dram"][:, :, n * P:(n + 1) * P].rearrange("h p i -> p h i"), f32(qt[:, n % 2, :, :])
                                  ).then_inc(s[f"store{n % 2}"], 16)
                eng.wait_ge(s["store0"], 16 * NT // 2)
                eng.wait_ge(s["store1"], 16 * NT // 2)

            @block.tensor
            def _(eng):
                def x_transpose(n):
                    eng.wait_ge(s["xn"], n + 1)
                    if n:
                        eng.wait_ge(s["xt_lo"], n)
                    for k in range(KD):
                        last = eng.transpose(xtr[:, k * P:(k + 1) * P], xb[:, n, k * P:(k + 1) * P], t["ident"][:])
                    last.then_inc(s["xtr"], 1)

                def left(n, k):
                    return [x[:, k, n * P:(n + 1) * P] for x in (xth, xtl)]

                def queries(n, c):
                    if c == 0:
                        eng.wait_ge(s["xt_lo"], n + 1)
                        if n >= 2:
                            eng.wait_ge(s["q_copy"], n - 1)
                    for k in range(KD):
                        last = three_products(eng, qps[n % 2][:, c * BANK:(c + 1) * BANK], left(n, k),
                                              [t[x][:, k, c * BANK:(c + 1) * BANK] for x in ("wq_h", "wq_l")],
                                              k == 0, k == KD - 1)
                    if c == H * DH // BANK - 1:
                        last.then_inc(s["q"], 1)

                def keys_values(n):
                    if n:
                        eng.wait_ge(s["kv_copy"], n)
                    for k in range(KD):
                        last = three_products(eng, kvp[:, 0:2 * DH + H], left(n, k), [t[x][:, k, :] for x in ("wx_h", "wx_l")],
                                              k == 0, k == KD - 1)
                    last.then_inc(s["kv"], 1)

                def head_transposes(n, *groups):
                    for g in groups:
                        m = n * GR + g
                        if g == 0:
                            eng.wait_ge(s["k_ready"], n + 1)
                            blocks = [khl[:, n % 2, c * P:(c + 1) * P] for c in range(2)]
                        else:
                            eng.wait_ge(s["q_lo"], n + 1)
                            blocks = [qhl[:, n % 2, (g - 1) * NG + c, :] for c in range(NG)]
                        if m >= 2:
                            copied(eng, m - 2)
                        for c, block in enumerate(blocks):
                            last = eng.transpose(trs[m % 2][:, c * P:(c + 1) * P].bitcast(FR), block, t["ident_r"][:])
                        last.then_inc(s["tr"], 1)

                for n in range(AHEAD):
                    x_transpose(n)
                for n in range(NT + LAG):
                    if n + AHEAD < NT:
                        x_transpose(n + AHEAD)
                    if n < NT:
                        queries(n, 0)
                    if n >= LAG:
                        head_transposes(n - LAG, 0, 1)
                    if n < NT:
                        queries(n, 1)
                    if n >= LAG:
                        head_transposes(n - LAG, 2, 3)
                    if n < NT:
                        keys_values(n)
                    if n >= LAG:
                        head_transposes(n - LAG, 4)

            def heads(n):
                return qs[:, n % NQ, :].rearrange("p (h d) -> p h d", h=H)

            def evacuate(eng, n, g, copy):
                m = n * GR + g
                out = s["out_d" if g in BY_DVE else "out_a"]
                eng.wait_ge(s["tr"], m + 1)
                if g == 0:
                    copy(t["k_hh"][:, n * P:(n + 1) * P], trs[m % 2][:, 0:P])
                    copy(t["k_lp"][:, n * P:(n + 1) * P], trs[m % 2][:, P:2 * P]).then_inc(out, 1)
                else:
                    if n >= 2:
                        eng.wait_ge(s[f"store{n % 2}"], 16 * (n // 2))
                    copy(qt[:, n % 2, (g - 1) * NG:g * NG, :].rearrange("p h i -> p (h i)"), trs[m % 2][:]
                         ).then_inc(out, 1)

            @block.vector
            def _(eng):
                own = Own(eng, s["dve"])
                for tile in (0, 1):
                    own.step(eng.memset(f32(khl[:, tile, P:2 * P]), 0.0))
                own.step(eng.tensor_copy(xb[:], t["x"][:, bass.ds(b * NT, NT), :]))
                own.step(eng.tensor_copy(pen[:], t["penalty"][:, bass.ds(b, 1), :].rearrange("p o t -> p (o t)")))
                own.settle()
                for n in range(NT):
                    own.step(eng.bn_stats(stats[:, n, :], xb[:, n, :]))
                own.settle()
                for n in range(NT):
                    own.step(eng.bn_aggr(mv[:, n, :], stats[:, n, :]))
                own.settle()
                eng.tensor_scalar(rstd[:], mv[:, :, 1], EPS, None, ALU.add).then_inc(s["var"], 1)
                eng.wait_ge(s["std"], 1)
                own.step(eng.reciprocal(rstd[:], rstd[:]))
                own.settle()
                for n in range(NT):
                    eng.tensor_scalar(xb[:, n, :], xb[:, n, :], mv[:, n, 0:1], rstd[:, n:n + 1],
                                      ALU.subtract, ALU.mult).then_inc(s["xn"], 1)

                def x_low(n):
                    eng.wait_ge(s["xt_hi"], n + 1)
                    eng.tensor_tensor(xtl[:, :, n * P:(n + 1) * P], xtr.rearrange("p (k i) -> p k i", k=KD),
                                      f32(xth[:, :, n * P:(n + 1) * P]), ALU.subtract).then_inc(s["xt_lo"], 1)

                def sum_squares(n):
                    eng.wait_ge(s["kv_copy"], n + 1)
                    eng.wait_ge(s["q_copy"], n + 1)
                    if n:
                        eng.wait_ge(s["sumsq"], n)
                    own.step(eng.tensor_tensor(ksq[:], kvs[:, n % 2, 0:DH], kvs[:, n % 2, 0:DH], ALU.mult))
                    own.step(eng.tensor_reduce(ss[:, n % 2, 0:H], sq[:, n % 2, :].rearrange("p (h d) -> p h d", h=H),
                                               AX.X, ALU.add))
                    own.settle()
                    eng.tensor_reduce(ss[:, n % 2, H:H + 1], ksq[:], AX.X, ALU.add).then_inc(s["sumsq"], 1)

                def keys(n):
                    c = n % 2
                    if n:
                        eng.wait_ge(s["k_ready"], n)
                    if normed:
                        eng.wait_ge(s["norm"], n + 1)
                        own.step(eng.tensor_scalar(ss[:, c, :], ss[:, c, :], 1e-12, None, ALU.max))
                        own.settle()
                        own.step(eng.reciprocal(ss[:, c, :], ss[:, c, :]))
                        own.settle()
                        eng.tensor_tensor(heads(n), heads(n), ss[:, c, 0:H].unsqueeze(2).to_broadcast([P, H, DH]), ALU.mult
                                          ).then_inc(s["q_ready"], 1)
                        own.step(eng.scalar_tensor_tensor(kn[:], kvs[:, c, 0:DH], ss[:, c, H:H + 1], t["kscale"][:],
                                                          ALU.mult, ALU.mult))
                        own.step(eng.tensor_tensor(nul[:], kvs[:, c, 2 * DH:], ss[:, c, 0:H], ALU.mult))
                    else:
                        eng.wait_ge(s["kv_copy"], n + 1)
                        own.step(eng.tensor_scalar(kn[:], kvs[:, c, 0:DH], DH ** -0.5, None, ALU.mult))
                        own.step(eng.tensor_copy(nul[:], kvs[:, c, 2 * DH:]))
                    if n >= 2:
                        eng.wait_ge(s["tr"], GR * (n - 2) + 1)
                    own.settle()
                    own.step(eng.tensor_copy(khl[:, c, 0:2 * DH].rearrange("p (r d) -> p r d", r=2),
                                             kn[:].unsqueeze(1).to_broadcast([P, 2, DH])))
                    own.step(eng.tensor_copy(khl[:, c, 3 * DH:3 * DH + 1], pen[:, n:n + 1]))
                    own.step(eng.scalar_tensor_tensor(t["neg_null"][:, n, :], nul[:], -1.0, t["null_bias"][:],
                                                      ALU.mult, ALU.subtract))
                    own.settle()
                    eng.tensor_tensor(khl[:, c, 2 * DH:3 * DH], kn[:], f32(khl[:, c, 0:DH]), ALU.subtract
                                      ).then_inc(s["k_ready"], 1)

                def q_low(n):
                    eng.wait_ge(s["q_hi"], n + 1)
                    eng.tensor_tensor(qhl[:, n % 2, :, DH:], heads(n), f32(qhl[:, n % 2, :, 0:DH]), ALU.subtract
                                      ).then_inc(s["q_lo"], 1)

                for n in range(AHEAD):
                    x_low(n)
                for n in range(NT + LAG):
                    if n >= LAG:
                        q_low(n - LAG)
                        evacuate(eng, n - LAG, 0, eng.tensor_copy)
                    if n + AHEAD < NT:
                        x_low(n + AHEAD)
                    if normed and 1 <= n <= NT:
                        sum_squares(n - 1)
                    if 1 <= n <= NT:
                        keys(n - 1)
                    if n >= LAG:
                        evacuate(eng, n - LAG, 3, eng.tensor_copy)

            @block.scalar
            def _(eng):
                def copy(out, in_):
                    return eng.activation(out, in_, ACT.Copy)

                eng.wait_ge(s["var"], 1)
                eng.activation(rstd[:], rstd[:], ACT.Sqrt).then_inc(s["std"], 1)

                def x_high(n):
                    eng.wait_ge(s["xtr"], n + 1)
                    eng.activation(xth[:, :, n * P:(n + 1) * P], xtr.rearrange("p (k i) -> p k i", k=KD), ACT.Copy
                                   ).then_inc(s["xt_hi"], 1)

                def copies(n):
                    c = n % 2
                    eng.wait_ge(s["q"], n + 1)
                    if n >= NQ:
                        eng.wait_ge(s["q_lo"], n - NQ + 1)
                    q_copied = eng.activation(qs[:, n % NQ, :], qps[c][:], ACT.Copy)
                    if normed:
                        if n >= 2:
                            eng.wait_ge(s["sumsq"], n - 1)
                        q_copied = eng.activation(sq[:, c, :], qps[c][:], ACT.Square)
                    q_copied.then_inc(s["q_copy"], 1)
                    eng.wait_ge(s["kv"], n + 1)
                    if n >= 2:
                        eng.wait_ge(s["k_ready"], n - 1)
                    eng.activation(t["v"][:, n, :], kvp[:, DH:2 * DH], ACT.Copy)
                    eng.activation(kvs[:, c, :], kvp[:, 0:2 * DH + H], ACT.Copy).then_inc(s["kv_copy"], 1)

                def norms(n):
                    eng.wait_ge(s["sumsq"], n + 1)
                    eng.activation(ss[:, n % 2, :], ss[:, n % 2, :], ACT.Sqrt).then_inc(s["norm"], 1)

                def q_high(n):
                    eng.wait_ge(s["q_ready" if normed else "q_copy"], n + 1)
                    if n >= 2:
                        eng.wait_ge(s["tr"], GR * (n - 1))
                    eng.activation(qhl[:, n % 2, :, 0:DH], heads(n), ACT.Copy).then_inc(s["q_hi"], 1)

                for n in range(AHEAD):
                    x_high(n)
                for n in range(NT + LAG):
                    if n + AHEAD < NT:
                        x_high(n + AHEAD)
                    if 1 <= n <= NT:
                        copies(n - 1)
                    if n >= LAG:
                        evacuate(eng, n - LAG, 1, copy)
                    if normed and 1 <= n <= NT:
                        norms(n - 1)
                    if n >= LAG:
                        evacuate(eng, n - LAG, 2, copy)
                    if 1 <= n <= NT:
                        q_high(n - 1)
                    if n >= LAG:
                        evacuate(eng, n - LAG, 4, copy)


def attend(nc, t, bias):
    HP = 2
    U = HP * NT * 2
    GU = 8
    NGRP = U // GU
    TURNS = NPAIR // HP
    NBIAS = 4
    VSTEPS = 6
    SKEW = VSTEPS + 1
    toeplitz = bias is None
    n_bias = HP * 2 if toeplitz else U

    pieces, starts = [], []
    for u in range(U):
        n = (u // 2) % NT + 1
        starts.append(len(pieces))
        pieces += [(at, min(4, n - at)) for at in range(0, n, 4)]
    NPC = len(pieces)
    assert NPC % 2 == 0 and U % NBIAS == 0 and NGRP % 2 == 0

    def first(u):
        return u // U * NPC + starts[u % U]

    marks = dict(qk=U, biased=U, exp=U, tr=NPC, ev_a=NPC // 2, ev_d=NPC // 2, pv=NGRP, null_d=NGRP, null_e=NGRP,
                 inv_b=NGRP, bc=NGRP, bc_s=NGRP, out=NGRP, diag=U, nulls=HP, sums=3 * NGRP)
    names = list(marks) + ["q0", "q1", "ones", "gate"] + [f"bias{n}" for n in range(NBIAS)]

    NARROW = BANK - P

    def weights_at(g, j):
        full = 4 * (g % 2)
        return min(j, full) * BANK + max(0, j - full) * NARROW

    def unit(u):
        tile = (u // 2) % NT
        return u % U // (2 * NT), tile, u % 2, (tile + 1) * P

    with tensors(nc) as (sb, ps):
        q_hl = sb("at_q_hl", [P, HP, 2, S], FR)
        q_h1 = sb("at_q_h1", [P, HP, 2, S], FR)
        bt = sb("at_bias", [P, NBIAS, S])
        neg = sb("at_neg", [P, 2, S])
        prob = sb("at_prob", [P, 2, S])
        pt = [sb(f"at_pt{n}", [P, 2, 4 * n * BANK + 3 * NARROW + BANK]) for n in range(2)]
        nmax, rsum, nd, p0, inv = (sb(f"at_{n}", [P, 2, GU]) for n in ("nmax", "rsum", "nd", "p0", "inv"))
        inv_b = sb("at_inv_b", [P, GU, DH])
        bc_s = sb("at_bc_s", [P, BANK])
        nn = sb("at_nn", [P, NT, 2 * HP])
        s_ps = [ps(f"at_s{n}", [P, S]) for n in range(2)]
        t_ps = [ps(f"at_t{n}", [P, BANK]) for n in range(2)]
        o_ps = ps("at_o", [P, BANK])
        b_ps = ps("at_b", [P, BANK])

        def evacuate(eng, turn, u, n, copy, parity, name):
            m = first(u) + n
            if m >= first(u + 1) or m % 2 != parity:
                return
            turn.wait(eng, "tr", m + 1)
            turn.wait(eng, "pv", u // GU - 1)
            at, blocks = pieces[m % NPC]
            col = ((u // 2) % 4) * P
            g = u // GU % 2
            here = weights_at(g, at) + col
            one = pt[g][:, u % 2, here:here + P]
            pitch = BANK if at < 4 * g else NARROW
            copy(bass.AP(one.tensor, one.offset, [one.ap[0], [pitch, blocks], [1, P]]),
                 t_ps[parity][:, 0:blocks * P].rearrange("p (c i) -> p c i", i=P)).then_inc(s[name], 1)

        with Phase(nc, t, names) as (block, s):
            @block.sync
            def _(eng):
                if toeplitz:
                    eng.wait_ge(t["bands_sem"], t["bands_n"])
                with eng.Fori(0, TURNS) as it:
                    turn = Turns(s, it, marks)

                    def queries(p):
                        turn.wait(eng, "qk", (p + 1) * 2 * NT - U)
                        two = bass.ds(it * 2 * HP + 2 * p, 2)
                        eng.dma_start(f32(q_hl[:, p, :, :]), t["q_dram"][two, :, :].rearrange("h p i -> p h i")
                                      ).then_inc(s[f"q{p}"], 16)
                        eng.dma_start(f32(q_h1[0:DH, p, :, :]), t["q_dram"][two, 0:DH, :].rearrange("h p i -> p h i")
                                      ).then_inc(s[f"q{p}"], 16)

                    for n in range(n_bias):
                        if n % (n_bias // HP) == 0:
                            queries(n // (n_bias // HP))
                        slot = n % NBIAS
                        if toeplitz:
                            turn.wait(eng, "biased", (n // 2) * 2 * NT + 2 * (NT - 1) + n % 2 + 1 - U)
                            head = bass.ds(it * 2 * HP + n, 1)
                            eng.dma_start(bt[:, slot, :], t["bands"][head, :, :].rearrange("o p c -> p (o c)")
                                          ).then_inc(s[f"bias{slot}"], 16)
                        else:
                            p, tile, side, width = unit(n)
                            turn.wait(eng, "biased", n + 1 - NBIAS)
                            head = bass.ds(it * 2 * HP + 2 * p + side, 1)
                            eng.dma_start(bt[:, slot, 0:width],
                                          bias[head, tile * P:(tile + 1) * P, 0:width].rearrange("o p c -> p (o c)")
                                          ).then_inc(s[f"bias{slot}"], 16)
                for p in range(HP):
                    eng.wait_ge(s[f"q{p}"], 32 * TURNS)
                for n in range(NBIAS):
                    eng.wait_ge(s[f"bias{n}"], 16 * TURNS * n_bias // NBIAS)

            @block.tensor
            def _(eng):
                def logits(it, u):
                    turn = Turns(s, it, marks)
                    p, tile, side, width = unit(u)
                    if u % (2 * NT) == 0:
                        eng.wait_ge(s[f"q{p}"], it * 32 + 32 * (u // U + 1))
                    turn.wait(eng, "biased", u - 1)
                    at = slice(tile * P, (tile + 1) * P)
                    for c in range(0, width, BANK):
                        n = min(BANK, width - c)
                        out = s_ps[u % 2][:, c:c + n]
                        eng.matmul(out, q_hl[:, p, side, at], t["k_hh"][:, c:c + n], start=True, stop=False)
                        last = eng.matmul(out, q_h1[0:DH + 1, p, side, at], t["k_lp"][0:DH + 1, c:c + n],
                                          start=False, stop=True)
                    last.then_inc(s["qk"], 1)

                def transposes(turn, u, n):
                    m = first(u) + n
                    if m >= first(u + 1):
                        return
                    turn.wait(eng, "exp", u + 1)
                    turn.wait(eng, ("ev_a", "ev_d")[m % 2], m // 2)
                    at, blocks = pieces[m % NPC]
                    for c in range(blocks):
                        last = eng.transpose(t_ps[m % 2][:, c * P:(c + 1) * P],
                                             prob[:, u % 2, (at + c) * P:(at + c + 1) * P], t["ident"][:])
                    last.then_inc(s["tr"], 1)

                def values(turn, g, part):
                    m = first(GU * (g + 1))
                    turn.wait(eng, "ev_a", m // 2)
                    turn.wait(eng, "ev_d", m // 2)
                    turn.wait(eng, "out", g)
                    blocks = 4 * (g % 2) + 4
                    products = [(j, side) for j in range(blocks) for side in range(2)]
                    for j, side in products[part * len(products) // VSTEPS:(part + 1) * len(products) // VSTEPS]:
                        i0 = max(0, j - (blocks - 4)) * P
                        at = weights_at(g, j)
                        last = eng.matmul(o_ps[side * DH:(side + 1) * DH, i0:BANK], t["v"][:, j, :],
                                          pt[g % 2][:, side, at + i0:at + BANK], start=j == 0, stop=j == blocks - 1)
                    if part == VSTEPS - 1:
                        last.then_inc(s["pv"], 1)

                def broadcast(turn, g):
                    turn.wait(eng, "inv_b", g + 1)
                    turn.wait(eng, "bc_s", g)
                    for c in range(4):
                        last = eng.transpose(b_ps[:, c * P:(c + 1) * P],
                                             inv_b[:, 2 * c:2 * c + 2, :].rearrange("p s d -> p (s d)"), t["ident"][:])
                    last.then_inc(s["bc"], 1)

                def step(it, u, has):
                    turn = Turns(s, it, marks)
                    if has(u, U):
                        transposes(turn, u, 0)
                    if has(u + 3, U):
                        logits(it, u + 3)
                    if has(u, U):
                        transposes(turn, u, 1)
                    g = u // GU - 1
                    if u % GU < VSTEPS and has(g, NGRP):
                        values(turn, g, u % GU)
                    if u % GU == VSTEPS - 2 and has(g, NGRP):
                        broadcast(turn, g)

                start(eng, s, marks, "qk", "tr", "pv", "bc")
                eng.wait_ge(s["ones"], 1)
                run(eng, step, TURNS, U, 3, SKEW)

            @block.vector
            def _(eng):
                start(eng, s, marks, "biased", "ev_d", "null_d", "nulls", "sums", "inv_b", "out")
                for p in range(HP):
                    for side in range(2):
                        last = eng.memset(f32(q_h1[DH:DH + 1, p, side, :]), 1.0)
                last.then_inc(s["ones"], 1)

                def null_logits(turn, it, pair):
                    p = pair % HP
                    turn.wait(eng, "null_d", 2 * (pair - HP) + 2)
                    eng.sem_inc(s["gate"], 1)
                    eng.tensor_copy(nn[:, :, 2 * p:2 * p + 2], t["neg_null"][:, :, bass.ds(it * 2 * HP + 2 * pair, 2)]
                                    ).then_inc(s["nulls"], 1)
                    turn.wait(eng, "nulls", pair + 1)

                def add_bias(turn, it, u):
                    p, tile, side, width = unit(u)
                    turn.wait(eng, "qk", u + 1)
                    turn.wait(eng, "exp", u - 1)
                    slot, lo = (2 * p + side, S - width) if toeplitz else (u % NBIAS, 0)
                    if not toeplitz:
                        turn.wait(eng, "diag", u + 1)
                    elif tile == 0:
                        eng.wait_ge(s[f"bias{slot}"], it * 16 + 16 * (u // U + 1))
                    eng.sem_inc(s["gate"], 1)
                    eng.tensor_tensor_reduce(
                        out=neg[:, u % 2, 0:width], in0=s_ps[u % 2][:, 0:width], in1=bt[:, slot, lo:lo + width],
                        scale=-1.0, scalar=nn[:, tile, 2 * p + side:2 * p + side + 1], op0=ALU.add, op1=ALU.min,
                        accum_out=nmax[:, (u // GU) % 2, u % GU:u % GU + 1]).then_inc(s["biased"], 1)

                def per_tile(x, g):
                    return x[:, g % 2, :].rearrange("p (t s) -> p t s", s=2)

                def tiles(g):
                    return slice(4 * (g % 2), 4 * (g % 2) + 4)

                def null_shift(turn, g):
                    p = g // 2 % HP
                    turn.wait(eng, "exp", GU * (g + 1))
                    turn.wait(eng, "null_e", g - 1)
                    eng.tensor_tensor(per_tile(nd, g), per_tile(nmax, g), nn[:, tiles(g), 2 * p:2 * p + 2], ALU.subtract
                                      ).then_inc(s["null_d"], 1)

                def sums(turn, it, g):
                    turn.wait(eng, "null_e", g + 1)
                    turn.wait(eng, "inv_b", g - 1)
                    c = g % 2
                    eng.tensor_tensor(inv[:, c, :], p0[:, c, :], rsum[:, c, :], ALU.add).then_inc(s["sums"], 1)
                    turn.wait(eng, "sums", 3 * g + 1)
                    eng.reciprocal(inv[:, c, :], inv[:, c, :]).then_inc(s["sums"], 1)
                    turn.wait(eng, "sums", 3 * g + 2)
                    eng.tensor_tensor(t["null_w"][:, tiles(g), bass.ds(it * 2 * HP + 2 * (g // 2), 2)],
                                      per_tile(p0, g), per_tile(inv, g), ALU.mult).then_inc(s["sums"], 1)
                    turn.wait(eng, "bc", g)
                    eng.tensor_copy(inv_b[:], inv[:, c, :].unsqueeze(2).to_broadcast([P, GU, DH])
                                    ).then_inc(s["inv_b"], 1)

                def output(turn, it, g):
                    turn.wait(eng, "bc_s", g + 1)
                    turn.wait(eng, "pv", g + 1)
                    at = (g % 2) * BANK
                    eng.tensor_tensor(t["o_t"][:, bass.ds(it * HP + g // 2, 1), at:at + BANK
                                               ].rearrange("p o i -> p (o i)"),
                                      o_ps[:], bc_s[:], ALU.mult).then_inc(s["out"], 1)

                def step(it, u, has):
                    turn = Turns(s, it, marks)
                    if has(u + 2, U):
                        if (u + 2) % (2 * NT) == 0:
                            null_logits(turn, it, (u + 2) // (2 * NT))
                        add_bias(turn, it, u + 2)
                    if has(u, U):
                        evacuate(eng, turn, u, 0, eng.tensor_copy, 1, "ev_d")
                        evacuate(eng, turn, u, 1, eng.tensor_copy, 1, "ev_d")
                        if u % GU == GU - 1:
                            null_shift(turn, u // GU)
                    g = u // GU - 1
                    if u % GU == 0 and has(g, NGRP):
                        sums(turn, it, g)
                    if u % GU == VSTEPS and has(g, NGRP):
                        output(turn, it, g)

                run(eng, step, TURNS, U, 3, SKEW)
                eng.wait_ge(s["out"], NGRP * (TURNS + 1))

            @block.scalar
            def _(eng):
                def copy(out, in_):
                    return eng.activation(out, in_, ACT.Copy)

                def exponent(turn, u):
                    width = unit(u)[3]
                    c, i = (u // GU) % 2, u % GU
                    turn.wait(eng, "biased", u + 1)
                    turn.wait(eng, "tr", first(u - 1))
                    turn.wait(eng, "inv_b", u // GU - 1)
                    eng.activation(prob[:, u % 2, 0:width], neg[:, u % 2, 0:width], ACT.Exp, scale=-1.0,
                                   bias=nmax[:, c, i:i + 1], accum_out=rsum[:, c, i:i + 1]).then_inc(s["exp"], 1)

                def null_exponent(turn, g):
                    turn.wait(eng, "null_d", g + 1)
                    turn.wait(eng, "inv_b", g - 1)
                    eng.activation(p0[:, g % 2, :], nd[:, g % 2, :], ACT.Exp).then_inc(s["null_e"], 1)

                def copy_broadcast(turn, g):
                    turn.wait(eng, "bc", g + 1)
                    turn.wait(eng, "out", g)
                    copy(bc_s[:], b_ps[:]).then_inc(s["bc_s"], 1)

                def step(it, u, has):
                    turn = Turns(s, it, marks)
                    if has(u + 1, U):
                        exponent(turn, u + 1)
                    g = u // GU - 1
                    if u % GU == VSTEPS and has(g, NGRP):
                        copy_broadcast(turn, g)
                    if has(u, U):
                        evacuate(eng, turn, u, 0, copy, 0, "ev_a")
                        evacuate(eng, turn, u, 1, copy, 0, "ev_a")
                        if u % GU == GU - 1:
                            null_exponent(turn, u // GU)

                start(eng, s, marks, "exp", "ev_a", "null_e", "bc_s")
                run(eng, step, TURNS, U, 3, SKEW)

            if not toeplitz:
                @block.gpsimd
                def _(eng):
                    start(eng, s, marks, "diag")
                    with eng.Fori(0, TURNS) as it:
                        for u in range(U):
                            tile, width = unit(u)[1], unit(u)[3]
                            slot = u % NBIAS
                            eng.wait_ge(s[f"bias{slot}"], it * (16 * U // NBIAS) + 16 * (u // NBIAS + 1))
                            eng.sem_inc(s["gate"], 1)
                            corner = bt[:, slot, tile * P:width]
                            eng.affine_select(out=corner, in_=corner, compare_op=ALU.is_ge, fill=-BIG, base=0,
                                              pattern=[[-1, P]], channel_multiplier=1).then_inc(s["diag"], 1)


def close_layer(nc, t, b, out):
    names = ["o_hi", "o_lo", "n_tr", "n_copy", "y", "y_copy", "var", "std", "dve", "added", "stored"]
    HALF = NT // 2
    AHEAD, SLOTS = 2, 4
    with tensors(nc) as (sb, ps):
        oh, ol = (sb(f"cl_o{n}", [P, SLOTS, NPAIR, P], FR) for n in "hl")
        nwt = sb("cl_nwt", [H, 2, P])
        y = sb("cl_y", [P, NT, D])
        stats = sb("cl_stats", [P, NT, 6])
        mv = sb("cl_mv", [P, NT, 2])
        rstd = sb("cl_rstd", [P, NT])
        yps = [ps(f"cl_y{n}", [P, BANK]) for n in range(2)]
        nps = [ps(f"cl_n{n}", [H, BANK]) for n in range(2)]
        with Phase(nc, t, names) as (block, s):
            @block.scalar
            def _(eng):
                def std(i):
                    half = slice(i * HALF, (i + 1) * HALF)
                    eng.wait_ge(s["var"], i + 1)
                    eng.activation(rstd[:, half], rstd[:, half], ACT.Sqrt).then_inc(s["std"], 1)

                def high(n):
                    if n >= SLOTS:
                        eng.wait_ge(s["y"], n - SLOTS + 1)
                    eng.activation(oh[:, n % SLOTS, :, :], t["o_t"][:, :, n * P:(n + 1) * P], ACT.Copy
                                   ).then_inc(s["o_hi"], 1)

                for n in range(AHEAD):
                    high(n)
                for n in range(NT):
                    if n == HALF + 1:
                        std(0)
                    if n + AHEAD < NT:
                        high(n + AHEAD)
                    eng.wait_ge(s["n_tr"], n + 1)
                    eng.activation(nwt[:, n % 2, :], nps[n % 2][:, 0:P], ACT.Copy).then_inc(s["n_copy"], 1)
                    if n:
                        eng.wait_ge(s["y"], n)
                        eng.activation(y[:, n - 1, :], yps[(n - 1) % 2][:, 0:D], ACT.Copy).then_inc(s["y_copy"], 1)
                eng.wait_ge(s["y"], NT)
                eng.activation(y[:, NT - 1, :], yps[(NT - 1) % 2][:, 0:D], ACT.Copy).then_inc(s["y_copy"], 1)
                std(1)

            @block.tensor
            def _(eng):
                for n in range(NT):
                    if n >= 2:
                        eng.wait_ge(s["n_copy"], n - 1)
                    eng.transpose(nps[n % 2][:, 0:P], t["null_w"][:, n, :], t["ident"][:]).then_inc(s["n_tr"], 1)
                    eng.wait_ge(s["o_lo"], n + 1)
                    if n >= 2:
                        eng.wait_ge(s["y_copy"], n - 1)
                    out_ = yps[n % 2][:, 0:D]
                    for a in range(NPAIR):
                        three_products(eng, out_, [x[:, n % SLOTS, a, :] for x in (oh, ol)],
                                       [t[x][:, a, :] for x in ("wo_h", "wo_l")], a == 0, False)
                    eng.wait_ge(s["n_copy"], n + 1)
                    eng.matmul(out_, nwt[:, n % 2, :], t["null_out"][:], start=False, stop=True).then_inc(s["y"], 1)

            @block.vector
            def _(eng):
                own = Own(eng, s["dve"])

                def low(n):
                    eng.wait_ge(s["o_hi"], n + 1)
                    eng.tensor_tensor(ol[:, n % SLOTS, :, :], t["o_t"][:, :, n * P:(n + 1) * P], f32(oh[:, n % SLOTS, :, :]),
                                      ALU.subtract).then_inc(s["o_lo"], 1)

                def statistics(n):
                    eng.wait_ge(s["y_copy"], n + 1)
                    own.step(eng.bn_stats(stats[:, n, :], y[:, n, :]))
                    own.settle()
                    own.step(eng.bn_aggr(mv[:, n, :], stats[:, n, :]))

                def variances(i):
                    half = slice(i * HALF, (i + 1) * HALF)
                    own.settle()
                    eng.tensor_scalar(rstd[:, half], mv[:, half, 1], EPS, None, ALU.add).then_inc(s["var"], 1)

                def close(i):
                    half = slice(i * HALF, (i + 1) * HALF)
                    eng.wait_ge(s["std"], i + 1)
                    own.step(eng.reciprocal(rstd[:, half], rstd[:, half]))
                    own.settle()
                    for n in range(i * HALF, (i + 1) * HALF):
                        own.step(eng.tensor_scalar(y[:, n, :], y[:, n, :], mv[:, n, 0:1], rstd[:, n:n + 1],
                                                   ALU.subtract, ALU.mult))
                    own.settle()
                    own.step(eng.tensor_tensor(y[:, half, :], y[:, half, :],
                                               t["gain_out"][:].unsqueeze(1).to_broadcast([P, HALF, D]), ALU.mult))
                    own.settle()
                    x = t["x"][:, bass.ds(b * NT + i * HALF, HALF), :]
                    if out is None:
                        own.step(eng.tensor_tensor(x, x, y[:, half, :], ALU.add))
                    else:
                        eng.tensor_tensor(y[:, half, :], x, y[:, half, :], ALU.add).then_inc(s["added"], 1)

                for n in range(AHEAD):
                    low(n)
                for n in range(NT):
                    if n + AHEAD < NT:
                        low(n + AHEAD)
                    if n:
                        statistics(n - 1)
                    if n == HALF:
                        variances(0)
                    if n == HALF + 1:
                        close(0)
                statistics(NT - 1)
                variances(1)
                close(1)
                own.settle()

            if out is not None:
                @block.sync
                def _(eng):
                    for i in range(2):
                        eng.wait_ge(s["added"], i + 1)
                        half = slice(i * HALF, (i + 1) * HALF)
                        eng.dma_start(out[bass.ds(b, 1), i * HALF * P:(i + 1) * HALF * P, :
                                          ].rearrange("o (t p) d -> p (o t) d", p=P), y[:, half, :]
                                      ).then_inc(s["stored"], 16)
                    eng.wait_ge(s["stored"], 32)


def program(nc, a, out):
    q_dram = nc.dram_tensor("q_dram", [H, P, S], F32, kind="Internal").ap()
    brow = nc.dram_tensor("brow_dram", [H, BROW], F32, kind="Internal").ap()
    with ExitStack() as stack, tensors(nc) as (sb, _):
        bands = nc.dram_tensor("bands_dram", [H, P, S], F32, kind="Internal").ap()
        t = {"in_ident": a["ident"], "in_iota": a["iota"], "in_dist": a["dist"], "q_dram": q_dram, "brow": brow,
             "bands": bands, "bands_sem": stack.enter_context(nc.semaphore("bands")), "bands_n": 0}
        t["pool"] = [stack.enter_context(nc.semaphore(f"phase{n}")) for n in range(Phase.POOL)]
        assert t["pool"][-1].num - t["pool"][0].num == Phase.POOL - 1
        t["x"] = sb("x", [P, NTT, D])
        t["ident"] = sb("ident", [P, P])
        t["ident_r"] = sb("ident_r", [P, P], FR)
        t["iota"] = sb("iota", [P, E])
        t["dist"] = sb("dist", [P, NT])
        with tensors(nc) as (sb0, _):
            t["xt_h"] = sb0("xt_h", [P, KD, NTT * P], FR)
            t["xt_l"] = sb0("xt_l", [P, KD, NTT * P], FR)
            t["expert_w"] = sb0("expert_w", [P, NU, NTT])
            moe_route(nc, t, a["x"].rearrange("b s d -> (b s) d"), a["wt_t"], a["cond_t"], a["wg_t"])
            moe_experts(nc, t, a["w_gate"], a["w_up"], a["w_down"])
        for layer, normed in ((1, True), (2, False), (3, True)):
            w = {n: a[f"L{layer}_{n}"] for n in WEIGHTS[layer]}
            if not normed:
                w = {{"g_in": "g_norm", "Wo": "Wout"}.get(n, n): ap for n, ap in w.items()}
            if normed:
                t["bands_n"] += 16
            with tensors(nc) as (sbl, _):
                for part in "hl":
                    t[f"wq_{part}"] = sbl(f"wq_{part}", [P, KD, H * DH], FR)
                    t[f"wx_{part}"] = sbl(f"wx_{part}", [P, KD, 2 * DH + H], FR)
                    t[f"wo_{part}"] = sbl(f"wo_{part}", [P, NPAIR, D], FR)
                t["kscale"] = sbl("kscale", [P, DH])
                t["null_bias"] = sbl("null_bias", [P, H])
                t["penalty"] = sbl("penalty", [P, B, NT])
                t["gain_out"] = sbl("gain_out", [P, D])
                t["null_out"] = sbl("null_out", [H, D])
                t["k_hh"] = sbl("k_hh", [P, S], FR)
                t["k_lp"] = sbl("k_lp", [P, S], FR)
                t["v"] = sbl("v", [P, NT, DH])
                t["neg_null"] = sbl("neg_null", [P, NT, H])
                t["null_w"] = sbl("null_w", [P, NT, H])
                t["o_t"] = sbl("o_t", [P, NPAIR, S])
                prepare_layer(nc, t, w, a["cond"], a["mask_f"] if normed else a["mask_k"], normed)
                with nc.Fori(0, B) as b:
                    project(nc, t, b, normed)
                    attend(nc, t, None if normed else a["fside"])
                    close_layer(nc, t, b, out if layer == 3 else None)


RELATIVE = ["g_norm", "Wq", "Wkv", "q_scale", "k_scale", "null_attn_bias", "w0", "b0", "g0", "w1", "b1", "g1", "w2", "b2",
            "Wout", "g_out"]
WEIGHTS = {1: RELATIVE, 2: ["g_in", "null_attn_bias", "Wq", "Wkv", "Wo", "g_out"], 3: RELATIVE}


def kernel(**inputs):
    import numpy as _np
    import concourse.bacc as _bacc
    from concourse import mybir as _mybir
    from concourse.bass_utils import run_bass_kernel_spmd as _run

    raw = {n: _np.asarray(v) for n, v in inputs.items()}
    arrays = {
        "x": raw["x"], "cond": raw["cond_64"], "cond_t": raw["cond_64"].T, "fside": raw["fside_16xSxS_0"],
        "mask_f": raw["mask_BxS_bf1"].reshape(B, NT, P).transpose(0, 2, 1),
        "mask_k": raw["mask_BxS_bk0"].reshape(B, NT, P).transpose(0, 2, 1),
        "wt_t": raw["L0_cond_wt"].T, "wg_t": raw["L0_cond_wg"].T,
        "w_gate": _np.concatenate([raw["L0_cond_w_gate"], raw["L0_cond_sw_gate"].reshape(D, 2, M).transpose(1, 0, 2)]),
        "w_up": _np.concatenate([raw["L0_cond_w_up"], raw["L0_cond_sw_up"].reshape(D, 2, M).transpose(1, 0, 2)]),
        "w_down": _np.concatenate([raw["L0_cond_w_down"], raw["L0_cond_sw_down"].reshape(2, M, D)]),
        "ident": _np.eye(P, dtype=_np.float32),
        "iota": _np.tile(_np.arange(E, dtype=_np.float32), (P, 1)),
        "dist": (S - 1 - _np.arange(S, dtype=_np.float32)).reshape(NT, P).T,
    }
    for layer, names in WEIGHTS.items():
        for n in names:
            arrays[f"L{layer}_{n}"] = raw[f"L{layer}_cond_{n}"]
            if n in ("g_norm", "g_in"):
                arrays[f"L{layer}_{n}"] = arrays[f"L{layer}_{n}"].reshape(KD, P).T
    arrays = {f"in_{n}": _np.ascontiguousarray(v) for n, v in arrays.items()}

    nc = _bacc.Bacc("TRN2", target_bir_lowering=False, num_devices=1)
    aps = {n[3:]: nc.dram_tensor(n, v.shape, _mybir.dt.from_np(v.dtype), kind="ExternalInput").ap()
           for n, v in arrays.items()}
    out = nc.dram_tensor("out", (B, S, D), F32, kind="ExternalOutput").ap()
    program(nc, aps, out)
    result = _run(nc, [arrays], core_ids=[0])
    return result.results[0]["out"]
```
